# Optimizing a Trainium2 kernel written in Bass

```python
import numpy as np
import jax
import jax.numpy as jnp

def _softmax(x, axis=-1):
    return jax.nn.softmax(x, axis=axis)

def _gelu(x):
    return jax.nn.gelu(x, approximate=True)

def _silu(x):
    return jax.nn.silu(x)

def _sigmoid(x):
    return jax.nn.sigmoid(x)

def _layernorm(x, axis=-1, eps=1e-05):
    m = jnp.mean(x, axis=axis, keepdims=True)
    v = jnp.var(x, axis=axis, keepdims=True)
    return (x - m) / jnp.sqrt(v + eps)

def _scatter_add(tgt, idx, src, axis=0):
    return tgt.at[idx].add(src)

def _segment_sum(src, seg, n):
    return jax.ops.segment_sum(src, seg, n)
kernel_name = 'mk_hybrid_d1_jaxref_r8_a66d30'

def setup_inputs(seed: int=0):
    np.random.seed(seed)
    _w = jnp.asarray

    def _L0_attn_a_setup():
        import jax, jax.numpy as jnp
        import numpy as np
        D_MODEL = 128
        N_HEADS = 16
        D_K = D_MODEL // N_HEADS
        THETA = 10000.0

        def _rope(x, pos):
            half = D_K // 2
            inv_freq = THETA ** (-jnp.arange(0, half, dtype=jnp.float32) * 2.0 / D_K)
            ang = pos[:, None].astype(jnp.float32) * inv_freq[None, :]
            cos, sin = (jnp.cos(ang), jnp.sin(ang))
            x1, x2 = (x[..., 0::2], x[..., 1::2])
            r1 = x1 * cos - x2 * sin
            r2 = x1 * sin + x2 * cos
            out = jnp.stack([r1, r2], axis=-1).reshape(x.shape)
            return out
        key = jax.random.key(seed)
        ks = jax.random.split(key, 5)
        b, s = (4, 256)
        sc = 1.0 / np.sqrt(D_MODEL)
        return {'x': jax.random.normal(ks[0], (b, s, D_MODEL), dtype=jnp.float32), 'Wq': jax.random.normal(ks[1], (D_MODEL, D_MODEL), dtype=jnp.float32) * sc, 'Wk': jax.random.normal(ks[2], (D_MODEL, D_MODEL), dtype=jnp.float32) * sc, 'Wv': jax.random.normal(ks[3], (D_MODEL, D_MODEL), dtype=jnp.float32) * sc, 'Wo': jax.random.normal(ks[4], (D_MODEL, D_MODEL), dtype=jnp.float32) * sc}
    _L0_attn_a_in = _L0_attn_a_setup()

    def _L0_attn_b_setup():
        import jax, jax.numpy as jnp
        import numpy as np
        from jax import lax
        D_MODEL = 128
        D_INNER = 256
        D_STATE = 64
        D_CONV = 4
        HEADDIM = 64
        NHEADS = D_INNER // HEADDIM
        CONV_DIM = D_INNER + 2 * D_STATE
        D_IN_PROJ = 2 * D_INNER + 2 * D_STATE + NHEADS
        D_FF = 4 * D_MODEL
        EPS = 1e-05

        def _layernorm(x, w, b):
            mu = jnp.mean(x, -1, keepdims=True)
            var = jnp.mean((x - mu) ** 2, -1, keepdims=True)
            return (x - mu) * lax.rsqrt(var + EPS) * w + b

        def _silu(x):
            return x * jax.nn.sigmoid(x)

        def _mamba2(x, in_proj_w, conv_w, conv_b, dt_bias, A_log, D_param, norm_w, out_proj_w):
            B, L, _ = x.shape
            zxbcdt = jnp.einsum('bld,ed->ble', x, in_proj_w)
            z = zxbcdt[..., :D_INNER]
            xBC = zxbcdt[..., D_INNER:D_INNER + CONV_DIM]
            dt_raw = zxbcdt[..., D_INNER + CONV_DIM:]
            dt = jax.nn.softplus(dt_raw + dt_bias)
            xp = jnp.pad(xBC, ((0, 0), (D_CONV - 1, 0), (0, 0)))
            xBC = sum((conv_w[:, k] * xp[:, k:k + L, :] for k in range(D_CONV))) + conv_b
            xBC = _silu(xBC)
            xs = xBC[..., :D_INNER].reshape(B, L, NHEADS, HEADDIM)
            Bm = xBC[..., D_INNER:D_INNER + D_STATE]
            Cm = xBC[..., D_INNER + D_STATE:]
            A = -jnp.exp(A_log)
            dA = jnp.exp(dt * A)
            dtx = dt[..., None] * xs

            def step(h, inp):
                dA_t, dtx_t, B_t, C_t = inp
                h = dA_t[:, :, None, None] * h + dtx_t[..., None] * B_t[:, None, None, :]
                y_t = jnp.einsum('bhpn,bn->bhp', h, C_t)
                return (h, y_t)
            h0 = jnp.zeros((B, NHEADS, HEADDIM, D_STATE), x.dtype)
            _, ys = lax.scan(step, h0, (jnp.swapaxes(dA, 0, 1), jnp.swapaxes(dtx, 0, 1), jnp.swapaxes(Bm, 0, 1), jnp.swapaxes(Cm, 0, 1)))
            y = jnp.swapaxes(ys, 0, 1) + D_param[None, None, :, None] * xs
            y = y.reshape(B, L, D_INNER)
            y = y * _silu(z)
            y = y * lax.rsqrt(jnp.mean(y * y, -1, keepdims=True) + EPS) * norm_w
            return jnp.einsum('ble,de->bld', y, out_proj_w)

        def _mlp(x, fc_w, fc_b, proj_w, proj_b):
            h = jax.nn.gelu(jnp.einsum('bld,fd->blf', x, fc_w) + fc_b, approximate=False)
            return jnp.einsum('blf,df->bld', h, proj_w) + proj_b
        key = jax.random.key(seed)
        ks = jax.random.split(key, 16)
        B, L = (4, 512)
        s = 0.02
        inp = {'x': jax.random.normal(ks[0], (B, L, D_MODEL), jnp.float32), 'ln1_w': jnp.ones((D_MODEL,), jnp.float32), 'ln1_b': jnp.zeros((D_MODEL,), jnp.float32), 'ln2_w': jnp.ones((D_MODEL,), jnp.float32), 'ln2_b': jnp.zeros((D_MODEL,), jnp.float32), 'in_proj_w': jax.random.normal(ks[1], (D_IN_PROJ, D_MODEL), jnp.float32) * s, 'conv_w': jax.random.normal(ks[2], (CONV_DIM, D_CONV), jnp.float32) * 0.1, 'conv_b': jnp.zeros((CONV_DIM,), jnp.float32), 'dt_bias': jax.random.normal(ks[3], (NHEADS,), jnp.float32) * 0.1, 'A_log': jnp.log(jax.random.uniform(ks[4], (NHEADS,), jnp.float32, 1.0, 16.0)), 'D_param': jnp.ones((NHEADS,), jnp.float32), 'norm_w': jnp.ones((D_INNER,), jnp.float32), 'out_proj_w': jax.random.normal(ks[5], (D_MODEL, D_INNER), jnp.float32) * s, 'fc_w': jax.random.normal(ks[6], (D_FF, D_MODEL), jnp.float32) * s, 'fc_b': jnp.zeros((D_FF,), jnp.float32), 'proj_w': jax.random.normal(ks[7], (D_MODEL, D_FF), jnp.float32) * s, 'proj_b': jnp.zeros((D_MODEL,), jnp.float32)}
        return inp
    _L0_attn_b_in = _L0_attn_b_setup()

    def _L0_ffn_setup():
        import jax, jax.numpy as jnp
        import numpy as np
        NUM_EXPERTS = 8
        TOP_K = 2
        DIM = 128
        HIDDEN = 512
        B, S = (4, 256)
        key = jax.random.key(seed)
        ks = jax.random.split(key, 6)
        scale = 0.02
        x = jax.random.normal(ks[0], (B, S, DIM), dtype=jnp.float32)
        wg = jax.random.normal(ks[1], (NUM_EXPERTS, DIM), dtype=jnp.float32) * scale
        bg = jnp.zeros((NUM_EXPERTS,), dtype=jnp.float32)
        Wgate = jax.random.normal(ks[2], (NUM_EXPERTS, HIDDEN, DIM), dtype=jnp.float32) * scale
        Wup = jax.random.normal(ks[3], (NUM_EXPERTS, HIDDEN, DIM), dtype=jnp.float32) * scale
        Wdown = jax.random.normal(ks[4], (NUM_EXPERTS, DIM, HIDDEN), dtype=jnp.float32) * scale
        return {'x': x, 'wg': wg, 'bg': bg, 'Wgate': Wgate, 'Wup': Wup, 'Wdown': Wdown}
    _L0_ffn_in = _L0_ffn_setup()
    _d = {'L0_attn_a_x': _L0_attn_a_in['x'], 'L0_attn_a_Wq': _L0_attn_a_in['Wq'], 'L0_attn_a_Wk': _L0_attn_a_in['Wk'], 'L0_attn_a_Wv': _L0_attn_a_in['Wv'], 'L0_attn_a_Wo': _L0_attn_a_in['Wo'], 'L0_attn_b_ln1_w': _L0_attn_b_in['ln1_w'], 'L0_attn_b_ln1_b': _L0_attn_b_in['ln1_b'], 'L0_attn_b_ln2_w': _L0_attn_b_in['ln2_w'], 'L0_attn_b_ln2_b': _L0_attn_b_in['ln2_b'], 'L0_attn_b_in_proj_w': _L0_attn_b_in['in_proj_w'], 'L0_attn_b_conv_w': _L0_attn_b_in['conv_w'], 'L0_attn_b_conv_b': _L0_attn_b_in['conv_b'], 'L0_attn_b_dt_bias': _L0_attn_b_in['dt_bias'], 'L0_attn_b_A_log': _L0_attn_b_in['A_log'], 'L0_attn_b_D_param': _L0_attn_b_in['D_param'], 'L0_attn_b_norm_w': _L0_attn_b_in['norm_w'], 'L0_attn_b_out_proj_w': _L0_attn_b_in['out_proj_w'], 'L0_attn_b_fc_w': _L0_attn_b_in['fc_w'], 'L0_attn_b_fc_b': _L0_attn_b_in['fc_b'], 'L0_attn_b_proj_w': _L0_attn_b_in['proj_w'], 'L0_attn_b_proj_b': _L0_attn_b_in['proj_b'], 'L0_ffn_wg': _L0_ffn_in['wg'], 'L0_ffn_bg': _L0_ffn_in['bg'], 'L0_ffn_Wgate': _L0_ffn_in['Wgate'], 'L0_ffn_Wup': _L0_ffn_in['Wup'], 'L0_ffn_Wdown': _L0_ffn_in['Wdown']}
    _x0 = _d['L0_attn_a_x']
    _d['L0_attn_a_x'] = jax.random.normal(jax.random.fold_in(jax.random.key(seed), 1), (1, 2048, 128), dtype=_x0.dtype)
    del _x0
    return _d

def reference(L0_attn_a_x, L0_attn_a_Wq, L0_attn_a_Wk, L0_attn_a_Wv, L0_attn_a_Wo, L0_attn_b_ln1_w, L0_attn_b_ln1_b, L0_attn_b_ln2_w, L0_attn_b_ln2_b, L0_attn_b_in_proj_w, L0_attn_b_conv_w, L0_attn_b_conv_b, L0_attn_b_dt_bias, L0_attn_b_A_log, L0_attn_b_D_param, L0_attn_b_norm_w, L0_attn_b_out_proj_w, L0_attn_b_fc_w, L0_attn_b_fc_b, L0_attn_b_proj_w, L0_attn_b_proj_b, L0_ffn_wg, L0_ffn_bg, L0_ffn_Wgate, L0_ffn_Wup, L0_ffn_Wdown):

    def _L0_attn_a_ref(x, Wq, Wk, Wv, Wo):
        import jax, jax.numpy as jnp
        import numpy as np
        D_MODEL = 128
        N_HEADS = 16
        D_K = D_MODEL // N_HEADS
        THETA = 10000.0

        def _rope(x, pos):
            half = D_K // 2
            inv_freq = THETA ** (-jnp.arange(0, half, dtype=jnp.float32) * 2.0 / D_K)
            ang = pos[:, None].astype(jnp.float32) * inv_freq[None, :]
            cos, sin = (jnp.cos(ang), jnp.sin(ang))
            x1, x2 = (x[..., 0::2], x[..., 1::2])
            r1 = x1 * cos - x2 * sin
            r2 = x1 * sin + x2 * cos
            out = jnp.stack([r1, r2], axis=-1).reshape(x.shape)
            return out
        b, s, _ = x.shape
        pos = jnp.arange(s)

        def split_heads(t):
            return t.reshape(b, s, N_HEADS, D_K).transpose(0, 2, 1, 3).reshape(b * N_HEADS, s, D_K)
        q = split_heads(x @ Wq.T)
        k = split_heads(x @ Wk.T)
        v = split_heads(x @ Wv.T)
        q = _rope(q, pos)
        k = _rope(k, pos)
        score = jnp.einsum('bqd,bkd->bqk', q, k)
        causal = jnp.tril(jnp.ones((s, s), dtype=bool))
        score = jnp.where(causal[None], score, -jnp.inf)
        attn = jax.nn.softmax(score / jnp.sqrt(jnp.float32(D_K)), axis=-1)
        out = jnp.einsum('bqk,bkd->bqd', attn, v)
        out = out.reshape(b, N_HEADS, s, D_K).transpose(0, 2, 1, 3).reshape(b, s, D_MODEL)
        return out @ Wo.T

    def _L0_attn_b_ref(x, ln1_w, ln1_b, ln2_w, ln2_b, in_proj_w, conv_w, conv_b, dt_bias, A_log, D_param, norm_w, out_proj_w, fc_w, fc_b, proj_w, proj_b):
        import jax, jax.numpy as jnp
        import numpy as np
        from jax import lax
        D_MODEL = 128
        D_INNER = 256
        D_STATE = 64
        D_CONV = 4
        HEADDIM = 64
        NHEADS = D_INNER // HEADDIM
        CONV_DIM = D_INNER + 2 * D_STATE
        D_IN_PROJ = 2 * D_INNER + 2 * D_STATE + NHEADS
        D_FF = 4 * D_MODEL
        EPS = 1e-05

        def _layernorm(x, w, b):
            mu = jnp.mean(x, -1, keepdims=True)
            var = jnp.mean((x - mu) ** 2, -1, keepdims=True)
            return (x - mu) * lax.rsqrt(var + EPS) * w + b

        def _silu(x):
            return x * jax.nn.sigmoid(x)

        def _mamba2(x, in_proj_w, conv_w, conv_b, dt_bias, A_log, D_param, norm_w, out_proj_w):
            B, L, _ = x.shape
            zxbcdt = jnp.einsum('bld,ed->ble', x, in_proj_w)
            z = zxbcdt[..., :D_INNER]
            xBC = zxbcdt[..., D_INNER:D_INNER + CONV_DIM]
            dt_raw = zxbcdt[..., D_INNER + CONV_DIM:]
            dt = jax.nn.softplus(dt_raw + dt_bias)
            xp = jnp.pad(xBC, ((0, 0), (D_CONV - 1, 0), (0, 0)))
            xBC = sum((conv_w[:, k] * xp[:, k:k + L, :] for k in range(D_CONV))) + conv_b
            xBC = _silu(xBC)
            xs = xBC[..., :D_INNER].reshape(B, L, NHEADS, HEADDIM)
            Bm = xBC[..., D_INNER:D_INNER + D_STATE]
            Cm = xBC[..., D_INNER + D_STATE:]
            A = -jnp.exp(A_log)
            dA = jnp.exp(dt * A)
            dtx = dt[..., None] * xs

            def step(h, inp):
                dA_t, dtx_t, B_t, C_t = inp
                h = dA_t[:, :, None, None] * h + dtx_t[..., None] * B_t[:, None, None, :]
                y_t = jnp.einsum('bhpn,bn->bhp', h, C_t)
                return (h, y_t)
            h0 = jnp.zeros((B, NHEADS, HEADDIM, D_STATE), x.dtype)
            _, ys = lax.scan(step, h0, (jnp.swapaxes(dA, 0, 1), jnp.swapaxes(dtx, 0, 1), jnp.swapaxes(Bm, 0, 1), jnp.swapaxes(Cm, 0, 1)))
            y = jnp.swapaxes(ys, 0, 1) + D_param[None, None, :, None] * xs
            y = y.reshape(B, L, D_INNER)
            y = y * _silu(z)
            y = y * lax.rsqrt(jnp.mean(y * y, -1, keepdims=True) + EPS) * norm_w
            return jnp.einsum('ble,de->bld', y, out_proj_w)

        def _mlp(x, fc_w, fc_b, proj_w, proj_b):
            h = jax.nn.gelu(jnp.einsum('bld,fd->blf', x, fc_w) + fc_b, approximate=False)
            return jnp.einsum('blf,df->bld', h, proj_w) + proj_b
        x = x + _mamba2(_layernorm(x, ln1_w, ln1_b), in_proj_w, conv_w, conv_b, dt_bias, A_log, D_param, norm_w, out_proj_w)
        x = x + _mlp(_layernorm(x, ln2_w, ln2_b), fc_w, fc_b, proj_w, proj_b)
        return x

    def _L0_ffn_ref(x, wg, bg, Wgate, Wup, Wdown):
        import jax, jax.numpy as jnp
        import numpy as np
        NUM_EXPERTS = 8
        TOP_K = 2
        DIM = 128
        HIDDEN = 512
        B, S = (4, 256)
        b, s, d = x.shape
        xf = x.reshape(-1, d)
        T = xf.shape[0]
        logits = xf @ wg.T + bg
        vals, idx = jax.lax.top_k(logits, TOP_K)
        masked = jnp.full_like(logits, -jnp.inf)
        rows = jnp.arange(T)[:, None]
        masked = masked.at[rows, idx].set(vals)
        weights = jax.nn.softmax(masked, axis=-1)
        out = jnp.zeros_like(xf)
        for e in range(NUM_EXPERTS):
            g = xf @ Wgate[e].T
            u = xf @ Wup[e].T
            h = g * jax.nn.sigmoid(g) * u
            out = out + h @ Wdown[e].T * weights[:, e:e + 1]
        return out.reshape(b, s, d)
    x = L0_attn_a_x
    x = x + _L0_attn_a_ref(_layernorm(x, axis=-1), L0_attn_a_Wq, L0_attn_a_Wk, L0_attn_a_Wv, L0_attn_a_Wo)
    x = x + _L0_ffn_ref(_layernorm(x, axis=-1), L0_ffn_wg, L0_ffn_bg, L0_ffn_Wgate, L0_ffn_Wup, L0_ffn_Wdown)
    x = x + _L0_attn_b_ref(_layernorm(x, axis=-1), L0_attn_b_ln1_w, L0_attn_b_ln1_b, L0_attn_b_ln2_w, L0_attn_b_ln2_b, L0_attn_b_in_proj_w, L0_attn_b_conv_w, L0_attn_b_conv_b, L0_attn_b_dt_bias, L0_attn_b_A_log, L0_attn_b_D_param, L0_attn_b_norm_w, L0_attn_b_out_proj_w, L0_attn_b_fc_w, L0_attn_b_fc_b, L0_attn_b_proj_w, L0_attn_b_proj_b)
    x = x + _L0_ffn_ref(_layernorm(x, axis=-1), L0_ffn_wg, L0_ffn_bg, L0_ffn_Wgate, L0_ffn_Wup, L0_ffn_Wdown)
    return x

_drawn_inputs = setup_inputs


def setup_inputs(seed=0):
    import zlib

    import numpy as np

    out = dict(_drawn_inputs(seed))
    spreads = {'L0_attn_b_ln1_w': (1.0, 0.2),
     'L0_attn_b_ln1_b': (0.0, 0.578),
     'L0_attn_b_ln2_w': (1.0, 0.6),
     'L0_attn_b_ln2_b': (0.0, 0.8),
     'L0_attn_b_conv_b': (0.0, 0.1),
     'L0_attn_b_D_param': (1.0, 0.6),
     'L0_attn_b_norm_w': (1.0, 0.561),
     'L0_attn_b_fc_b': (0.0, 0.715),
     'L0_attn_b_proj_b': (0.0, 0.1),
     'L0_ffn_bg': (0.0, 0.8)}
    factors = {'L0_attn_b_dt_bias': 46.857,
     'L0_attn_b_A_log': 8.0,
     'L0_ffn_wg': 5.523,
     'L0_ffn_Wgate': 4.673,
     'L0_ffn_Wup': 4.659,
     'L0_ffn_Wdown': 4.654}
    for name, (base, spread) in spreads.items():
        noise = np.random.default_rng([zlib.crc32(name.encode()), seed]).standard_normal(out[name].shape)
        drawn = base * np.exp(spread * noise) if base else spread * noise
        out[name] = jnp.asarray(drawn.astype(out[name].dtype))
    for name, factor in factors.items():
        out[name] = (out[name] * factor).astype(out[name].dtype)
    return out
```

```python
from contextlib import ExitStack

import numpy as np

import concourse.bass as bass
from concourse import mybir

F32 = mybir.dt.float32
BF16 = mybir.dt.bfloat16
U32 = mybir.dt.uint32
I32 = mybir.dt.int32
ALU = mybir.AluOpType
ACT = mybir.ActivationFunctionType
AX_X = mybir.AxisListType.X
DS = bass.DynSlice

P = 128
T = 2048
NT = T // P
QB = 512
NQB = T // QB
TPB = QB // P
EPS = 1e-5

NH, DK = 16, 8
HG = 4
NG = NH // HG
SCALE = float(1.0 / np.sqrt(np.float32(DK)))
NEG = -1e30
Q_PARTS = (0, 0, 1, 1, 0, 2, 1, 2)
K_PARTS = (0, 1, 0, 1, 2, 0, 2, 1)
MROW = 64
UNROLL = 2
KROWS = 96


class Chain:

    def __init__(self, eng, sem):
        self.eng, self.sem, self.n = eng, sem, 0

    def __call__(self, ins):
        self.n += 1
        ins.then_inc(self.sem, 1)
        self.eng.wait_ge(self.sem, self.n)


def wait_apart(eng, sem, count, passed):
    eng.wait_ge(sem, count)
    eng.sem_inc(passed, 1)


def stage(nc, tag=""):
    ctx = ExitStack()
    sb = lambda name, shape, dt=F32: ctx.enter_context(nc.sbuf_tensor(tag + name, shape, dt))
    ps = lambda name, shape, dt=F32: ctx.enter_context(nc.psum_tensor(tag + name, shape, dt))
    sem = lambda name: nc.alloc_semaphore(tag + name)
    return ctx, sb, ps, sem


def norm_block(nc, tag, src, xn, xnt, ident, w=None, b=None):
    ctx, sb, ps, sem = stage(nc)
    with ctx:
        st = sb(f"{tag}_st", [P, NT, 6])
        half = sb(f"{tag}_half", [P, 4, NT])
        mean, var = half[:, 0], half[:, 1]
        rstd = sb(f"{tag}_rstd", [P, NT])
        std = sb(f"{tag}_std", [P, NT])
        tr = ps(f"{tag}_tr", [P, 2, QB])
        stats, step, var_ready = sem(f"{tag}_stats"), sem(f"{tag}_step"), sem(f"{tag}_var_ready")
        std_ready, xn_ready = sem(f"{tag}_std_ready"), sem(f"{tag}_xn_ready")
        turned, evacuated = sem(f"{tag}_turned"), sem(f"{tag}_evacuated")
        block = ctx.enter_context(nc.Block())

        @block.vector
        def _(dve):
            link = Chain(dve, step)
            for t in range(NT):
                dve.bn_stats(st[:, t, :], src[:, t, :]).then_inc(stats, 1)
            dve.wait_ge(stats, NT)
            link(dve.tensor_tensor(half[:, 2], st[:, :, 1], st[:, :, 4], ALU.subtract))
            link(dve.scalar_tensor_tensor(half[:, 2], half[:, 2], 0.25, half[:, 2], ALU.mult, ALU.mult))
            link(dve.tensor_tensor(half[:, 3], st[:, :, 2], st[:, :, 5], ALU.add))
            dve.scalar_tensor_tensor(var, half[:, 3], 1.0 / P, half[:, 2], ALU.mult, ALU.add).then_inc(var_ready, 1)
            link(dve.tensor_tensor(mean, st[:, :, 1], st[:, :, 4], ALU.add))
            link(dve.tensor_scalar(mean, mean, 0.5, None, ALU.mult))
            dve.wait_ge(std_ready, 1)
            link(dve.reciprocal(rstd[:], std[:]))
            for t in range(NT):
                dve.tensor_scalar(xn[:, t, :], src[:, t, :], half[:, 0, t:t + 1], rstd[:, t:t + 1],
                                  ALU.subtract, ALU.mult).then_inc(xn_ready, 1)

        @block.scalar
        def _(act):
            act.wait_ge(var_ready, 1)
            act.activation(std[:], var, ACT.Sqrt, bias=EPS).then_inc(std_ready, 1)
            for q in range(NQB if xnt is not None else 0):
                act.wait_ge(turned, q + 1)
                if w is None:
                    act.copy(xnt[:, q * QB:(q + 1) * QB], tr[:, q % 2, :]).then_inc(evacuated, 1)
                else:
                    act.activation(xnt[:, q * QB:(q + 1) * QB], tr[:, q % 2, :], ACT.Identity,
                                   bias=b, scale=w).then_inc(evacuated, 1)

        @block.tensor
        def _(pe):
            for q in range(NQB if xnt is not None else 0):
                if q >= 2:
                    pe.wait_ge(evacuated, q - 1)
                for i in range(TPB):
                    pe.wait_ge(xn_ready, q * TPB + i + 1)
                    last = pe.transpose(tr[:, q % 2, i * P:(i + 1) * P], xn[:, q * TPB + i, :], ident[:])
                last.then_inc(turned, 1)


def qkv_block(nc, xnt, weights, rope, vaug, qk_dram):
    wq, wqs, wk, wks, wv = weights
    ctx, sb, ps, sem = stage(nc)
    with ctx:
        cs = sb("rope_sb", [P, 2, 2, QB])
        t1, t2 = sb("rope_a", [P, 2, QB]), sb("rope_b", [P, 2, QB])
        rot, rest = sb("rot", [P, 3, QB]), sb("rest", [P, 3, QB])
        parts = sb("parts", [P, 4, 3, QB], BF16)
        proj = ps("proj", [P, 2, 2, QB])
        vps = ps("vps", [P, 2, QB])
        rope_in = [sem(f"rope_in{i}") for i in range(2)]
        ones = sem("ones")
        projected, rope_read, rope_sum = sem("projected"), sem("rope_read"), sem("rope_sum")
        hi_done, rest_done, mid_done, lo_done = sem("hi_done"), sem("rest_done"), sem("mid_done"), sem("lo_done")
        parts_sent = [sem(f"parts_sent{i}") for i in range(4)]
        v_done, v_copied = sem("v_done"), sem("v_copied")
        block = ctx.enter_context(nc.Block())
        NU = 2 * NQB

        @block.sync
        def _(sp):
            for n in range(NU):
                for b in ((0, 1) if n == 0 else (n // 2 + 2,) if n % 2 and n // 2 + 2 < NQB else ()):
                    if b >= 2:
                        sp.wait_ge(rope_read, 4 * (b - 1))
                    sp.dma_start(cs[:, b % 2], rope[:, :, b * QB:(b + 1) * QB]).then_inc(rope_in[b % 2], 16)
                sp.wait_ge(lo_done, n + 1)
                blk = slice(n // 2 * QB, (n // 2 + 1) * QB)
                sp.dma_start(qk_dram[n % 2, :, :, blk].rearrange("c p n -> p c n"), parts[:, n % 4]).then_inc(parts_sent[n % 4], 16)
            for i in range(4):
                sp.wait_ge(parts_sent[i], 16 * NU // 4)

        @block.gpsimd
        def _(pool):
            pool.memset(vaug[:, :, :, DK:DK + 1], 1.0).then_inc(ones, 1)
            pool.wait_ge(ones, 1)

        @block.tensor
        def _(pe):
            for n in range(NU):
                if n >= 2:
                    pe.wait_ge(rope_read, 2 * (n - 1))
                blk = slice(n // 2 * QB, (n // 2 + 1) * QB)
                for s, wt in enumerate(((wq, wqs), (wk, wks))[n % 2]):
                    last = pe.matmul(proj[:, n % 2, s, :], wt, xnt[:, blk], start=True, stop=True)
                last.then_inc(projected, 1)
                if n % 2:
                    b = n // 2
                    if b >= 2:
                        pe.wait_ge(v_copied, b - 1)
                    for i in range(TPB):
                        t = b * TPB + i
                        last = pe.matmul(vps[:, b % 2, i * P:(i + 1) * P], xnt[:, t * P:(t + 1) * P], wv,
                                         start=True, stop=True)
                    last.then_inc(v_done, 1)

        @block.vector
        def _(dve):
            for s in range(NU + 2):
                if s < NU:
                    tab = cs[:, s // 2 % 2]
                    dve.wait_ge(rope_in[s // 2 % 2], 16 * (s // 4 + 1))
                    dve.wait_ge(projected, s + 1)
                    dve.tensor_tensor(t1[:, s % 2], proj[:, s % 2, 0], tab[:, 0], ALU.mult).then_inc(rope_read, 1)
                    dve.tensor_tensor(t2[:, s % 2], proj[:, s % 2, 1], tab[:, 1], ALU.mult).then_inc(rope_read, 1)
                    dve.wait_ge(rope_read, 2 * s + 2)
                    dve.tensor_tensor(rot[:, s % 3], t1[:, s % 2], t2[:, s % 2], ALU.add).then_inc(rope_sum, 1)
                if 1 <= s <= NU:
                    n = s - 1
                    dve.wait_ge(hi_done, n + 1)
                    dve.tensor_tensor(rest[:, n % 3], rot[:, n % 3], parts[:, n % 4, 0], ALU.subtract).then_inc(rest_done, 1)
                if s >= 2:
                    n = s - 2
                    dve.wait_ge(mid_done, n + 1)
                    dve.tensor_tensor(parts[:, n % 4, 2], rest[:, n % 3], parts[:, n % 4, 1], ALU.subtract).then_inc(lo_done, 1)

        @block.scalar
        def _(act):
            for s in range(NU + 1):
                if s < NU:
                    act.wait_ge(rope_sum, s + 1)
                    if s >= 4:
                        act.wait_ge(parts_sent[s % 4], 16 * (s // 4))
                    act.copy(parts[:, s % 4, 0], rot[:, s % 3]).then_inc(hi_done, 1)
                if s >= 1:
                    n = s - 1
                    act.wait_ge(rest_done, n + 1)
                    act.copy(parts[:, n % 4, 1], rest[:, n % 3]).then_inc(mid_done, 1)
                if s % 2 and s < NU:
                    b = s // 2
                    act.wait_ge(v_done, b + 1)
                    act.copy(vaug[:, b * TPB:(b + 1) * TPB, :, 0:DK],
                             vps[:, b % 2].rearrange("p (i h d) -> p i h d", i=TPB, d=DK)).then_inc(v_copied, 1)


def attention_plan():
    steps = []
    for j in range(NQB):
        for p in range(2 * j):
            steps.append((j, [(2 * p, 0, 0), (2 * p + 1, QB, 0)], 2 * QB))
        d = TPB * j
        steps.append((j, [(d, 0, 0), (d + 1, QB, P), (d + 3, QB + 3 * P, 3 * P)], 2 * QB))
        steps.append((j, [(d + 2, 0, 2 * P)], 2 * P))
    units = {j: [(j, i, h, b) for i in range(TPB) for h in range(HG) for b in range(j + 1)] for j in range(NQB)}
    lead = (0, 1)
    order = [j for j in range(NQB) if j not in lead] + [j for j in lead]
    events, pv, late = [], [], []
    t_exp = t_max = 0.0
    ready = {j: 0.0 for j in lead}
    todo = [(j, u) for j in order for u in units[j]]
    m = 0

    def due(t):
        for x in sorted([x for x in late if x[0] <= t], key=lambda x: x[0]):
            late.remove(x)
            events.append(x[1])

    def maxima(t):
        nonlocal t_max, m
        while m < len(todo) and t_max <= t:
            j, u = todo[m]
            events.append(("max", u, m))
            t_max = t_max + 0.63
            m += 1
            if m == len(todo) or todo[m][0] != j:
                events.append(("chain", j))
                late.append((t_max + 3.0, ("rows", j)))
                if j not in lead:
                    ready[j] = t_max + 6.0
            due(t_max)

    slot = 0
    for s, (j, tiles, width) in enumerate(steps):
        while j not in ready:
            maxima(t_max)
        t_exp = max(t_exp, ready[j])
        for h in range(HG if width > 2 * P else 1):
            maxima(t_exp)
            due(t_exp)
            events.append(("scores", s, h, slot))
            slot += 1
            t_exp += 1.05
            if pv and (h % 2 or width == 2 * P):
                events.append(("values",) + pv.pop(0))
        while pv:
            events.append(("values",) + pv.pop(0))
        cut = 1 if len(tiles) > 1 else 0
        pv = [(s, 0)] + [(s, 1)] * cut
    while pv:
        events.append(("values",) + pv.pop(0))
    maxima(1e9)
    due(1e9)
    out, seen = [], {}
    for e in events:
        out.append(e)
        if e[0] == "values" and (e[1] + 1 == len(steps) or steps[e[1] + 1][0] != steps[e[1]][0]):
            seen[steps[e[1]][0]] = len(out)
            out.append(("gather", steps[e[1]][0]))
    final = []
    hold = None
    for e in out:
        final.append(e)
        if e[0] == "gather":
            hold = [e[1], 2]
        elif hold and e[0] == "scores":
            hold[1] -= 1
            if hold[1] == 0:
                final.append(("turn", hold[0]))
                hold = None
    if hold:
        final.append(("turn", hold[0]))
    return steps, units, lead, final, slot


def attention_block(nc, qk_dram, vaug, ao, ident, identb, maskq):
    steps, units, lead, events, slots = attention_plan()
    n_steps, n_max = len(steps), sum(len(u) for u in units.values())
    n_lead = sum(len(units[j]) for j in lead)
    ctx, sb, ps, sem = stage(nc)
    with ctx:
        qst = [sb(f"qst{i}", [P, HG, T], BF16) for i in range(2)]
        kst = [sb(f"kst{i}", [P, HG, T], BF16) for i in range(2)]
        vg = sb("vg", [P, 2, NT, HG, DK + 1])
        prob = sb("prob", [P, 2, HG, 2 * QB])
        pmax = sb("pmax", [P, 2, TPB * HG, NQB])
        small = sb("small", [P, 3, TPB * HG])
        nt = sb("nt", [P, TPB, 3, HG], BF16)
        ntt = sb("ntt", [3 * HG, QB], BF16)
        osb = sb("osb", [P, QB])
        rec = sb("rec", [P, TPB, HG])
        s_ps = ps("s_ps", [P, 2, 2 * QB])
        m_ps = ps("m_ps", [P, 2, QB])
        o_ps = ps("o_ps", [P, QB])
        t_ps = ps("t_ps", [P, QB])
        dve_passed, pool_passed = sem("dve_passed"), sem("pool_passed")
        cleared, stack_in = sem("cleared"), [sem(f"stack_in{i}") for i in range(2)]
        scores_ready, exp_done = sem("scores_ready"), sem("exp_done")
        pv_done, max_ready, reduced = sem("pv_done"), sem("max_ready"), sem("reduced")
        max_found = sem("max_found")
        pool_step, nt_ready, nt_turned = sem("pool_step"), sem("nt_ready"), sem("nt_turned")
        ntt_ready, mrow_in, turn_free = sem("ntt_ready"), sem("mrow_in"), sem("turn_free")
        v_here, o_copied, o_turned = sem("v_here"), sem("o_copied"), sem("o_turned")
        pool_ready, rec_done, cut_done = sem("pool_ready"), sem("rec_done"), sem("cut_done")
        block = ctx.enter_context(nc.Block())
        CREDIT = 2
        STACK_IN = 16 * (2 * len(Q_PARTS) + 1)

        def loop(eng, body):
            if UNROLL == NG:
                for g in range(NG):
                    body(lambda per, n, g=g: g * per + n, g, g == NG - 1)
            else:
                with eng.Fori(0, NG // UNROLL) as turn:
                    for g in range(UNROLL):
                        body(lambda per, n, g=g: turn * (UNROLL * per) + (g * per + n), g, False)

        def diagonal(tiles):
            return tiles[0][0] if len(tiles) == 3 or len(tiles) == 1 else None

        def pe_max(pe, g, unit, idx, n):
            j, i, h, b = unit
            if n >= 2:
                pe.wait_ge(reduced, idx)
            w = QB if b < j else (i + 1) * P
            tile = TPB * j + i
            pe.matmul(m_ps[:, n % 2, 0:w], qst[g][0:KROWS, h, tile * P:(tile + 1) * P],
                      kst[g][0:KROWS, h, b * QB:b * QB + w], start=True, stop=True).then_inc(max_ready, 1)

        def pe_rows(pe, c, c1, use):
            pe.wait_ge(nt_ready, c1)
            pe.wait_ge(turn_free, use)
            for i in range(TPB):
                last = pe.transpose(t_ps[:].bitcast(BF16)[0:3 * HG, i * P:(i + 1) * P],
                                    nt[:, i].rearrange("p c h -> p (c h)"), identb[:])
            last.then_inc(nt_turned, 1)

        def dve_max(dve, unit, idx1, n):
            j, i, h, b = unit
            wait_apart(dve, max_ready, idx1, dve_passed)
            found = pmax[:, j % 2, i * HG + h, b:b + 1]
            if b < j:
                dve.reduce_max(found, m_ps[:, n % 2], AX_X).then_inc(reduced, 1)
            else:
                w = (i + 1) * P
                dve.tensor_tensor_reduce(m_ps[:, n % 2, 0:w], m_ps[:, n % 2, 0:w], maskq[:, QB - w:QB], 1.0, NEG,
                                         ALU.add, ALU.max, found).then_inc(reduced, 1)

        def dve_chain(dve, j, idx, c, first):
            dve.wait_ge(reduced, idx)
            if not first:
                dve.wait_ge(nt_ready, c)
            dve.reduce_max(small[:, 0].rearrange("p (a o) -> p a o", o=1), pmax[:, j % 2, :, 0:j + 1], AX_X).then_inc(max_found, 1)

        def pool_chain(pool, count, c, first):
            pool.wait_ge(max_found, count(NQB, c + 1))
            hi, mid, lo = (nt[:, :, k, :] for k in range(3))
            neg = small[:, 1].rearrange("p (i h) -> p i h", h=HG)
            rst = small[:, 2].rearrange("p (i h) -> p i h", h=HG)
            if not first:
                wait_apart(pool, nt_turned, count(NQB, c), pool_passed)
            pool.tensor_scalar(small[:, 1], small[:, 0], -1.0, None, ALU.mult).then_inc(pool_step, 1)
            wait_apart(pool, pool_step, count(4 * NQB, 4 * c + 1), pool_passed)
            pool.tensor_copy(hi, neg).then_inc(pool_step, 1)
            pool.wait_ge(pool_step, count(4 * NQB, 4 * c + 2))
            pool.tensor_tensor(rst, neg, hi, ALU.subtract).then_inc(pool_step, 1)
            wait_apart(pool, pool_step, count(4 * NQB, 4 * c + 3), pool_passed)
            pool.tensor_copy(mid, rst).then_inc(pool_step, 1)
            pool.wait_ge(pool_step, count(4 * NQB, 4 * c + 4))
            pool.tensor_tensor(lo, rst, mid, ALU.subtract).then_inc(nt_ready, 1)
            pool.wait_ge(nt_ready, count(NQB, c + 1))

        def act_rows(act, count, c, first):
            act.wait_ge(nt_turned, count(NQB, c + 1))
            if not first:
                act.wait_ge(mrow_in, count(48 * NQB, 48 * c))
            act.copy(ntt[:], t_ps[:].bitcast(BF16)[0:3 * HG, 0:QB]).then_inc(ntt_ready, 1)
            act.wait_ge(ntt_ready, count(NQB, c + 1))
            act.sem_inc(turn_free, 1)

        def sp_rows(sp, count, g, j, c):
            sp.wait_ge(ntt_ready, count(NQB, c + 1))
            for k in range(3):
                sp.dma_start(qst[g][MROW + k:MROW + k + 1, :, j * QB:(j + 1) * QB],
                             ntt[HG * k:HG * (k + 1), :]).then_inc(mrow_in, 16)

        def sp_stacks(sp, buf, head_row):
            sp.dma_start(qst[buf][MROW:MROW + 3], qst[buf][MROW + 3:MROW + 6]).then_inc(stack_in[buf], 16)
            for which, stack, order in ((0, qst[buf], Q_PARTS), (1, kst[buf], K_PARTS)):
                for r, part in enumerate(order):
                    sp.dma_start(stack[r * DK:(r + 1) * DK],
                                 qk_dram[which, part, DS(head_row, HG * DK), :].rearrange("(h d) n -> d h n", d=DK)).then_inc(stack_in[buf], 16)

        def copy_v(pool, buf, head):
            pool.tensor_copy(vg[:, buf], vaug[:, :, DS(head, HG), :]).then_inc(v_here, 1)

        def next_c(j):
            return j + NQB if j in lead else j

        @block.tensor
        def _(pe):
            n = 0
            pe.wait_ge(cleared, 5)
            pe.wait_ge(stack_in[0], STACK_IN)
            for j in lead:
                for u in units[j]:
                    pe_max(pe, 0, u, n - 1, n)
                    n += 1
                pe_rows(pe, j, j + 1, j)

            def body(count, g, end):
                use = 0
                b = g % 2
                for e in events:
                    if e[0] == "max":
                        if end and e[1][0] in lead:
                            continue
                        ahead = e[1][0] in lead
                        if ahead and e[1] == units[lead[0]][0]:
                            pe.wait_ge(stack_in[1 - b], count(STACK_IN // 2, STACK_IN if b == 0 else STACK_IN * 3 // 2))
                        pe_max(pe, 1 - b if ahead else b, e[1], count(n_max, n_lead + e[2] - 1), n_lead + e[2])
                    elif e[0] == "rows":
                        if end and e[1] in lead:
                            continue
                        c = next_c(e[1])
                        pe_rows(pe, c, count(NQB, c + 1), count(2 * NQB, len(lead) + use))
                        use += 1
                    elif e[0] == "scores":
                        _, s, h, slot = e
                        j, tiles, width = steps[s]
                        pe.wait_ge(exp_done, count(slots, slot - 1 + CREDIT))
                        if h == 0 and (s == 0 or steps[s - 1][0] != j):
                            pe.wait_ge(mrow_in, count(48 * NQB, 48 * (j + 1)))
                        out = s_ps[:, slot % 2]
                        todo = [(h, c) for c in tiles] if width > 2 * P else [(hh, (kt, hh * 2 * P, q0)) for hh in range(HG) for kt, _, q0 in tiles]
                        for hh, (kt, col, q0) in todo:
                            last = pe.matmul(out[:, col:col + QB - q0], kst[b][0:KROWS, hh, kt * P:(kt + 1) * P],
                                             qst[b][0:KROWS, hh, j * QB + q0:(j + 1) * QB], start=True, stop=True)
                        last.then_inc(scores_ready, 1)
                    elif e[0] == "values":
                        _, s, half = e
                        j, tiles, width = steps[s]
                        if half == 0:
                            pe.wait_ge(exp_done, count(slots, last_slot(events, s) + 1 + CREDIT))
                            if diagonal(tiles) is not None:
                                pe.wait_ge(cut_done, count(2 * NQB, 2 * j + (1 if width > 2 * P else 2)))
                            if s == 0:
                                pe.wait_ge(v_here, count(1, 1))
                            if s == 0 or steps[s - 1][0] != j:
                                pe.wait_ge(o_copied, count(NQB, j + 1))
                        for kt, col, q0 in tiles[:1] if half == 0 else tiles[1:]:
                            for hh in range(HG):
                                src = prob[:, s % 2, hh, col:col + QB - q0] if width > 2 * P else \
                                    prob[:, s % 2, 0, hh * 2 * P:(hh + 1) * 2 * P]
                                last = pe.matmul(o_ps[32 * hh:32 * hh + DK + 1, q0:QB], vg[:, b, kt, hh, :], src,
                                                 start=(kt == 0), stop=(kt == TPB * j + 2), skip_group_check=True,
                                                 tile_position=(0, 32 * hh))
                        if half == 1 or len(tiles) == 1:
                            last.then_inc(pv_done, 1)
                    elif e[0] == "turn":
                        pe.wait_ge(o_copied, count(NQB, e[1] + 2))
                        pe.wait_ge(turn_free, count(2 * NQB, len(lead) + use))
                        use += 1
                        for i in range(TPB):
                            last = pe.transpose(t_ps[:, i * P:(i + 1) * P], osb[:, i * P:(i + 1) * P], ident[:])
                        last.then_inc(o_turned, 1)

            loop(pe, body)

        @block.vector
        def _(dve):
            dve.memset(o_ps[:], 0.0).then_inc(cleared, 1)
            for i in range(2):
                dve.memset(qst[i][MROW:KROWS].bitcast(U32), 0).then_inc(cleared, 1)
            n = 0
            for j in lead:
                for u in units[j]:
                    dve_max(dve, u, n + 1, n)
                    n += 1
                dve_chain(dve, j, n, j, j == 0)

            def body(count, g, end):
                for e in events:
                    if end and (e[0] == "max" and e[1][0] in lead or e[0] == "chain" and e[1] in lead):
                        continue
                    if e[0] == "max":
                        dve_max(dve, e[1], count(n_max, n_lead + e[2] + 1), n_lead + e[2])
                        found = e[2] + 1
                    elif e[0] == "chain":
                        dve_chain(dve, e[1], count(n_max, n_lead + found), count(NQB, next_c(e[1])), False)
                    elif e[0] == "turn":
                        j = e[1]
                        dve.wait_ge(o_turned, count(NQB, j + 2))
                        v = t_ps[:].rearrange("p (i h d) -> p i h d", i=TPB, h=HG)
                        dve.reciprocal(rec[:], v[:, :, :, DK]).then_inc(rec_done, 1)
                        dve.wait_ge(rec_done, count(NQB, j + 1))
                        dve.tensor_tensor(ao[:, j * TPB:(j + 1) * TPB, DS(count(HG * DK, 0), HG * DK)].rearrange("p i (h d) -> p i h d", h=HG),
                                          v[:, :, :, 0:DK], rec[:].rearrange("p i (h o) -> p i h o", o=1).broadcast_to([P, TPB, HG, DK]),
                                          ALU.mult).then_inc(turn_free, 1)

            loop(dve, body)

        @block.scalar
        def _(act):
            act.sem_inc(exp_done, CREDIT)
            act.sem_inc(pv_done, CREDIT)
            act.sem_inc(o_copied, 1)
            act.sem_inc(o_turned, 1)
            plain = lambda per, n: n
            for j in lead:
                act_rows(act, plain, j, j == 0)

            def body(count, g, end):
                for e in events:
                    if e[0] == "rows":
                        if end and e[1] in lead:
                            continue
                        act_rows(act, count, next_c(e[1]), False)
                    elif e[0] == "scores":
                        _, s, h, slot = e
                        act.wait_ge(scores_ready, count(slots, slot + 1))
                        if h == 0:
                            act.wait_ge(pv_done, count(n_steps, s - 1 + CREDIT))
                        act.activation(prob[:, s % 2, h, :], s_ps[:, slot % 2], ACT.Exp, scale=SCALE).then_inc(exp_done, 1)
                    elif e[0] == "gather":
                        j = e[1]
                        done = max(s for s, st in enumerate(steps) if st[0] == j) + 1
                        act.wait_ge(pv_done, count(n_steps, done + CREDIT))
                        act.wait_ge(o_turned, count(NQB, j + 1))
                        act.copy(osb[:], o_ps[:]).then_inc(o_copied, 1)

            loop(act, body)

        @block.gpsimd
        def _(pool):
            for i in range(2):
                pool.memset(kst[i][MROW:KROWS].bitcast(U32), 0).then_inc(pool_ready, 1)
                pool.wait_ge(pool_ready, 2 * i + 1)
                pool.memset(kst[i][MROW:MROW + 3], 1.0).then_inc(pool_ready, 1)
                pool.wait_ge(pool_ready, 2 * i + 2)
            pool.sem_inc(cleared, 2)
            copy_v(pool, 0, 0)
            plain = lambda per, n: n
            for j in lead:
                pool_chain(pool, plain, j, j == 0)

            def body(count, g, end):
                for e in events:
                    if e[0] == "chain":
                        if not (end and e[1] in lead):
                            pool_chain(pool, count, next_c(e[1]), False)
                    elif e[0] == "values" and e[1] == 3 and e[2] == 0 and not end:
                        pool.wait_ge(pv_done, count(n_steps, CREDIT))
                        copy_v(pool, 1 - g % 2, (count(HG, HG)) % NH)
                    elif e[0] == "scores":
                        _, s, h, slot = e
                        j, tiles, width = steps[s]
                        if diagonal(tiles) is None or (width > 2 * P and h < HG - 1):
                            continue
                        wait_apart(pool, exp_done, count(slots, slot + 1 + CREDIT), pool_passed)
                        src = prob[:, s % 2]
                        if width > 2 * P:
                            cuts = [src[:, :, c:c + P] for _, c, _ in tiles]
                        else:
                            cuts = [src[:, 0].rearrange("p (h q) -> p h q", h=HG)[:, :, 0:P]]
                        for cut in cuts:
                            last = pool.affine_select(out=cut, in_=cut, compare_op=ALU.is_ge, fill=0.0, base=0,
                                                      pattern=[[0, HG], [1, P]], channel_multiplier=-1)
                        last.then_inc(cut_done, 1)

            loop(pool, body)

        @block.sync
        def _(sp):
            sp.wait_ge(cleared, 5)
            sp_stacks(sp, 0, 0)
            sp_stacks(sp, 1, HG * DK)
            plain = lambda per, n: n
            for j in lead:
                sp_rows(sp, plain, 0, j, j)

            def body(count, g, end):
                for e in events:
                    if e[0] == "rows":
                        j = e[1]
                        if end and j in lead:
                            continue
                        sp_rows(sp, count, 1 - g % 2 if j in lead else g % 2, j, next_c(j))
                if UNROLL < NG or g + 2 < NG:
                    sp.wait_ge(scores_ready, count(slots, slots))
                    sp_stacks(sp, g % 2, count(HG * DK, 2 * HG * DK) % (NH * DK))

            loop(sp, body)
            sp.wait_ge(mrow_in, 48 * (NQB * NG + (len(lead) if UNROLL < NG else 0)))
            for i in range(2):
                sp.wait_ge(stack_in[i], STACK_IN * (NG // 2 + (1 if UNROLL < NG else 0)))


def last_slot(events, s):
    return max(e[3] for e in events if e[0] == "scores" and e[1] == s)


def project_add_block(nc, src, w, x, ident):
    ctx, sb, ps, sem = stage(nc)
    with ctx:
        turned_sb = sb("pa_t", [P, 2, QB])
        tr, out = ps("pa_tr", [P, 2, QB]), ps("pa_out", [P, 2, QB])
        turned, copied, projected, added = sem("pa_turned"), sem("pa_copied"), sem("pa_projected"), sem("pa_added")
        block = ctx.enter_context(nc.Block())

        @block.tensor
        def _(pe):
            for q in range(NQB + 1):
                if q < NQB:
                    if q >= 2:
                        pe.wait_ge(copied, q - 1)
                    for i in range(TPB):
                        last = pe.transpose(tr[:, q % 2, i * P:(i + 1) * P], src[:, q * TPB + i, :], ident[:])
                    last.then_inc(turned, 1)
                if q >= 1:
                    n = q - 1
                    pe.wait_ge(copied, n + 1)
                    if n >= 2:
                        pe.wait_ge(added, n - 1)
                    for i in range(TPB):
                        last = pe.matmul(out[:, n % 2, i * P:(i + 1) * P], turned_sb[:, n % 2, i * P:(i + 1) * P], w,
                                         start=True, stop=True)
                    last.then_inc(projected, 1)

        @block.scalar
        def _(act):
            for q in range(NQB):
                act.wait_ge(turned, q + 1)
                if q >= 2:
                    act.wait_ge(projected, q - 1)
                act.copy(turned_sb[:, q % 2], tr[:, q % 2]).then_inc(copied, 1)

        @block.vector
        def _(dve):
            for q in range(NQB):
                dve.wait_ge(projected, q + 1)
                xs = x[:, q * TPB:(q + 1) * TPB, :].rearrange("p t d -> p (t d)")
                dve.tensor_tensor(xs, xs, out[:, q % 2], ALU.add).then_inc(added, 1)


NE, DH = 8, 512
HC = DH // P
SLOT_TILES = (2 * T + NE * (P - 1)) // P
SLOT_TILES += SLOT_TILES % 2
DUMP = 2 * T


def moe_tables():
    row = lambda v: np.broadcast_to(np.asarray(v, np.float32), (P, len(v)))
    tok = (np.arange(NT)[None, :] * P + np.arange(P)[:, None] + 1).astype(np.float32)
    return np.ascontiguousarray(np.concatenate([
        row(NE - np.arange(NE)), row(np.arange(P)), row(np.arange(SLOT_TILES)), tok, tok + np.float32(T),
        (DUMP + 1 + np.arange(SLOT_TILES)[None, :] * P + np.arange(P)[:, None]).astype(np.float32), row(np.arange(P))[:, :P] > np.arange(P)[:, None],
        np.ones((P, P), np.float32)], axis=1).astype(np.float32))


def moe_table_slices(t):
    out, at = [], 0
    for n in (NE, P, SLOT_TILES, 2 * NT, SLOT_TILES, P, P):
        out.append(t[:, at:at + n])
        at += n
    return out


def route_block(nc, tag, xn, xnt, wg, bg, tables, route, xn_dram):
    weights, src_idx, dst_idx, expert_of = route
    desc, iota_lo, iota_hi, token1, dump, before, ones = moe_table_slices(tables)
    ctx, sb, ps, sem = stage(nc, tag)
    with ctx:
        lg = sb("lg", [P, NT, NE])
        one = sb("one", [P, 2, NT, NE])
        tmp, key = sb("rt_tmp", [P, NT, NE]), sb("rt_key", [P, NT, NE])
        both = sb("both", [P, NT, NE])
        top, kmax = sb("top", [P, 2, NT]), sb("kmax", [P, 2, NT])
        ex, den = sb("rt_ex", [P, 2, NT]), sb("rt_den", [P, NT])
        cum = sb("cum", [P, 2, NT, NE])
        cnt = sb("cnt", [P, NE], I32)
        tiles_e, tcum, base = sb("tiles_e", [P, NE]), sb("tcum", [P, 2, NE]), sb("base", [P, NE])
        slot = sb("slot", [P, 2, NT])
        sloti, part = sb("sloti", [P, 2, NT], I32), sb("part", [P, 2, 2, NT], I32)
        hilo = sb("hilo", [P, 2, 2, NT])
        onelo, onehi = sb("onelo", [P, 4, P]), sb("onehi", [P, 4, SLOT_TILES])
        inv, t2 = sb("inv", [P, SLOT_TILES]), sb("inv2", [P, 3, SLOT_TILES])
        ge = sb("ge", [P, SLOT_TILES, NE])
        eo = sb("eo", [P, SLOT_TILES])
        lg_ps, rank_ps, tot_ps = ps("lg_ps", [P, NT, NE]), ps("rank_ps", [P, NT, NE]), ps("tot_ps", [P, NT, NE])
        inv_ps = ps("inv_ps", [P, SLOT_TILES])
        xn_out, step, logits_ready = sem("xn_out"), sem("rt_step"), sem("logits_ready")
        gap_ready, exp_ready, mask_ready, ranked = sem("gap_ready"), sem("exp_ready"), sem("mask_ready"), sem("ranked")
        hot_ready, hot_used, inv_done = sem("hot_ready"), sem("hot_used"), sem("inv_done")
        block = ctx.enter_context(nc.Block())
        bc = lambda v: v.rearrange("p (t o) -> p t o", o=1).broadcast_to([P, NT, NE])
        NHOT = 2 * NT

        @block.sync
        def _(sp):
            sp.dma_start(xn_dram.rearrange("(t p) d -> p t d", p=P), xn[:]).then_inc(xn_out, 16)
            sp.wait_ge(xn_out, 16)

        @block.tensor
        def _(pe):
            for t in range(NT):
                last = pe.matmul(lg_ps[:, t], xnt[:, t * P:(t + 1) * P], wg, start=True, stop=True)
            last.then_inc(logits_ready, 1)
            pe.wait_ge(mask_ready, 1)
            flat = both[:].rearrange("p t e -> p (t e)")
            pe.matmul(rank_ps[:].rearrange("p t e -> p (t e)"), before, flat, start=True, stop=True)
            pe.matmul(tot_ps[:].rearrange("p t e -> p (t e)"), ones, flat, start=True, stop=True).then_inc(ranked, 1)
            for n in range(NHOT):
                pe.wait_ge(hot_ready, n + 1)
                pe.matmul(inv_ps[:], onelo[:, n % 4], onehi[:, n % 4], start=(n == 0), stop=(n == NHOT - 1)).then_inc(hot_used, 1)

        @block.scalar
        def _(act):
            act.wait_ge(gap_ready, 1)
            act.activation(ex[:, 1], ex[:, 0], ACT.Exp).then_inc(exp_ready, 1)

        @block.vector
        def _(dve):
            link = Chain(dve, step)
            dve.wait_ge(logits_ready, 1)
            link(dve.tensor_tensor(lg[:], lg_ps[:], bg.rearrange("p (o e) -> p o e", o=1).broadcast_to([P, NT, NE]), ALU.add))
            for k in range(2):
                link(dve.reduce_max(top[:, k].rearrange("p (t o) -> p t o", o=1), lg[:], AX_X))
                link(dve.tensor_tensor(tmp[:], lg[:], bc(top[:, k]), ALU.is_equal))
                link(dve.tensor_tensor(key[:], tmp[:], desc.rearrange("p (o e) -> p o e", o=1).broadcast_to([P, NT, NE]), ALU.mult))
                link(dve.reduce_max(kmax[:, k].rearrange("p (t o) -> p t o", o=1), key[:], AX_X))
                link(dve.tensor_tensor(one[:, k], key[:], bc(kmax[:, k]), ALU.is_equal))
                if k == 0:
                    link(dve.tensor_scalar(tmp[:], one[:, 0], 0.0, None, ALU.is_equal))
                    link(dve.tensor_tensor(lg[:], lg[:], tmp[:], ALU.mult))
                    link(dve.scalar_tensor_tensor(lg[:], one[:, 0], -3e38, lg[:], ALU.mult, ALU.add))
            dve.tensor_tensor(both[:], one[:, 0], one[:, 1], ALU.add).then_inc(mask_ready, 1)
            dve.tensor_tensor(ex[:, 0], top[:, 1], top[:, 0], ALU.subtract).then_inc(gap_ready, 1)
            dve.wait_ge(exp_ready, 1)
            link(dve.tensor_scalar(den[:], ex[:, 1], 1.0, None, ALU.add))
            link(dve.reciprocal(weights[:, 0], den[:]))
            link(dve.tensor_tensor(weights[:, 1], weights[:, 0], ex[:, 1], ALU.mult))
            dve.wait_ge(ranked, 1)
            link(dve.tensor_copy(cum[:, 0], tot_ps[:]))
            a = 0
            for d in (1, 2, 4, 8):
                link(dve.tensor_copy(cum[:, 1 - a, 0:d], cum[:, a, 0:d]))
                link(dve.tensor_tensor(cum[:, 1 - a, d:NT], cum[:, a, d:NT], cum[:, a, 0:NT - d], ALU.add))
                a = 1 - a
            link(dve.tensor_scalar(cnt[:], cum[:, a, NT - 1], float(P - 1), None, ALU.add))
            link(dve.tensor_scalar(cnt[:], cnt[:], 7, None, ALU.arith_shift_right))
            link(dve.tensor_copy(tiles_e[:], cnt[:]))
            link(dve.tensor_copy(tcum[:, 0], tiles_e[:]))
            c = 0
            for d in (1, 2, 4):
                link(dve.tensor_copy(tcum[:, 1 - c, 0:d], tcum[:, c, 0:d]))
                link(dve.tensor_tensor(tcum[:, 1 - c, d:NE], tcum[:, c, d:NE], tcum[:, c, 0:NE - d], ALU.add))
                c = 1 - c
            link(dve.tensor_tensor(base[:], tcum[:, c], tiles_e[:], ALU.subtract))
            link(dve.tensor_tensor(ge[:], iota_hi.rearrange("p (s o) -> p s o", o=1).broadcast_to([P, SLOT_TILES, NE]),
                                   tcum[:, c].rearrange("p (o e) -> p o e", o=1).broadcast_to([P, SLOT_TILES, NE]), ALU.is_ge))
            link(dve.reduce_sum(eo[:].rearrange("p (s o) -> p s o", o=1), ge[:], AX_X))
            link(dve.tensor_scalar(expert_of[:], eo[:], float(NE - 1), float(DH), ALU.min, ALU.mult))
            link(dve.tensor_tensor(tmp[:], cum[:, a], tot_ps[:], ALU.subtract))
            link(dve.tensor_tensor(tmp[:], tmp[:], rank_ps[:], ALU.add))
            link(dve.scalar_tensor_tensor(tmp[:], base[:].rearrange("p (o e) -> p o e", o=1).broadcast_to([P, NT, NE]), float(P),
                                          tmp[:], ALU.mult, ALU.add))
            for k in range(2):
                link(dve.tensor_tensor(key[:], one[:, k], tmp[:], ALU.mult))
                link(dve.reduce_sum(slot[:, k].rearrange("p (t o) -> p t o", o=1), key[:], AX_X))
            link(dve.tensor_copy(sloti[:], slot[:]))
            link(dve.tensor_scalar(part[:, 0], sloti[:], 7, None, ALU.arith_shift_right))
            link(dve.tensor_scalar(part[:, 1], sloti[:], P - 1, None, ALU.bitwise_and))
            link(dve.tensor_copy(hilo[:], part[:]))
            for n in range(NHOT):
                k, t = n // NT, n % NT
                if n >= 4:
                    dve.wait_ge(hot_used, n - 3)
                dve.tensor_scalar(onelo[:, n % 4], iota_lo, hilo[:, 1, k, t:t + 1], None, ALU.is_equal).then_inc(inv_done, 1)
                dve.wait_ge(inv_done, n + 1)
                dve.tensor_scalar(onehi[:, n % 4], iota_hi, hilo[:, 0, k, t:t + 1], token1[:, n:n + 1],
                                  ALU.is_equal, ALU.mult).then_inc(hot_ready, 1)
            dve.wait_ge(hot_used, NHOT)
            link(dve.tensor_copy(inv[:], inv_ps[:]))
            link(dve.tensor_scalar(t2[:, 0], inv[:], 0.0, None, ALU.is_equal))
            link(dve.tensor_scalar(t2[:, 1], inv[:], float(T), float(-T), ALU.is_gt, ALU.mult))
            link(dve.tensor_tensor(t2[:, 1], t2[:, 1], t2[:, 0], ALU.add))
            link(dve.tensor_tensor(t2[:, 1], t2[:, 1], inv[:], ALU.add))
            link(dve.tensor_scalar(src_idx[:], t2[:, 1], -1.0, None, ALU.add))
            link(dve.tensor_tensor(t2[:, 2], t2[:, 0], dump, ALU.mult))
            link(dve.tensor_tensor(t2[:, 2], t2[:, 2], inv[:], ALU.add))
            link(dve.tensor_scalar(dst_idx[:], t2[:, 2], -1.0, None, ALU.add))


def experts_block(nc, tag, w_gate, w_up, w_down, route, x, ident, xn_dram, y_dram):
    weights, src_idx, dst_idx, expert_of = route
    ctx, sb, ps, sem = stage(nc, tag)
    with ctx:
        si, di = sb("si", [P, 2], U32), sb("di", [P, 2], U32)
        xg, xt = sb("xg", [P, 2, P]), sb("xt", [P, 2, P])
        sg, h, ht = sb("sg", [P, 2, DH]), sb("h", [P, 2, DH]), sb("ht", [P, 2, DH])
        yo = sb("yo", [P, 2, P])
        yb = sb("yb", [P, 2, NT, P])
        g_ps, u_ps, h_ps = ps("g_ps", [P, 2, DH]), ps("u_ps", [P, 2, DH]), ps("h_ps", [P, 2, DH])
        x_ps, y_ps = ps("x_ps", [P, P]), ps("y_ps", [P, P])
        pair = lambda name: [sem(f"{name}{i}") for i in range(2)]
        gathered, scattered = pair("gathered"), pair("scattered")
        pool_passed = sem("pool_passed")
        si_ready, di_ready = sem("si_ready"), sem("di_ready")
        x_turned, x_copied, gate_done, up_done = sem("x_turned"), sem("x_copied"), sem("gate_done"), sem("up_done")
        silu_done, h_done, h_turned, h_copied = sem("silu_done"), sem("h_done"), sem("h_turned"), sem("h_copied")
        down_done, y_copied, y_loaded, added = sem("down_done"), sem("y_copied"), sem("y_loaded"), sem("added")
        block = ctx.enter_context(nc.Block())
        S = SLOT_TILES

        def count2(t, b):
            return t * 8 + (16 - 8 * b)

        def turns(eng, step, first, last):
            for t in range(first):
                step(t, t % 2, t)
            assert (S - first - last) % 2 == 0
            with eng.Fori(0, (S - first - last) // 2) as turn:
                for k in range(2):
                    step(turn * 2 + (first + k), (first + k) % 2, None)
            for t in range(S - last, S):
                step(t, t % 2, t)

        @block.gpsimd
        def _(pool):
            def gather(t, b, at, first):
                pool.tensor_copy(si[:, b:b + 1], src_idx[:, DS(t, 1)]).then_inc(si_ready, 1)
                wait_apart(pool, si_ready, t + 1, pool_passed)
                pool.indirect_dma_start(xg[:, b], None, xn_dram, bass.IndirectOffsetOnAxis(si[:, b:b + 1], 0)).then_inc(gathered[b], 16)

            def scatter(t, b):
                pool.tensor_copy(di[:, b:b + 1], dst_idx[:, DS(t, 1)]).then_inc(di_ready, 1)
                pool.wait_ge(di_ready, t + 1)
                wait_apart(pool, y_copied, t + 1, pool_passed)
                pool.indirect_dma_start(y_dram, bass.IndirectOffsetOnAxis(di[:, b:b + 1], 0), yo[:, b], None).then_inc(scattered[b], 16)

            gather(0, 0, 0, True)
            gather(1, 1, 1, True)

            def step(t, b, at):
                if at is None or at < S - 2:
                    pool.wait_ge(x_turned, t + 1)
                    gather(t + 2, b, at, False)
                if at is None or at >= 3:
                    pool.wait_ge(scattered[1 - b], count2(t - 3, 1 - b))
                if at is None or at >= 1:
                    scatter(t - 1, 1 - b)

            turns(pool, step, 3, 3)
            pool.wait_ge(scattered[1], count2(S - 3, 1))
            scatter(S - 1, 1)

        @block.sync
        def _(sp):
            for b in range(2):
                sp.wait_ge(scattered[b], 8 * S)
            for k in range(2):
                sp.dma_start(yb[:, k], y_dram[k * T:(k + 1) * T, :].rearrange("(t p) d -> p t d", p=P)).then_inc(y_loaded, 16)

        @block.tensor
        def _(pe):
            def turn_x(t, b):
                pe.wait_ge(gathered[b], count2(t, b))
                if not isinstance(t, int) or t >= 1:
                    pe.wait_ge(x_copied, t)
                pe.transpose(x_ps[:], xg[:, b], ident).then_inc(x_turned, 1)

            def turn_h(t, b):
                pe.wait_ge(h_done, t + 1)
                for c in range(HC):
                    last = pe.transpose(h_ps[:, b, c * P:(c + 1) * P], h[:, b, c * P:(c + 1) * P], ident)
                last.then_inc(h_turned, 1)

            def down(t, b, off):
                pe.wait_ge(h_copied, t + 1)
                for c in range(HC):
                    last = pe.matmul(y_ps[:], ht[:, b, c * P:(c + 1) * P], w_down[:, DS(off + c * P, P)],
                                     start=(c == 0), stop=(c == HC - 1))
                last.then_inc(down_done, 1)

            def value(t):
                return pe.value_load(expert_of[0:1, DS(t, 1)], min_val=0, max_val=(NE - 1) * DH)

            def step(t, b, at):
                off = value(t)
                if at is None or at < S - 1:
                    turn_x(t + 1, 1 - b)
                pe.wait_ge(x_copied, t + 1)
                if at is None or at >= 2:
                    pe.wait_ge(h_done, t - 1)
                pe.matmul(g_ps[:, b], xt[:, b], w_gate[:, DS(off, DH)], start=True, stop=True).then_inc(gate_done, 1)
                if at is None or at >= 1:
                    turn_h(t - 1, 1 - b)
                pe.matmul(u_ps[:, b], xt[:, b], w_up[:, DS(off, DH)], start=True, stop=True).then_inc(up_done, 1)
                if at is None or at >= 1:
                    off_before = value(t - 1)
                    if at is None or at >= 2:
                        pe.wait_ge(y_copied, t - 1)
                    down(t - 1, 1 - b, off_before)

            turn_x(0, 0)
            turns(pe, step, 3, 3)
            turn_h(S - 1, 1)
            pe.wait_ge(y_copied, S - 1)
            down(S - 1, 1, value(S - 1))

        @block.scalar
        def _(act):
            def copy_h(t, b):
                act.wait_ge(h_turned, t + 1)
                act.wait_ge(down_done, t - 1) if not isinstance(t, int) or t >= 2 else None
                act.copy(ht[:, b], h_ps[:, b]).then_inc(h_copied, 1)

            def step(t, b, at):
                act.wait_ge(gate_done, t + 1)
                if at is None or at >= 2:
                    act.wait_ge(h_done, t - 1)
                act.activation(sg[:, b], g_ps[:, b], ACT.Silu).then_inc(silu_done, 1)
                if at is None or at >= 1:
                    copy_h(t - 1, 1 - b)

            turns(act, step, 3, 3)
            copy_h(S - 1, 1)

        @block.vector
        def _(dve):
            def copy_x(t, b):
                dve.wait_ge(x_turned, t + 1)
                if not isinstance(t, int) or t >= 2:
                    dve.wait_ge(up_done, t - 1)
                dve.tensor_copy(xt[:, b], x_ps[:]).then_inc(x_copied, 1)

            def copy_y(t, b):
                dve.wait_ge(down_done, t + 1)
                if not isinstance(t, int) or t >= 2:
                    dve.wait_ge(scattered[b], count2(t - 2, b))
                dve.tensor_copy(yo[:, b], y_ps[:]).then_inc(y_copied, 1)

            def step(t, b, at):
                if at is None or at < S - 1:
                    copy_x(t + 1, 1 - b)
                dve.wait_ge(up_done, t + 1)
                dve.wait_ge(silu_done, t + 1)
                if at is None or at >= 2:
                    dve.wait_ge(h_turned, t - 1)
                dve.tensor_tensor(h[:, b], sg[:, b], u_ps[:, b], ALU.mult).then_inc(h_done, 1)
                if at is None or at >= 1:
                    copy_y(t - 1, 1 - b)

            copy_x(0, 0)
            turns(dve, step, 3, 3)
            copy_y(S - 1, 1)
            dve.wait_ge(y_loaded, 32)
            for k in range(2):
                for t in range(NT):
                    if k:
                        dve.wait_ge(added, t + 1)
                    dve.scalar_tensor_tensor(x[:, t], yb[:, k, t], weights[:, k, t:t + 1], x[:, t], ALU.mult, ALU.add).then_inc(added, 1)


DI, DST, HD = 256, 64, 64
MH = DI // HD
DCONV = 4
CCH = (DI + 2 * DST) // P
FC = 512 // P
PAD = DCONV - 1
SERIES = 9


def mamba_in_block(nc, xnt, w_conv_in, w_z, w_dt, small, conv, sz, dt_raw):
    cw, cb = small["conv_w"], small["conv_b"]
    ctx, sb, ps, sem = stage(nc)
    with ctx:
        raw = sb("raw", [P, CCH, PAD + T])
        acc = sb("acc", [P, 2, QB])
        c_ps = ps("c_ps", [P, CCH, QB])
        z_ps = ps("z_ps", [P, 2, 2, DI])
        d_ps = ps("d_ps", [P, NT, MH])
        padded, projected, raw_ready = sem("padded"), sem("mi_projected"), sem("raw_ready")
        z_done, z_read, d_done, d_read = sem("z_done"), sem("z_read"), sem("d_done"), sem("d_read")
        tap, conv_done, silu_done = sem("tap"), sem("conv_done"), sem("mi_silu")
        block = ctx.enter_context(nc.Block())

        @block.tensor
        def _(pe):
            for t in range(NT):
                last = pe.matmul(d_ps[:, t], xnt[:, t * P:(t + 1) * P], w_dt, start=True, stop=True)
            last.then_inc(d_done, 1)
            for b in range(NQB):
                for c in range(CCH):
                    if b:
                        pe.wait_ge(raw_ready, (b - 1) * CCH + c + 1)
                    pe.matmul(c_ps[:, c], w_conv_in[:, c * P:(c + 1) * P], xnt[:, b * QB:(b + 1) * QB],
                              start=True, stop=True).then_inc(projected, 1)
                for half in range(2):
                    n = 2 * b + half
                    if n >= 2:
                        pe.wait_ge(z_read, n - 1)
                    for i in range(2):
                        t = 2 * n + i
                        last = pe.matmul(z_ps[:, n % 2, i], xnt[:, t * P:(t + 1) * P], w_z, start=True, stop=True)
                    last.then_inc(z_done, 1)

        @block.scalar
        def _(act):
            for b in range(NQB):
                for c in range(CCH):
                    n = b * CCH + c
                    act.wait_ge(projected, n + 1)
                    act.copy(raw[:, c, PAD + b * QB:PAD + (b + 1) * QB], c_ps[:, c]).then_inc(raw_ready, 1)
                for half in range(2):
                    n = 2 * b + half
                    act.wait_ge(z_done, n + 1)
                    act.activation(sz[:, 2 * n:2 * n + 2], z_ps[:, n % 2], ACT.Silu).then_inc(z_read, 1)
                for c in range(CCH):
                    n = b * CCH + c
                    act.wait_ge(conv_done, n + 1)
                    blk = conv[:, c, b * QB:(b + 1) * QB]
                    act.activation(blk, acc[:, n % 2], ACT.Silu).then_inc(silu_done, 1)

        @block.vector
        def _(dve):
            dve.memset(raw[:, :, 0:PAD], 0.0).then_inc(padded, 1)
            dve.wait_ge(padded, 1)
            dve.wait_ge(d_done, 1)
            dve.tensor_copy(dt_raw[:], d_ps[:]).then_inc(d_read, 1)
            for b in range(NQB):
                for c in range(CCH):
                    n = b * CCH + c
                    dve.wait_ge(raw_ready, n + 1)
                    if n >= 2:
                        dve.wait_ge(silu_done, n - 1)
                    at = lambda k: raw[:, c, b * QB + k:b * QB + k + QB]
                    dve.tensor_scalar(acc[:, n % 2], at(0), cw[:, c, 0:1], cb[:, c:c + 1], ALU.mult, ALU.add).then_inc(tap, 1)
                    for k in range(1, DCONV):
                        dve.wait_ge(tap, n * (DCONV - 1) + k)
                        dve.scalar_tensor_tensor(acc[:, n % 2], at(k), cw[:, c, k:k + 1], acc[:, n % 2], ALU.mult, ALU.add).then_inc(
                            tap if k < DCONV - 1 else conv_done, 1)


def mamba_rates_block(nc, dt_raw, small, dt, a, ecum, dec, etot, w_out, norm_w, u_incl, below, ones):
    ctx, sb, ps, sem = stage(nc)
    with ctx:
        v = sb("sp_v", [P, 6, NT, MH])
        ea = sb("ea", [P, MH])
        sums = ps("sums", [P, 3, QB])
        step, asked, given, a_ready, summed, exped = (sem(f"mr_{n}") for n in ("step", "asked", "given", "a_ready", "summed", "exped"))
        block = ctx.enter_context(nc.Block())
        bias = small["dt_bias"].rearrange("p (o h) -> p o h", o=1).broadcast_to([P, NT, MH])

        @block.vector
        def _(dve):
            link = Chain(dve, step)
            for c in range(2):
                link(dve.tensor_scalar(w_out[:, c], w_out[:, c], norm_w[:, c:c + 1], None, ALU.mult))
            link(dve.tensor_tensor(v[:, 0], dt_raw[:], bias, ALU.add))
            link(dve.tensor_scalar(v[:, 1], v[:, 0], -1.0, None, ALU.mult))
            link(dve.tensor_tensor(v[:, 2], v[:, 0], v[:, 1], ALU.min))
            dve.sem_inc(asked, 1)
            dve.wait_ge(given, 2)
            link(dve.tensor_scalar(v[:, 4], v[:, 3], 2.0, None, ALU.add))
            link(dve.reciprocal(v[:, 4], v[:, 4]))
            link(dve.tensor_tensor(v[:, 3], v[:, 3], v[:, 4], ALU.mult))
            link(dve.tensor_tensor(v[:, 4], v[:, 3], v[:, 3], ALU.mult))
            link(dve.tensor_scalar(v[:, 5], v[:, 4], 1.0 / (2 * SERIES - 1), 1.0 / (2 * SERIES - 3), ALU.mult, ALU.add))
            for k in range(SERIES - 2, 0, -1):
                link(dve.tensor_tensor(v[:, 5], v[:, 5], v[:, 4], ALU.mult))
                link(dve.tensor_scalar(v[:, 5], v[:, 5], 1.0 / (2 * k - 1), None, ALU.add))
            link(dve.tensor_tensor(v[:, 5], v[:, 5], v[:, 3], ALU.mult))
            link(dve.tensor_scalar(v[:, 0], v[:, 0], 0.0, None, ALU.max))
            link(dve.scalar_tensor_tensor(dt[:], v[:, 5], 2.0, v[:, 0], ALU.mult, ALU.add))
            dve.scalar_tensor_tensor(a[:], dt[:], -1.0, ea[:].rearrange("p (o h) -> p o h", o=1).broadcast_to([P, NT, MH]),
                                     ALU.mult, ALU.mult).then_inc(a_ready, 1)

        @block.scalar
        def _(act):
            act.activation(ea[:], small["A_log"], ACT.Exp).then_inc(given, 1)
            act.wait_ge(asked, 1)
            act.activation(v[:, 3], v[:, 2], ACT.Exp).then_inc(given, 1)
            act.wait_ge(summed, 1)
            for i, out in enumerate((ecum, dec, etot)):
                act.activation(out[:].rearrange("p t h -> p (t h)"), sums[:, i, 0:NT * MH], ACT.Exp).then_inc(exped, 1)

        @block.tensor
        def _(pe):
            pe.wait_ge(a_ready, 1)
            for i, lhs in enumerate((u_incl, below, ones)):
                last = pe.matmul(sums[:, i, 0:NT * MH], lhs, a[:].rearrange("p t h -> p (t h)"), start=True, stop=True)
            last.then_inc(summed, 1)


def ssd_block(nc, conv, sz, dt, a, ecum, dec, etot, d_param, y, ssq, ident, u_incl, below):
    ctx, sb, ps, sem = stage(nc)
    with ctx:
        cin = sb("cin", [P, 2, CCH, P])
        tok = sb("tok", [P, 2, CCH, P])
        ct = sb("ct", [DST, 2, P])
        r = sb("seg_in", [P, 2, MH, P])
        e = sb("seg_exp", [P, 2, MH, P])
        gm = sb("gm", [P, 2, P])
        mt = sb("mt", [P, 2, MH, P])
        dtx, dtxd, dx = sb("dtx", [P, 2, MH, HD]), sb("dtxd", [P, 2, MH, HD]), sb("dx", [P, 2, MH, HD])
        state = sb("state", [DST, 2, MH, HD])
        yt = sb("yt", [P, 2, MH, HD])
        sq = sb("sq", [P, 2, DI])
        bank = lambda name: ps(name, [P, QB])
        t_ps, c_ps, g_ps, s_ps, i_ps, y_ps, u_ps = (bank(f"ssd_{n}") for n in "tcgsiyu")
        names = ("staged r_ready dtx_ready dtxd_ready dx_ready t_done t_copied c_done c_copied g_done s_done e_done "
                 "pe_passed gm_done mt_done i_done y_done u_done sdec_done state_ready yt1 yt2 yt3 y_ready sq_done")
        s = {n: sem("ssd_" + n) for n in names.split()}
        block = ctx.enter_context(nc.Block())
        N = NT

        def turns(eng, step):
            for t in range(2):
                step(t, t % 2, t)
            with eng.Fori(0, (N - 4) // 2) as turn:
                for k in range(2):
                    step(turn * 2 + (2 + k), k, None)
            for t in range(N - 2, N):
                step(t, t % 2, t)

        some = lambda at, n: at is None or at >= n
        head = lambda v, t: v[:, DS(t, 1), :].rearrange("p o h -> p (o h)").rearrange("p (h o) -> p h o", o=1)

        @block.gpsimd
        def _(pool):
            def step(t, b, at):
                if some(at, 2):
                    pool.wait_ge(s["g_done"], t - 1)
                    pool.wait_ge(s["s_done"], t - 1)
                pool.tensor_copy(cin[:, b], conv[:, :, DS(t * P, P)]).then_inc(s["staged"], 1)
                pool.wait_ge(s["staged"], t + 1)
                pool.tensor_tensor(r[:, b], u_incl.rearrange("p (o i) -> p o i", o=1).broadcast_to([P, MH, P]),
                                   head(a, t).broadcast_to([P, MH, P]), ALU.mult).then_inc(s["r_ready"], 1)
                pool.wait_ge(s["r_ready"], t + 1)
                pool.wait_ge(s["t_copied"], t + 1)
                if some(at, 2):
                    pool.wait_ge(s["y_done"], t - 1)
                    pool.wait_ge(s["u_done"], t - 1)
                    pool.wait_ge(s["yt2"], t - 1)
                xs = tok[:, b, 0:2].rearrange("p c (h d) -> p (c h) d", d=HD)
                pool.tensor_tensor(dtx[:, b], xs, head(dt, t).broadcast_to([P, MH, HD]), ALU.mult).then_inc(s["dtx_ready"], 1)
                pool.wait_ge(s["dtx_ready"], t + 1)
                pool.tensor_tensor(dtxd[:, b], dtx[:, b], head(dec, t).broadcast_to([P, MH, HD]), ALU.mult).then_inc(s["dtxd_ready"], 1)
                pool.wait_ge(s["dtxd_ready"], t + 1)
                pool.tensor_tensor(dx[:, b], xs, d_param.rearrange("p (h o) -> p h o", o=1).broadcast_to([P, MH, HD]),
                                   ALU.mult).then_inc(s["dx_ready"], 1)
                pool.wait_ge(s["dx_ready"], t + 1)

            turns(pool, step)

        @block.tensor
        def _(pe):
            def front(t, b, at):
                pe.wait_ge(s["staged"], t + 1)
                if some(at, 1):
                    pe.wait_ge(s["t_copied"], t)
                for c in range(CCH):
                    last = pe.transpose(t_ps[:, c * P:(c + 1) * P], cin[:, b, c], ident)
                last.then_inc(s["t_done"], 1)
                pe.wait_ge(s["r_ready"], t + 1)
                if some(at, 1):
                    pe.wait_ge(s["e_done"], t)
                pe.matmul(s_ps[:], below, r[:, b].rearrange("p h i -> p (h i)"), start=True, stop=True).then_inc(s["s_done"], 1)
                wait_apart(pe, s["t_copied"], t + 1, s["pe_passed"])
                pe.transpose(c_ps[0:DST, 0:P], tok[:, b, 2, DST:P], ident).then_inc(s["c_done"], 1)
                pe.wait_ge(s["c_copied"], t + 1)
                if some(at, 1):
                    pe.wait_ge(s["gm_done"], t)
                pe.matmul(g_ps[:, 0:P], cin[0:DST, b, 2], ct[:, b], start=True, stop=True).then_inc(s["g_done"], 1)

            def step(t, b, at):
                if at is None or at < N - 1:
                    front(t + 1, 1 - b, None if at is None else at + 1)
                pe.wait_ge(s["dtxd_ready"], t + 1)
                if some(at, 1):
                    pe.wait_ge(s["state_ready"], t + 1)
                pe.matmul(u_ps[0:DST, 0:DI], tok[:, b, 2, 0:DST], dtxd[:, b].rearrange("p h d -> p (h d)"),
                          start=True, stop=True).then_inc(s["u_done"], 1)
                pe.wait_ge(s["state_ready"], t + 1)
                if some(at, 1):
                    pe.wait_ge(s["yt1"], t)
                pe.matmul(i_ps[:, 0:DI], ct[:, b], state[:, b].rearrange("p h d -> p (h d)"), start=True, stop=True).then_inc(s["i_done"], 1)
                pe.wait_ge(s["mt_done"], t + 1)
                if some(at, 1):
                    pe.wait_ge(s["yt2"], t)
                for h in range(MH):
                    last = pe.matmul(y_ps[:, h * HD:(h + 1) * HD], mt[:, b, h], dtx[:, b, h], start=True, stop=True)
                last.then_inc(s["y_done"], 1)

            front(0, 0, 0)
            turns(pe, step)

        @block.scalar
        def _(act):
            def front(t, b, at):
                act.wait_ge(s["t_done"], t + 1)
                if some(at, 2):
                    act.wait_ge(s["u_done"], t - 1)
                    act.wait_ge(s["dx_ready"], t - 1)
                act.copy(tok[:, b].rearrange("p c i -> p (c i)"), t_ps[:, 0:CCH * P]).then_inc(s["t_copied"], 1)
                act.wait_ge(s["s_done"], t + 1)
                if some(at, 2):
                    act.wait_ge(s["mt_done"], t - 1)
                act.activation(e[:, b].rearrange("p h i -> p (h i)"), s_ps[:], ACT.Exp).then_inc(s["e_done"], 1)
                act.wait_ge(s["c_done"], t + 1)
                if some(at, 2):
                    act.wait_ge(s["i_done"], t - 1)
                act.copy(ct[:, b], c_ps[0:DST, 0:P]).then_inc(s["c_copied"], 1)

            def step(t, b, at):
                if at is None or at < N - 1:
                    front(t + 1, 1 - b, None if at is None else at + 1)
                act.wait_ge(s["y_ready"], t + 1)
                if some(at, 2):
                    act.wait_ge(s["sq_done"], t - 1)
                act.activation(sq[:, b], y[:, DS(t, 1), :].rearrange("p o d -> p (o d)"), ACT.Square,
                               accum_out=ssq[:, DS(t, 1)]).then_inc(s["sq_done"], 1)

            front(0, 0, 0)
            turns(act, step)

        @block.vector
        def _(dve):
            dve.memset(state[:, 0], 0.0).then_inc(s["state_ready"], 1)

            def step(t, b, at):
                dve.wait_ge(s["g_done"], t + 1)
                if some(at, 2):
                    dve.wait_ge(s["mt_done"], t - 1)
                dve.tensor_tensor(gm[:, b], g_ps[:, 0:P], u_incl, ALU.mult).then_inc(s["gm_done"], 1)
                dve.wait_ge(s["gm_done"], t + 1)
                dve.wait_ge(s["e_done"], t + 1)
                if some(at, 2):
                    dve.wait_ge(s["y_done"], t - 1)
                dve.tensor_tensor(mt[:, b], e[:, b], gm[:, b].rearrange("p (o i) -> p o i", o=1).broadcast_to([P, MH, P]),
                                  ALU.mult).then_inc(s["mt_done"], 1)
                dve.wait_ge(s["state_ready"], t + 1)
                if some(at, 1):
                    dve.wait_ge(s["i_done"], t)
                dve.tensor_tensor(state[:, 1 - b], state[:, b], head(etot, t)[0:DST].broadcast_to([DST, MH, HD]), ALU.mult).then_inc(s["sdec_done"], 1)
                dve.wait_ge(s["sdec_done"], t + 1)
                dve.wait_ge(s["u_done"], t + 1)
                dve.tensor_tensor(state[:, 1 - b], state[:, 1 - b], u_ps[0:DST, 0:DI].rearrange("p (h d) -> p h d", d=HD), ALU.add).then_inc(s["state_ready"], 1)
                dve.wait_ge(s["i_done"], t + 1)
                if some(at, 2):
                    dve.wait_ge(s["y_ready"], t - 1)
                dve.tensor_tensor(yt[:, b], i_ps[:, 0:DI].rearrange("p (h d) -> p h d", d=HD), head(ecum, t).broadcast_to([P, MH, HD]), ALU.mult).then_inc(s["yt1"], 1)
                dve.wait_ge(s["yt1"], t + 1)
                dve.wait_ge(s["dx_ready"], t + 1)
                dve.tensor_tensor(yt[:, b], yt[:, b], dx[:, b], ALU.add).then_inc(s["yt3"], 1)
                dve.wait_ge(s["yt3"], t + 1)
                dve.wait_ge(s["y_done"], t + 1)
                dve.tensor_tensor(yt[:, b], yt[:, b], y_ps[:, 0:DI].rearrange("p (h d) -> p h d", d=HD), ALU.add).then_inc(s["yt2"], 1)
                dve.wait_ge(s["yt2"], t + 1)
                dve.tensor_tensor(y[:, DS(t, 1), :].rearrange("p o d -> p (o d)"), yt[:, b].rearrange("p h d -> p (h d)"),
                                  sz[:, DS(t, 1), :].rearrange("p o d -> p (o d)"), ALU.mult).then_inc(s["y_ready"], 1)

            turns(dve, step)


def mamba_out_block(nc, y, ssq, w_out, x0, ident):
    ctx, sb, ps, sem = stage(nc)
    with ctx:
        std, rstd = sb("mo_std", [P, NT]), sb("mo_rstd", [P, NT])
        yt = sb("mo_t", [P, 2, 2, 2, P])
        tr, out = ps("mo_tr", [P, 2, QB]), ps("mo_out", [P, 2, QB])
        std_ready, rstd_ready, turned, copied, projected, added = (
            sem(f"mo_{n}") for n in ("std", "rstd", "turned", "copied", "projected", "added"))
        block = ctx.enter_context(nc.Block())
        NPAIR = NT // 2

        @block.tensor
        def _(pe):
            for n in range(NPAIR + 1):
                if n < NPAIR:
                    if n >= 2:
                        pe.wait_ge(copied, n - 1)
                    for i in range(2):
                        for c in range(2):
                            last = pe.transpose(tr[:, n % 2, (2 * i + c) * P:(2 * i + c + 1) * P], y[:, 2 * n + i, c * P:(c + 1) * P], ident)
                    last.then_inc(turned, 1)
                if n >= 1:
                    m = n - 1
                    pe.wait_ge(copied, m + 1)
                    if m >= 2:
                        pe.wait_ge(added, 2 * (m - 1))
                    for i in range(2):
                        for c in range(2):
                            last = pe.matmul(out[:, m % 2, i * P:(i + 1) * P], yt[:, m % 2, i, c], w_out[:, c], start=(c == 0), stop=(c == 1))
                    last.then_inc(projected, 1)

        @block.scalar
        def _(act):
            act.activation(std[:], ssq[:], ACT.Sqrt, bias=EPS, scale=1.0 / DI).then_inc(std_ready, 1)
            for n in range(NPAIR):
                act.wait_ge(turned, n + 1)
                if n >= 2:
                    act.wait_ge(projected, n - 1)
                act.copy(yt[:, n % 2].rearrange("p i c t -> p (i c t)"), tr[:, n % 2]).then_inc(copied, 1)

        @block.vector
        def _(dve):
            dve.wait_ge(std_ready, 1)
            dve.reciprocal(rstd[:], std[:]).then_inc(rstd_ready, 1)
            dve.wait_ge(rstd_ready, 1)
            for n in range(NPAIR):
                dve.wait_ge(projected, n + 1)
                for i in range(2):
                    t = 2 * n + i
                    dve.scalar_tensor_tensor(x0[:, t], out[:, n % 2, i * P:(i + 1) * P], rstd[:, t:t + 1], x0[:, t], ALU.mult, ALU.add).then_inc(added, 1)


def mlp_block(nc, vt, w_fc, fc_b, w_proj, proj_b, x0, x):
    ctx, sb, ps, sem = stage(nc)
    with ctx:
        h = sb("mlp_h", [P, 2, FC, QB])
        h_ps, o_ps = ps("mlp_hps", [P, FC, QB]), ps("mlp_ops", [P, 2, QB])
        h_done, gelu_done, o_done, x_step, sum_done = (sem(f"mlp_{n}") for n in ("h_done", "gelu", "o_done", "x_step", "sum_done"))
        block = ctx.enter_context(nc.Block())

        @block.tensor
        def _(pe):
            for b in range(NQB + 1):
                if b < NQB:
                    for c in range(FC):
                        if b:
                            pe.wait_ge(gelu_done, (b - 1) * FC + c + 1)
                        pe.matmul(h_ps[:, c], w_fc[:, c * P:(c + 1) * P], vt[:, b * QB:(b + 1) * QB], start=True, stop=True).then_inc(h_done, 1)
                if b:
                    n = b - 1
                    pe.wait_ge(gelu_done, (n + 1) * FC)
                    if n >= 2:
                        pe.wait_ge(sum_done, n - 1)
                    for i in range(TPB):
                        for c in range(FC):
                            last = pe.matmul(o_ps[:, n % 2, i * P:(i + 1) * P], h[:, n % 2, c, i * P:(i + 1) * P], w_proj[:, c],
                                             start=(c == 0), stop=(c == FC - 1))
                    last.then_inc(o_done, 1)

        @block.scalar
        def _(act):
            for n in range(NQB * FC):
                b, c = n // FC, n % FC
                act.wait_ge(h_done, n + 1)
                if b >= 2:
                    act.wait_ge(o_done, b - 1)
                act.activation(h[:, b % 2, c], h_ps[:, c], ACT.Gelu, bias=fc_b[:, c:c + 1]).then_inc(gelu_done, 1)

        @block.vector
        def _(dve):
            flat = lambda v, b: v[:, b * TPB:(b + 1) * TPB, :]
            for b in range(NQB):
                dve.tensor_tensor(flat(x, b), flat(x, b), flat(x0, b), ALU.add).then_inc(x_step, 1)
            dve.wait_ge(x_step, NQB)
            for b in range(NQB):
                dve.tensor_tensor(flat(x, b), flat(x, b), proj_b.rearrange("p (o d) -> p o d", o=1).broadcast_to([P, TPB, P]), ALU.add).then_inc(x_step, 1)
            for b in range(NQB):
                dve.wait_ge(x_step, NQB + b + 1)
                dve.wait_ge(o_done, b + 1)
                dve.tensor_tensor(flat(x, b), flat(x, b), o_ps[:, b % 2].rearrange("p (t d) -> p t d", d=P), ALU.add).then_inc(sum_done, 1)


def store_block(nc, x, out):
    ctx, sb, ps, sem = stage(nc)
    with ctx:
        stored = sem("stored")
        block = ctx.enter_context(nc.Block())

        @block.sync
        def _(sp):
            sp.dma_start(out.rearrange("(t p) d -> p t d", p=P), x[:]).then_inc(stored, 16)
            sp.wait_ge(stored, 16)


def vectors_layout():
    at, cols = 0, {}
    for name, width in (("ln1_w", 1), ("ln1_b", 1), ("ln2_w", 1), ("ln2_b", 1), ("conv_w", CCH * DCONV), ("conv_b", CCH),
                        ("dt_bias", MH), ("A_log", MH), ("D", MH), ("norm_w", 2), ("fc_b", FC), ("proj_b", P)):
        cols[name] = (at, width)
        at += width
    return cols, at


def rope_tables():
    inv = (np.float32(10000.0) ** (-np.arange(0, DK // 2, dtype=np.float32) * np.float32(2.0) / np.float32(DK))).astype(np.float32)
    ang = (np.arange(T, dtype=np.float32)[:, None] * inv[None, :]).astype(np.float32)
    cos, sin = np.cos(ang).astype(np.float32), np.sin(ang).astype(np.float32)
    c = np.repeat(cos, 2, axis=1).T
    s = np.stack([-sin, sin], axis=-1).reshape(T, DK).T
    return np.ascontiguousarray(np.stack([np.tile(c, (NH, 1)), np.tile(s, (NH, 1))], axis=1))


def mask_tables():
    row, col = np.arange(P)[:, None], np.arange(P)[None, :]
    f = lambda c, v: np.where(c, np.float32(v), np.float32(0))
    zero = np.zeros((P, P), np.float32)
    return np.ascontiguousarray(np.stack([f(row == col, 1), zero, zero, zero, f(col > row, NEG), f(row <= col, 1), f(row > col, 1)], axis=1))


def setup_block(nc, loads, masks, small):
    ctx, sb, ps, sem = stage(nc)
    with ctx:
        loaded, cast = sem("loaded"), sem("cast")
        block = ctx.enter_context(nc.Block())

        @block.sync
        def _(sp):
            for dst, src in loads:
                sp.dma_start(dst, src).then_inc(loaded, 16)
            sp.wait_ge(loaded, 16 * len(loads))

        @block.vector
        def _(dve):
            dve.wait_ge(loaded, 16 * len(loads))
            for i, m in enumerate(small):
                dve.tensor_copy(m, masks[:, i]).then_inc(cast, 1)
            dve.wait_ge(cast, len(small))


def program(nc, a, out, only=("att", "moe1", "mamba", "moe2")):
    ctx, sb, ps, sem = stage(nc)
    with ctx:
        before = nc.snapshot_sems()
        x = sb("x", [P, NT, P])
        masks = sb("masks", [P, 7, P])
        ident = masks[:, 0]
        identb = sb("identb", [P, P], BF16)
        maskq = masks[:, 1:5].rearrange("p a b -> p (a b)")
        watt = sb("watt", [P, 6, P])
        by_token = lambda t: t.rearrange("(t p) d -> p t d", p=P)
        watt_in = (watt[:], a["w_att"])
        w_gate, w_up, w_down = (sb(n, [P, NE * DH]) for n in ("w_gate", "w_up", "w_down"))
        wg, bg = sb("wg", [P, NE]), sb("bg", [P, NE])
        mt = sb("moe_tables", [P, a["moe_tables"].shape[1]])
        weights = sb("weights", [P, 2, NT])
        src_idx, dst_idx = sb("src_idx", [P, SLOT_TILES], U32), sb("dst_idx", [P, SLOT_TILES], U32)
        expert_of = sb("expert_of", [P, SLOT_TILES], I32)
        route = weights, src_idx, dst_idx, expert_of
        xn_dram = nc.dram_tensor("xn_rows", [T, P], F32).ap()
        y_dram = nc.dram_tensor("expert_rows", [DUMP + SLOT_TILES * P, P], F32).ap()
        w_mamba = sb("w_mamba", [P, CCH * P + DI + MH])
        w_out, w_fc, w_proj = sb("w_out", [P, 2, P]), sb("w_fc", [P, FC * P]), sb("w_proj", [P, FC, P])
        cols, width = vectors_layout()
        vectors = sb("vectors", [P, width])
        vec = {n: vectors[:, at:at + w] for n, (at, w) in cols.items()}
        small = dict(vec, conv_w=vec["conv_w"].rearrange("p (c k) -> p c k", k=DCONV))
        setup_block(nc, [(w_mamba[:], a["w_mamba"]), (w_out[:], a["w_out"]), (w_fc[:], a["w_fc"]), (w_proj[:], a["w_proj"]),
                         (vectors[:], a["vectors"]), (x[:], by_token(a["x"])), (masks[:], a["masks"]), watt_in, (mt[:], a["moe_tables"]),
                         (wg[:], a["wg"]), (bg[:], a["bg"]), (w_gate[:], a["w_gate"]), (w_up[:], a["w_up"]), (w_down[:], a["w_down"])],
                    masks, (identb[:],))

        def mixture(tag):
            with ExitStack() as m:
                xn = m.enter_context(nc.sbuf_tensor(f"{tag}_xn", [P, NT, P], F32))
                xnt = m.enter_context(nc.sbuf_tensor(f"{tag}_xnt", [P, T], F32))
                norm_block(nc, tag, x, xn, xnt, ident)
                route_block(nc, tag + "_", xn, xnt, wg[:], bg[:], mt[:], route, xn_dram)
            experts_block(nc, tag + "_", w_gate, w_up, w_down, route, x, ident, xn_dram, y_dram)

        if "att" in only:
            with ExitStack() as att:
                sba = lambda name, shape, dt=F32: att.enter_context(nc.sbuf_tensor(name, shape, dt))
                ao = sba("ao", [P, NT, P])
                vaug = sba("vaug", [P, NT, NH, DK + 1])
                qk = nc.dram_tensor("qk_parts", [2, 3, P, T], BF16).ap()
                with ExitStack() as pre:
                    xnt = pre.enter_context(nc.sbuf_tensor("xnt", [P, T], F32))
                    norm_block(nc, "ln0", x, ao, xnt, ident)
                    qkv_block(nc, xnt, [watt[:, i] for i in range(5)], a["rope"], vaug, qk)
                nc.disable_value_cache = True
                attention_block(nc, qk, vaug, ao, ident, identb, maskq)
                nc.disable_value_cache = False
                project_add_block(nc, ao, watt[:, 5], x, ident)
        if "moe1" in only:
            mixture("moe1")
        nc.clear_and_free_semaphores(nc.allocated_since(before))
        nc.all_engine_barrier()
        if "mamba" in only:
            with ExitStack() as mam:
                sbm = lambda name, shape, dt=F32: mam.enter_context(nc.sbuf_tensor(name, shape, dt))
                x0 = sbm("x0", [P, NT, P])
                y, sz = sbm("y", [P, NT, DI]), sbm("sz", [P, NT, DI])
                conv = sbm("conv", [P, CCH, T])
                dt_raw, dt, rate, ecum, dec, etot = (sbm(n, [P, NT, MH]) for n in ("dt_raw", "dt", "rate", "ecum", "dec", "etot"))
                ssq = sbm("ssq", [P, NT])
                u_incl, below = masks[:, 5], masks[:, 6]
                norm_block(nc, "ln2", x, x0, None, ident)
                with ExitStack() as pre:
                    x0n = pre.enter_context(nc.sbuf_tensor("x0n", [P, NT, P], F32))
                    xnt = pre.enter_context(nc.sbuf_tensor("mxnt", [P, T], F32))
                    norm_block(nc, "ln3", x0, x0n, xnt, ident, vec["ln1_w"], vec["ln1_b"])
                    mamba_in_block(nc, xnt, w_mamba[:, 0:CCH * P], w_mamba[:, CCH * P:CCH * P + DI], w_mamba[:, CCH * P + DI:],
                                   small, conv, sz, dt_raw)
                mamba_rates_block(nc, dt_raw, small, dt, rate, ecum, dec, etot, w_out, vec["norm_w"], u_incl, below, mt[:, -P:])
                ssd_block(nc, conv, sz, dt, rate, ecum, dec, etot, vec["D"], y, ssq, ident, u_incl, below)
                mamba_out_block(nc, y, ssq, w_out, x0, ident)
                with ExitStack() as post:
                    x1n = post.enter_context(nc.sbuf_tensor("x1n", [P, NT, P], F32))
                    vt = post.enter_context(nc.sbuf_tensor("vt", [P, T], F32))
                    norm_block(nc, "ln4", x0, x1n, vt, ident, vec["ln2_w"], vec["ln2_b"])
                    mlp_block(nc, vt, w_fc, vec["fc_b"], w_proj, vec["proj_b"], x0, x)
        if "moe2" in only:
            mixture("moe2")
        store_block(nc, x, out)


def layouts(i):
    c = np.ascontiguousarray
    swap = np.arange(P) ^ 1
    att = [i["L0_attn_a_Wq"], i["L0_attn_a_Wq"][swap], i["L0_attn_a_Wk"], i["L0_attn_a_Wk"][swap],
           i["L0_attn_a_Wv"], i["L0_attn_a_Wo"]]
    rows = lambda v: np.broadcast_to(v, (P,) + v.shape)
    b = lambda name: i["L0_attn_b_" + name]
    w_in = b("in_proj_w")
    by_chunk = lambda v: v.reshape(-1, P).T
    vectors = {
        "ln1_w": b("ln1_w")[:, None], "ln1_b": b("ln1_b")[:, None], "ln2_w": b("ln2_w")[:, None], "ln2_b": b("ln2_b")[:, None],
        "conv_w": b("conv_w").reshape(CCH, P, DCONV).transpose(1, 0, 2).reshape(P, -1), "conv_b": by_chunk(b("conv_b")),
        "dt_bias": rows(b("dt_bias")), "A_log": rows(b("A_log")), "D": rows(b("D_param")), "norm_w": by_chunk(b("norm_w")),
        "fc_b": by_chunk(b("fc_b")), "proj_b": rows(b("proj_b")),
    }
    return {
        "x": c(i["L0_attn_a_x"].reshape(T, P)),
        "masks": mask_tables(), "rope": rope_tables(), "moe_tables": moe_tables(),
        "w_mamba": c(np.concatenate([w_in[DI:2 * DI + 2 * DST], w_in[:DI], w_in[2 * DI + 2 * DST:]]).T),
        "w_out": c(b("out_proj_w").reshape(P, 2, P).transpose(2, 1, 0)),
        "w_fc": c(b("fc_w").T), "w_proj": c(b("proj_w").reshape(P, FC, P).transpose(2, 1, 0)),
        "vectors": c(np.concatenate([vectors[n] for n in vectors_layout()[0]], axis=1)),
        "w_att": c(np.stack([w.T for w in att], axis=1)),
        "wg": c(i["L0_ffn_wg"].T), "bg": c(rows(i["L0_ffn_bg"])),
        "w_gate": c(i["L0_ffn_Wgate"].transpose(2, 0, 1).reshape(P, NE * DH)),
        "w_up": c(i["L0_ffn_Wup"].transpose(2, 0, 1).reshape(P, NE * DH)),
        "w_down": c(i["L0_ffn_Wdown"].reshape(NE, P, HC, P).transpose(3, 0, 2, 1).reshape(P, NE * DH)),
    }


def kernel(**inputs):
    import concourse.bacc as bacc
    from concourse.bass_utils import run_bass_kernel_spmd

    nc = bacc.Bacc("TRN2", target_bir_lowering=False, num_devices=1)
    arrays = {f"in_{k}": v for k, v in layouts({k: np.asarray(v) for k, v in inputs.items()}).items()}
    a = {k[3:]: nc.dram_tensor(k, v.shape, F32, kind="ExternalInput").ap() for k, v in arrays.items()}
    out = nc.dram_tensor("out_0", (T, P), F32, kind="ExternalOutput").ap()
    program(nc, a, out)
    r = run_bass_kernel_spmd(nc, [arrays], core_ids=[0])
    return r.results[0]["out_0"].reshape(1, T, P)
```

```python
from contextlib import ExitStack

import numpy as np

import concourse.bass as bass
from concourse import mybir

F32 = mybir.dt.float32
BF16 = mybir.dt.bfloat16
U32 = mybir.dt.uint32
I32 = mybir.dt.int32
ALU = mybir.AluOpType
ACT = mybir.ActivationFunctionType
AX_X = mybir.AxisListType.X
DS = bass.DynSlice

P = 128
T = 2048
NT = T // P
QB = 512
NQB = T // QB
TPB = QB // P
EPS = 1e-5

NH, DK = 16, 8
HG = 4
NG = NH // HG
SCALE = float(1.0 / np.sqrt(np.float32(DK)))
NEG = -1e30
Q_PARTS = (0, 0, 1, 1, 0, 2, 1, 2)
K_PARTS = (0, 1, 0, 1, 2, 0, 2, 1)
MROW = 64
M_BANKS, S_BANKS = 3, 3
P_BUFS = 4
KROWS = 96


class Chain:

    def __init__(self, eng, sem):
        self.eng, self.sem, self.n = eng, sem, 0

    def __call__(self, ins):
        self.n += 1
        ins.then_inc(self.sem, 1)
        self.eng.wait_ge(self.sem, self.n)


def wait_apart(eng, sem, count, passed):
    eng.wait_ge(sem, count)
    eng.sem_inc(passed, 1)


def stage(nc, tag=""):
    ctx = ExitStack()
    sb = lambda name, shape, dt=F32: ctx.enter_context(nc.sbuf_tensor(tag + name, shape, dt))
    ps = lambda name, shape, dt=F32: ctx.enter_context(nc.psum_tensor(tag + name, shape, dt))
    sem = lambda name: nc.alloc_semaphore(tag + name)
    return ctx, sb, ps, sem


def norm_block(nc, tag, src, xn, xnt, ident, w=None, b=None):
    ctx, sb, ps, sem = stage(nc)
    with ctx:
        st = sb(f"{tag}_st", [P, NT, 6])
        half = sb(f"{tag}_half", [P, 4, NT])
        mean, var = half[:, 0], half[:, 1]
        rstd = sb(f"{tag}_rstd", [P, NT])
        std = sb(f"{tag}_std", [P, NT])
        tr = ps(f"{tag}_tr", [P, 2, QB])
        stats, step, var_ready = sem(f"{tag}_stats"), sem(f"{tag}_step"), sem(f"{tag}_var_ready")
        std_ready, xn_ready = sem(f"{tag}_std_ready"), sem(f"{tag}_xn_ready")
        turned, evacuated = sem(f"{tag}_turned"), sem(f"{tag}_evacuated")
        block = ctx.enter_context(nc.Block())

        @block.vector
        def _(dve):
            link = Chain(dve, step)
            for t in range(NT):
                dve.bn_stats(st[:, t, :], src[:, t, :]).then_inc(stats, 1)
            dve.wait_ge(stats, NT)
            link(dve.tensor_tensor(half[:, 2], st[:, :, 1], st[:, :, 4], ALU.subtract))
            link(dve.scalar_tensor_tensor(half[:, 2], half[:, 2], 0.25, half[:, 2], ALU.mult, ALU.mult))
            link(dve.tensor_tensor(half[:, 3], st[:, :, 2], st[:, :, 5], ALU.add))
            dve.scalar_tensor_tensor(var, half[:, 3], 1.0 / P, half[:, 2], ALU.mult, ALU.add).then_inc(var_ready, 1)
            link(dve.tensor_tensor(mean, st[:, :, 1], st[:, :, 4], ALU.add))
            link(dve.tensor_scalar(mean, mean, 0.5, None, ALU.mult))
            dve.wait_ge(std_ready, 1)
            link(dve.reciprocal(rstd[:], std[:]))
            for t in range(NT):
                dve.tensor_scalar(xn[:, t, :], src[:, t, :], half[:, 0, t:t + 1], rstd[:, t:t + 1],
                                  ALU.subtract, ALU.mult).then_inc(xn_ready, 1)

        @block.scalar
        def _(act):
            act.wait_ge(var_ready, 1)
            act.activation(std[:], var, ACT.Sqrt, bias=EPS).then_inc(std_ready, 1)
            for q in range(NQB if xnt is not None else 0):
                act.wait_ge(turned, q + 1)
                if w is None:
                    act.copy(xnt[:, q * QB:(q + 1) * QB], tr[:, q % 2, :]).then_inc(evacuated, 1)
                else:
                    act.activation(xnt[:, q * QB:(q + 1) * QB], tr[:, q % 2, :], ACT.Identity,
                                   bias=b, scale=w).then_inc(evacuated, 1)

        @block.tensor
        def _(pe):
            for q in range(NQB if xnt is not None else 0):
                if q >= 2:
                    pe.wait_ge(evacuated, q - 1)
                for i in range(TPB):
                    pe.wait_ge(xn_ready, q * TPB + i + 1)
                    last = pe.transpose(tr[:, q % 2, i * P:(i + 1) * P], xn[:, q * TPB + i, :], ident[:])
                last.then_inc(turned, 1)


def qkv_block(nc, xnt, weights, rope, vaug, qk_dram, stacks):
    wq, wqs, wk, wks, wv = weights
    ctx, sb, ps, sem = stage(nc)
    with ctx:
        cs = sb("rope_sb", [P, 2, 2, QB])
        t1, t2 = sb("rope_a", [P, 2, QB]), sb("rope_b", [P, 2, QB])
        rot, rest = sb("rot", [P, 3, QB]), sb("rest", [P, 3, QB])
        parts = sb("parts", [P, 4, 3, QB], BF16)
        proj = ps("proj", [P, 2, 2, QB])
        vps = ps("vps", [P, 2, QB])
        rope_in = [sem(f"rope_in{i}") for i in range(2)]
        prepared = sem("prepared")
        projected, rope_read, rope_sum = sem("projected"), sem("rope_read"), sem("rope_sum")
        hi_done, rest_done, mid_done, lo_done = sem("hi_done"), sem("rest_done"), sem("mid_done"), sem("lo_done")
        parts_sent = [sem(f"parts_sent{i}") for i in range(4)]
        v_done, v_copied = sem("v_done"), sem("v_copied")
        block = ctx.enter_context(nc.Block())
        NU = 2 * NQB

        @block.sync
        def _(sp):
            for n in range(NU):
                for b in ((0, 1) if n == 0 else (n // 2 + 2,) if n % 2 and n // 2 + 2 < NQB else ()):
                    if b >= 2:
                        sp.wait_ge(rope_read, 4 * (b - 1))
                    sp.dma_start(cs[:, b % 2], rope[:, :, b * QB:(b + 1) * QB]).then_inc(rope_in[b % 2], 16)
                sp.wait_ge(lo_done, n + 1)
                blk = slice(n // 2 * QB, (n // 2 + 1) * QB)
                sp.dma_start(qk_dram[n % 2, :, :, blk].rearrange("c p n -> p c n"), parts[:, n % 4]).then_inc(parts_sent[n % 4], 16)
            for i in range(4):
                sp.wait_ge(parts_sent[i], 16 * NU // 4)

        @block.gpsimd
        def _(pool):
            link = Chain(pool, prepared)
            link(pool.memset(vaug[:, :, :, DK:DK + 1], 1.0))
            qst, kst = stacks
            for i in range(2):
                link(pool.memset(qst[i][MROW:KROWS].bitcast(U32), 0))
                link(pool.memset(kst[i][MROW:KROWS].bitcast(U32), 0))
                link(pool.memset(kst[i][MROW:MROW + 3], 1.0))

        @block.tensor
        def _(pe):
            for n in range(NU):
                if n >= 2:
                    pe.wait_ge(rope_read, 2 * (n - 1))
                blk = slice(n // 2 * QB, (n // 2 + 1) * QB)
                for s, wt in enumerate(((wq, wqs), (wk, wks))[n % 2]):
                    last = pe.matmul(proj[:, n % 2, s, :], wt, xnt[:, blk], start=True, stop=True)
                last.then_inc(projected, 1)
                if n % 2:
                    b = n // 2
                    if b >= 2:
                        pe.wait_ge(v_copied, b - 1)
                    for i in range(TPB):
                        t = b * TPB + i
                        last = pe.matmul(vps[:, b % 2, i * P:(i + 1) * P], xnt[:, t * P:(t + 1) * P], wv,
                                         start=True, stop=True)
                    last.then_inc(v_done, 1)

        @block.vector
        def _(dve):
            for s in range(NU + 2):
                if s < NU:
                    tab = cs[:, s // 2 % 2]
                    dve.wait_ge(rope_in[s // 2 % 2], 16 * (s // 4 + 1))
                    dve.wait_ge(projected, s + 1)
                    dve.tensor_tensor(t1[:, s % 2], proj[:, s % 2, 0], tab[:, 0], ALU.mult).then_inc(rope_read, 1)
                    dve.tensor_tensor(t2[:, s % 2], proj[:, s % 2, 1], tab[:, 1], ALU.mult).then_inc(rope_read, 1)
                    dve.wait_ge(rope_read, 2 * s + 2)
                    dve.tensor_tensor(rot[:, s % 3], t1[:, s % 2], t2[:, s % 2], ALU.add).then_inc(rope_sum, 1)
                if 1 <= s <= NU:
                    n = s - 1
                    dve.wait_ge(hi_done, n + 1)
                    dve.tensor_tensor(rest[:, n % 3], rot[:, n % 3], parts[:, n % 4, 0], ALU.subtract).then_inc(rest_done, 1)
                if s >= 2:
                    n = s - 2
                    dve.wait_ge(mid_done, n + 1)
                    dve.tensor_tensor(parts[:, n % 4, 2], rest[:, n % 3], parts[:, n % 4, 1], ALU.subtract).then_inc(lo_done, 1)

        @block.scalar
        def _(act):
            for s in range(NU + 1):
                if s < NU:
                    act.wait_ge(rope_sum, s + 1)
                    if s >= 4:
                        act.wait_ge(parts_sent[s % 4], 16 * (s // 4))
                    act.copy(parts[:, s % 4, 0], rot[:, s % 3]).then_inc(hi_done, 1)
                if s >= 1:
                    n = s - 1
                    act.wait_ge(rest_done, n + 1)
                    act.copy(parts[:, n % 4, 1], rest[:, n % 3]).then_inc(mid_done, 1)
                if s % 2 and s < NU:
                    b = s // 2
                    act.wait_ge(v_done, b + 1)
                    act.copy(vaug[:, b * TPB:(b + 1) * TPB, :, 0:DK],
                             vps[:, b % 2].rearrange("p (i h d) -> p i h d", i=TPB, d=DK)).then_inc(v_copied, 1)


def attention_plan():
    blocks = [(g, j) for g in range(NG) for j in (range(NQB) if g < NG - 1 else reversed(range(NQB)))]
    steps = []
    for c, (g, j) in enumerate(blocks):
        d = TPB * j
        steps += [(c, [(kt, 0, 0)], HG) for kt in range(d)]
        steps += [(c, [(d, 0, 0)], HG), (c, [(d + 1, 0, P), (d + 3, 3 * P, 3 * P)], HG), (c, [(d + 2, 0, 2 * P)], HG // 2)]
    slots = [(s, k) for s, st in enumerate(steps) for k in range(st[2])]
    units = [(c, i, h, b) for c, (g, j) in enumerate(blocks) for i in range(TPB) for h in range(HG) for b in range(j + 1)]
    last_step = {st[0]: s for s, st in enumerate(steps)}
    SEM, NEVER = 0.1, 1e9
    now = dve = act = pool = 0.0
    reduced, exped, cut, valued = [], [], {}, []
    nt_at, rows_at, gathered, o_free = {}, {}, {}, 0.0
    stack_at = {0: 0.0, 1: 1.0}
    events = []
    m = s = v = rows = turned = 0
    slot_end = []
    for st in steps:
        slot_end.append((slot_end[-1] if slot_end else 0) + st[2])
    while turned < len(blocks):
        cand = []
        if rows in nt_at:
            cand.append((nt_at[rows], 0, "rows"))
        if turned in gathered:
            cand.append((gathered[turned], 1, "turn"))
        if m < len(units):
            g = blocks[units[m][0]][0]
            if g in stack_at:
                cand.append((max(stack_at[g], reduced[m - M_BANKS] + SEM if m >= M_BANKS else 0.0), 2, "max"))
        if s < len(slots):
            step = slots[s][0]
            if steps[step][0] in rows_at and (step < P_BUFS or v > step - P_BUFS):
                t = rows_at[steps[step][0]]
                if s >= S_BANKS:
                    t = max(t, exped[s - S_BANKS] + SEM)
                cand.append((t, 3, "scores"))
        if v < len(steps) and slot_end[v] <= len(exped):
            t = max(exped[slot_end[v] - 1] + SEM, cut.get(v, 0.0) + SEM)
            if v == 0 or steps[v - 1][0] != steps[v][0]:
                t = max(t, o_free + SEM)
            cand.append((t, 4, "values"))
        t, _, what = min((max(t, now), rank, what) for t, rank, what in cand)
        now = t
        if what == "max":
            c, i, h, b = units[m]
            w = QB if b < blocks[c][1] else (i + 1) * P
            now += 0.216 * w / QB
            dve = max(dve, now + SEM) + 0.065 + 0.535 * w / QB
            reduced.append(dve)
            events.append(("max", units[m], m))
            m += 1
            if m == len(units) or units[m][0] != c:
                events.append(("chain", c, m))
                dve += 0.15
                pool = max(pool, dve + SEM) + 1.8
                nt_at[c] = pool + SEM
        elif what == "rows":
            now += 0.22
            act = max(act, now + SEM) + 0.48
            rows_at[rows] = act + 3.0
            events.append(("rows", rows))
            rows += 1
        elif what == "scores":
            step, k = slots[s]
            now += 0.216
            act = max(act, now + SEM, valued[step - P_BUFS] + SEM if step >= P_BUFS else 0.0) + 0.48
            exped.append(act)
            events.append(("scores", step, k, s))
            s += 1
            if k == steps[step][2] - 1:
                if steps[step][1][0][0] >= TPB * blocks[steps[step][0]][1]:
                    pool = max(pool, act + SEM) + 0.65 * len(steps[step][1])
                    cut[step] = pool
                c = steps[step][0]
                if s == len(slots) or steps[slots[s][0]][0] != c:
                    g = blocks[c][0]
                    if all(blocks[x][0] != g for x in range(c + 1, len(blocks))):
                        stack_at[g + 2] = now + 12.0
        elif what == "values":
            now += 0.86
            valued.append(now)
            events.append(("values", v))
            c = steps[v][0]
            v += 1
            if last_step[c] == v - 1:
                act = max(act, now + SEM) + 0.48
                gathered[c] = act + SEM
                o_free = act
                events.append(("gather", c, v))
        else:
            now += 0.45
            dve = max(dve, now + SEM) + 0.4
            events.append(("turn", turned))
            turned += 1
    return blocks, steps, slot_end, events


def attention_block(nc, stacks, qk_dram, vaug, ao, ident, identb, maskq):
    blocks, steps, slot_end, events = attention_plan()
    qst, kst = stacks
    ctx, sb, ps, sem = stage(nc)
    with ctx:
        prob = sb("prob", [P, P_BUFS, HG, QB])
        pmax = sb("pmax", [P, 2, TPB * HG, NQB])
        small = sb("small", [P, 3, TPB * HG])
        nt = sb("nt", [P, TPB, 3, HG], BF16)
        ntt = sb("ntt", [3 * HG, QB], BF16)
        osb = sb("osb", [P, QB])
        rec = sb("rec", [P, TPB, HG])
        s_ps = ps("s_ps", [P, S_BANKS, QB])
        m_ps = ps("m_ps", [P, M_BANKS, QB])
        o_ps = ps("o_ps", [P, QB])
        t_ps = ps("t_ps", [P, QB])
        stack_in, cleared = [sem(f"stack_in{i}") for i in range(2)], sem("cleared")
        scores_ready, exp_done, cut_done, pv_done = sem("scores_ready"), sem("exp_done"), sem("cut_done"), sem("pv_done")
        max_ready, reduced, max_found = sem("max_ready"), sem("reduced"), sem("max_found")
        pool_step, nt_ready, nt_turned = sem("pool_step"), sem("nt_ready"), sem("nt_turned")
        ntt_ready, mrow_in, turn_free = sem("ntt_ready"), sem("mrow_in"), sem("turn_free")
        o_copied, o_turned, rec_done = sem("o_copied"), sem("o_turned"), sem("rec_done")
        block = ctx.enter_context(nc.Block())
        STACK_IN = 16 * (2 * len(Q_PARTS) + 1)
        cuts = {}
        for s, (c, tiles, _) in enumerate(steps):
            if tiles[0][0] >= TPB * blocks[c][1]:
                cuts[s] = len(cuts)
        uses = [e for e in events if e[0] in ("rows", "turn")]
        first_step = lambda s: s == 0 or steps[s - 1][0] != steps[s][0]

        def head_at(step, slot, h):
            return (h, 0) if steps[step][2] == HG else (h // 2, h % 2 * 2 * P)

        @block.tensor
        def _(pe):
            pe.wait_ge(cleared, 1)
            loaded = [0, 0]
            for e in events:
                if e[0] == "max":
                    _, (c, i, h, b), n = e
                    g, j = blocks[c]
                    if i == h == b == 0:
                        pe.wait_ge(stack_in[g % 2], STACK_IN * (g // 2 + 1))
                    if n >= M_BANKS:
                        pe.wait_ge(reduced, n - M_BANKS + 1)
                    w = QB if b < j else (i + 1) * P
                    tile = TPB * j + i
                    pe.matmul(m_ps[:, n % M_BANKS, 0:w], qst[g % 2][0:KROWS, h, tile * P:(tile + 1) * P],
                              kst[g % 2][0:KROWS, h, b * QB:b * QB + w], start=True, stop=True).then_inc(max_ready, 1)
                elif e[0] == "rows":
                    pe.wait_ge(nt_ready, e[1] + 1)
                    if uses.index(e):
                        pe.wait_ge(turn_free, uses.index(e))
                    for i in range(TPB):
                        last = pe.transpose(t_ps[:].bitcast(BF16)[0:3 * HG, i * P:(i + 1) * P],
                                            nt[:, i].rearrange("p c h -> p (c h)"), identb[:])
                    last.then_inc(nt_turned, 1)
                elif e[0] == "scores":
                    _, s, k, slot = e
                    c, tiles, n_slots = steps[s]
                    g, j = blocks[c]
                    if slot >= S_BANKS:
                        pe.wait_ge(exp_done, slot - S_BANKS + 1)
                    if k == 0 and first_step(s):
                        pe.wait_ge(mrow_in, 48 * (c + 1))
                    for h in range(HG):
                        if head_at(s, k, h)[0] != k:
                            continue
                        for kt, col, q0 in tiles:
                            at = head_at(s, k, h)[1] + col
                            last = pe.matmul(s_ps[:, slot % S_BANKS, at:at + QB - q0], kst[g % 2][0:KROWS, h, kt * P:(kt + 1) * P],
                                             qst[g % 2][0:KROWS, h, j * QB + q0:(j + 1) * QB], start=True, stop=True)
                    last.then_inc(scores_ready, 1)
                elif e[0] == "values":
                    s = e[1]
                    c, tiles, _ = steps[s]
                    g, j = blocks[c]
                    pe.wait_ge(exp_done, slot_end[s])
                    if s in cuts:
                        pe.wait_ge(cut_done, cuts[s] + 1)
                    if first_step(s) and c:
                        pe.wait_ge(o_copied, c)
                    for kt, col, q0 in tiles:
                        for h in range(HG):
                            k, at = head_at(s, None, h)
                            last = pe.matmul(o_ps[32 * h:32 * h + DK + 1, q0:QB], vaug[:, kt, g * HG + h, :],
                                             prob[:, s % P_BUFS, k, at + col:at + col + QB - q0],
                                             start=(kt == 0), stop=(kt == TPB * j + 2), skip_group_check=True, tile_position=(0, 32 * h))
                    last.then_inc(pv_done, 1)
                elif e[0] == "turn":
                    pe.wait_ge(o_copied, e[1] + 1)
                    pe.wait_ge(turn_free, uses.index(e))
                    for i in range(TPB):
                        last = pe.transpose(t_ps[:, i * P:(i + 1) * P], osb[:, i * P:(i + 1) * P], ident[:])
                    last.then_inc(o_turned, 1)

        @block.vector
        def _(dve):
            dve.memset(o_ps[:], 0.0).then_inc(cleared, 1)
            for e in events:
                if e[0] == "max":
                    _, (c, i, h, b), n = e
                    dve.wait_ge(max_ready, n + 1)
                    found = pmax[:, c % 2, i * HG + h, b:b + 1]
                    if b < blocks[c][1]:
                        dve.reduce_max(found, m_ps[:, n % M_BANKS], AX_X).then_inc(reduced, 1)
                    else:
                        w = (i + 1) * P
                        dve.tensor_tensor_reduce(m_ps[:, n % M_BANKS, 0:w], m_ps[:, n % M_BANKS, 0:w], maskq[:, QB - w:QB], 1.0, NEG,
                                                 ALU.add, ALU.max, found).then_inc(reduced, 1)
                elif e[0] == "chain":
                    _, c, n = e
                    dve.wait_ge(reduced, n)
                    if c:
                        dve.wait_ge(nt_ready, c)
                    dve.reduce_max(small[:, 0].rearrange("p (a o) -> p a o", o=1), pmax[:, c % 2, :, 0:blocks[c][1] + 1],
                                   AX_X).then_inc(max_found, 1)
                elif e[0] == "turn":
                    c = e[1]
                    g, j = blocks[c]
                    dve.wait_ge(o_turned, c + 1)
                    v = t_ps[:].rearrange("p (i h d) -> p i h d", i=TPB, h=HG)
                    dve.reciprocal(rec[:], v[:, :, :, DK]).then_inc(rec_done, 1)
                    dve.wait_ge(rec_done, c + 1)
                    dve.tensor_tensor(ao[:, j * TPB:(j + 1) * TPB, g * HG * DK:(g + 1) * HG * DK].rearrange("p i (h d) -> p i h d", h=HG),
                                      v[:, :, :, 0:DK], rec[:].rearrange("p i (h o) -> p i h o", o=1).broadcast_to([P, TPB, HG, DK]),
                                      ALU.mult).then_inc(turn_free, 1)

        @block.scalar
        def _(act):
            for e in events:
                if e[0] == "rows":
                    c = e[1]
                    act.wait_ge(nt_turned, c + 1)
                    if c:
                        act.wait_ge(mrow_in, 48 * c)
                    act.copy(ntt[:], t_ps[:].bitcast(BF16)[0:3 * HG, 0:QB]).then_inc(ntt_ready, 1)
                    act.wait_ge(ntt_ready, c + 1)
                    act.sem_inc(turn_free, 1)
                elif e[0] == "scores":
                    _, s, k, slot = e
                    act.wait_ge(scores_ready, slot + 1)
                    if k == 0 and s >= P_BUFS:
                        act.wait_ge(pv_done, s - P_BUFS + 1)
                    act.activation(prob[:, s % P_BUFS, k, :], s_ps[:, slot % S_BANKS], ACT.Exp, scale=SCALE).then_inc(exp_done, 1)
                elif e[0] == "gather":
                    _, c, done = e
                    act.wait_ge(pv_done, done)
                    if c:
                        act.wait_ge(o_turned, c)
                    act.copy(osb[:], o_ps[:]).then_inc(o_copied, 1)

        @block.gpsimd
        def _(pool):
            link = Chain(pool, pool_step)
            for e in events:
                if e[0] == "chain":
                    c = e[1]
                    pool.wait_ge(max_found, c + 1)
                    hi, mid, lo = (nt[:, :, k, :] for k in range(3))
                    neg = small[:, 1].rearrange("p (i h) -> p i h", h=HG)
                    rst = small[:, 2].rearrange("p (i h) -> p i h", h=HG)
                    if c:
                        pool.wait_ge(nt_turned, c)
                    link(pool.tensor_scalar(small[:, 1], small[:, 0], -1.0, None, ALU.mult))
                    link(pool.tensor_copy(hi, neg))
                    link(pool.tensor_tensor(rst, neg, hi, ALU.subtract))
                    link(pool.tensor_copy(mid, rst))
                    pool.tensor_tensor(lo, rst, mid, ALU.subtract).then_inc(nt_ready, 1)
                    pool.wait_ge(nt_ready, c + 1)
                elif e[0] == "scores":
                    _, s, k, slot = e
                    c, tiles, n_slots = steps[s]
                    if s not in cuts or k < n_slots - 1:
                        continue
                    pool.wait_ge(exp_done, slot + 1)
                    src = prob[:, s % P_BUFS]
                    if n_slots == HG:
                        where = [src[:, :, col:col + P] for _, col, _ in tiles]
                    else:
                        where = [src[:, 0:n_slots].rearrange("p s (k q) -> p (s k) q", k=2)[:, :, 0:P]]
                    for cut in where:
                        last = pool.affine_select(out=cut, in_=cut, compare_op=ALU.is_ge, fill=0.0, base=0,
                                                  pattern=[[0, HG], [1, P]], channel_multiplier=-1)
                    last.then_inc(cut_done, 1)

        @block.sync
        def _(sp):
            def load_stacks(g):
                q, k, done = qst[g % 2], kst[g % 2], stack_in[g % 2]
                sp.dma_start(q[MROW:MROW + 3], q[MROW + 3:MROW + 6]).then_inc(done, 16)
                for which, stack, order in ((0, q, Q_PARTS), (1, k, K_PARTS)):
                    for r, part in enumerate(order):
                        sp.dma_start(stack[r * DK:(r + 1) * DK],
                                     qk_dram[which, part, g * HG * DK:(g + 1) * HG * DK, :].rearrange("(h d) n -> d h n", d=DK)).then_inc(done, 16)

            load_stacks(0)
            load_stacks(1)
            for e in events:
                if e[0] == "rows":
                    c = e[1]
                    g, j = blocks[c]
                    sp.wait_ge(ntt_ready, c + 1)
                    for k in range(3):
                        sp.dma_start(qst[g % 2][MROW + k:MROW + k + 1, :, j * QB:(j + 1) * QB],
                                     ntt[HG * k:HG * (k + 1), :]).then_inc(mrow_in, 16)
                elif e[0] == "scores" and e[3] + 1 == slot_end[e[1]]:
                    g = blocks[steps[e[1]][0]][0]
                    ends = e[1] + 1 == len(steps) or blocks[steps[e[1] + 1][0]][0] != g
                    if ends and g + 2 < NG:
                        sp.wait_ge(scores_ready, e[3] + 1)
                        load_stacks(g + 2)
            sp.wait_ge(mrow_in, 48 * len(blocks))
            for i in range(2):
                sp.wait_ge(stack_in[i], STACK_IN * (NG // 2))


def project_add_block(nc, src, w, x, ident):
    ctx, sb, ps, sem = stage(nc)
    with ctx:
        turned_sb = sb("pa_t", [P, 2, QB])
        tr, out = ps("pa_tr", [P, 2, QB]), ps("pa_out", [P, 2, QB])
        turned, copied, projected, added = sem("pa_turned"), sem("pa_copied"), sem("pa_projected"), sem("pa_added")
        block = ctx.enter_context(nc.Block())

        @block.tensor
        def _(pe):
            for q in range(NQB + 1):
                if q < NQB:
                    if q >= 2:
                        pe.wait_ge(copied, q - 1)
                    for i in range(TPB):
                        last = pe.transpose(tr[:, q % 2, i * P:(i + 1) * P], src[:, q * TPB + i, :], ident[:])
                    last.then_inc(turned, 1)
                if q >= 1:
                    n = q - 1
                    pe.wait_ge(copied, n + 1)
                    if n >= 2:
                        pe.wait_ge(added, n - 1)
                    for i in range(TPB):
                        last = pe.matmul(out[:, n % 2, i * P:(i + 1) * P], turned_sb[:, n % 2, i * P:(i + 1) * P], w,
                                         start=True, stop=True)
                    last.then_inc(projected, 1)

        @block.scalar
        def _(act):
            for q in range(NQB):
                act.wait_ge(turned, q + 1)
                if q >= 2:
                    act.wait_ge(projected, q - 1)
                act.copy(turned_sb[:, q % 2], tr[:, q % 2]).then_inc(copied, 1)

        @block.vector
        def _(dve):
            for q in range(NQB):
                dve.wait_ge(projected, q + 1)
                xs = x[:, q * TPB:(q + 1) * TPB, :].rearrange("p t d -> p (t d)")
                dve.tensor_tensor(xs, xs, out[:, q % 2], ALU.add).then_inc(added, 1)


NE, DH = 8, 512
HC = DH // P
SLOT_TILES = (2 * T + NE * (P - 1)) // P
SLOT_TILES += SLOT_TILES % 2
X_BUFS, AHEAD = 4, 3
DUMP = 2 * T


def moe_tables():
    row = lambda v: np.broadcast_to(np.asarray(v, np.float32), (P, len(v)))
    tok = (np.arange(NT)[None, :] * P + np.arange(P)[:, None] + 1).astype(np.float32)
    return np.ascontiguousarray(np.concatenate([
        row(NE - np.arange(NE)), row(np.arange(P)), row(np.arange(SLOT_TILES)), tok, tok + np.float32(T),
        (DUMP + 1 + np.arange(SLOT_TILES)[None, :] * P + np.arange(P)[:, None]).astype(np.float32), row(np.arange(P))[:, :P] > np.arange(P)[:, None],
        np.ones((P, P), np.float32)], axis=1).astype(np.float32))


def moe_table_slices(t):
    out, at = [], 0
    for n in (NE, P, SLOT_TILES, 2 * NT, SLOT_TILES, P, P):
        out.append(t[:, at:at + n])
        at += n
    return out


def route_block(nc, tag, xn, xnt, wg, bg, tables, route, xn_dram):
    weights, src_idx, dst_idx, expert_of = route
    desc, iota_lo, iota_hi, token1, dump, before, ones = moe_table_slices(tables)
    ctx, sb, ps, sem = stage(nc, tag)
    with ctx:
        lg = sb("lg", [P, NT, NE])
        one = sb("one", [P, 2, NT, NE])
        tmp, key = sb("rt_tmp", [P, NT, NE]), sb("rt_key", [P, NT, NE])
        both = sb("both", [P, NT, NE])
        top, kmax = sb("top", [P, 2, NT]), sb("kmax", [P, 2, NT])
        ex, den = sb("rt_ex", [P, 2, NT]), sb("rt_den", [P, NT])
        cum = sb("cum", [P, 2, NT, NE])
        cnt = sb("cnt", [P, NE], I32)
        tiles_e, tcum, base = sb("tiles_e", [P, NE]), sb("tcum", [P, 2, NE]), sb("base", [P, NE])
        slot = sb("slot", [P, 2, NT])
        sloti, part = sb("sloti", [P, 2, NT], I32), sb("part", [P, 2, 2, NT], I32)
        hilo = sb("hilo", [P, 2, 2, NT])
        onelo, onehi = sb("onelo", [P, 4, P]), sb("onehi", [P, 4, SLOT_TILES])
        inv, t2 = sb("inv", [P, SLOT_TILES]), sb("inv2", [P, 3, SLOT_TILES])
        ge = sb("ge", [P, SLOT_TILES, NE])
        eo = sb("eo", [P, SLOT_TILES])
        lg_ps, rank_ps, tot_ps = ps("lg_ps", [P, NT, NE]), ps("rank_ps", [P, NT, NE]), ps("tot_ps", [P, NT, NE])
        inv_ps = ps("inv_ps", [P, SLOT_TILES])
        xn_out, step, logits_ready = sem("xn_out"), sem("rt_step"), sem("logits_ready")
        gap_ready, exp_ready, mask_ready, ranked = sem("gap_ready"), sem("exp_ready"), sem("mask_ready"), sem("ranked")
        hot_ready, hot_used, inv_done = sem("hot_ready"), sem("hot_used"), sem("inv_done")
        block = ctx.enter_context(nc.Block())
        bc = lambda v: v.rearrange("p (t o) -> p t o", o=1).broadcast_to([P, NT, NE])
        NHOT = 2 * NT

        @block.sync
        def _(sp):
            sp.dma_start(xn_dram.rearrange("(t p) d -> p t d", p=P), xn[:]).then_inc(xn_out, 16)
            sp.wait_ge(xn_out, 16)

        @block.tensor
        def _(pe):
            for t in range(NT):
                last = pe.matmul(lg_ps[:, t], xnt[:, t * P:(t + 1) * P], wg, start=True, stop=True)
            last.then_inc(logits_ready, 1)
            pe.wait_ge(mask_ready, 1)
            flat = both[:].rearrange("p t e -> p (t e)")
            pe.matmul(rank_ps[:].rearrange("p t e -> p (t e)"), before, flat, start=True, stop=True)
            pe.matmul(tot_ps[:].rearrange("p t e -> p (t e)"), ones, flat, start=True, stop=True).then_inc(ranked, 1)
            for n in range(NHOT):
                pe.wait_ge(hot_ready, n + 1)
                pe.matmul(inv_ps[:], onelo[:, n % 4], onehi[:, n % 4], start=(n == 0), stop=(n == NHOT - 1)).then_inc(hot_used, 1)

        @block.scalar
        def _(act):
            act.wait_ge(gap_ready, 1)
            act.activation(ex[:, 1], ex[:, 0], ACT.Exp).then_inc(exp_ready, 1)

        @block.vector
        def _(dve):
            link = Chain(dve, step)
            dve.wait_ge(logits_ready, 1)
            link(dve.tensor_tensor(lg[:], lg_ps[:], bg.rearrange("p (o e) -> p o e", o=1).broadcast_to([P, NT, NE]), ALU.add))
            for k in range(2):
                link(dve.reduce_max(top[:, k].rearrange("p (t o) -> p t o", o=1), lg[:], AX_X))
                link(dve.tensor_tensor(tmp[:], lg[:], bc(top[:, k]), ALU.is_equal))
                link(dve.tensor_tensor(key[:], tmp[:], desc.rearrange("p (o e) -> p o e", o=1).broadcast_to([P, NT, NE]), ALU.mult))
                link(dve.reduce_max(kmax[:, k].rearrange("p (t o) -> p t o", o=1), key[:], AX_X))
                link(dve.tensor_tensor(one[:, k], key[:], bc(kmax[:, k]), ALU.is_equal))
                if k == 0:
                    link(dve.tensor_scalar(tmp[:], one[:, 0], 0.0, None, ALU.is_equal))
                    link(dve.tensor_tensor(lg[:], lg[:], tmp[:], ALU.mult))
                    link(dve.scalar_tensor_tensor(lg[:], one[:, 0], -3e38, lg[:], ALU.mult, ALU.add))
            dve.tensor_tensor(both[:], one[:, 0], one[:, 1], ALU.add).then_inc(mask_ready, 1)
            dve.tensor_tensor(ex[:, 0], top[:, 1], top[:, 0], ALU.subtract).then_inc(gap_ready, 1)
            dve.wait_ge(exp_ready, 1)
            link(dve.tensor_scalar(den[:], ex[:, 1], 1.0, None, ALU.add))
            link(dve.reciprocal(weights[:, 0], den[:]))
            link(dve.tensor_tensor(weights[:, 1], weights[:, 0], ex[:, 1], ALU.mult))
            dve.wait_ge(ranked, 1)
            link(dve.tensor_copy(cum[:, 0], tot_ps[:]))
            a = 0
            for d in (1, 2, 4, 8):
                link(dve.tensor_copy(cum[:, 1 - a, 0:d], cum[:, a, 0:d]))
                link(dve.tensor_tensor(cum[:, 1 - a, d:NT], cum[:, a, d:NT], cum[:, a, 0:NT - d], ALU.add))
                a = 1 - a
            link(dve.tensor_scalar(cnt[:], cum[:, a, NT - 1], float(P - 1), None, ALU.add))
            link(dve.tensor_scalar(cnt[:], cnt[:], 7, None, ALU.arith_shift_right))
            link(dve.tensor_copy(tiles_e[:], cnt[:]))
            link(dve.tensor_copy(tcum[:, 0], tiles_e[:]))
            c = 0
            for d in (1, 2, 4):
                link(dve.tensor_copy(tcum[:, 1 - c, 0:d], tcum[:, c, 0:d]))
                link(dve.tensor_tensor(tcum[:, 1 - c, d:NE], tcum[:, c, d:NE], tcum[:, c, 0:NE - d], ALU.add))
                c = 1 - c
            link(dve.tensor_tensor(base[:], tcum[:, c], tiles_e[:], ALU.subtract))
            link(dve.tensor_tensor(ge[:], iota_hi.rearrange("p (s o) -> p s o", o=1).broadcast_to([P, SLOT_TILES, NE]),
                                   tcum[:, c].rearrange("p (o e) -> p o e", o=1).broadcast_to([P, SLOT_TILES, NE]), ALU.is_ge))
            link(dve.reduce_sum(eo[:].rearrange("p (s o) -> p s o", o=1), ge[:], AX_X))
            link(dve.tensor_scalar(expert_of[:], eo[:], float(NE - 1), float(DH), ALU.min, ALU.mult))
            link(dve.tensor_tensor(tmp[:], cum[:, a], tot_ps[:], ALU.subtract))
            link(dve.tensor_tensor(tmp[:], tmp[:], rank_ps[:], ALU.add))
            link(dve.scalar_tensor_tensor(tmp[:], base[:].rearrange("p (o e) -> p o e", o=1).broadcast_to([P, NT, NE]), float(P),
                                          tmp[:], ALU.mult, ALU.add))
            for k in range(2):
                link(dve.tensor_tensor(key[:], one[:, k], tmp[:], ALU.mult))
                link(dve.reduce_sum(slot[:, k].rearrange("p (t o) -> p t o", o=1), key[:], AX_X))
            link(dve.tensor_copy(sloti[:], slot[:]))
            link(dve.tensor_scalar(part[:, 0], sloti[:], 7, None, ALU.arith_shift_right))
            link(dve.tensor_scalar(part[:, 1], sloti[:], P - 1, None, ALU.bitwise_and))
            link(dve.tensor_copy(hilo[:], part[:]))
            for n in range(NHOT):
                k, t = n // NT, n % NT
                if n >= 4:
                    dve.wait_ge(hot_used, n - 3)
                dve.tensor_scalar(onelo[:, n % 4], iota_lo, hilo[:, 1, k, t:t + 1], None, ALU.is_equal).then_inc(inv_done, 1)
                dve.wait_ge(inv_done, n + 1)
                dve.tensor_scalar(onehi[:, n % 4], iota_hi, hilo[:, 0, k, t:t + 1], token1[:, n:n + 1],
                                  ALU.is_equal, ALU.mult).then_inc(hot_ready, 1)
            dve.wait_ge(hot_used, NHOT)
            link(dve.tensor_copy(inv[:], inv_ps[:]))
            link(dve.tensor_scalar(t2[:, 0], inv[:], 0.0, None, ALU.is_equal))
            link(dve.tensor_scalar(t2[:, 1], inv[:], float(T), float(-T), ALU.is_gt, ALU.mult))
            link(dve.tensor_tensor(t2[:, 1], t2[:, 1], t2[:, 0], ALU.add))
            link(dve.tensor_tensor(t2[:, 1], t2[:, 1], inv[:], ALU.add))
            link(dve.tensor_scalar(src_idx[:], t2[:, 1], -1.0, None, ALU.add))
            link(dve.tensor_tensor(t2[:, 2], t2[:, 0], dump, ALU.mult))
            link(dve.tensor_tensor(t2[:, 2], t2[:, 2], inv[:], ALU.add))
            link(dve.tensor_scalar(dst_idx[:], t2[:, 2], -1.0, None, ALU.add))


def experts_block(nc, tag, w_gate, w_up, w_down, route, x, ident, xn_dram, y_dram):
    weights, src_idx, dst_idx, expert_of = route
    ctx, sb, ps, sem = stage(nc, tag)
    with ctx:
        si, di = sb("si", [P, X_BUFS], U32), sb("di", [P, 2], U32)
        xg, xt = sb("xg", [P, X_BUFS, P]), sb("xt", [P, 2, P])
        sg, h, ht = sb("sg", [P, 2, DH]), sb("h", [P, 2, DH]), sb("ht", [P, 2, DH])
        yo = sb("yo", [P, 2, P])
        yb = sb("yb", [P, 2, NT, P])
        g_ps, u_ps, h_ps = ps("g_ps", [P, 2, DH]), ps("u_ps", [P, 2, DH]), ps("h_ps", [P, 2, DH])
        x_ps, y_ps = ps("x_ps", [P, P]), ps("y_ps", [P, P])
        gathered, scattered = [sem(f"gathered{i}") for i in range(X_BUFS)], [sem(f"scattered{i}") for i in range(2)]
        si_ready, di_ready = sem("si_ready"), sem("di_ready")
        x_turned, x_copied, gate_done, up_done = sem("x_turned"), sem("x_copied"), sem("gate_done"), sem("up_done")
        silu_done, h_done, h_turned, h_copied = sem("silu_done"), sem("h_done"), sem("h_turned"), sem("h_copied")
        down_done, y_copied, added = sem("down_done"), sem("y_copied"), sem("added")
        y_loaded = [[sem(f"y_loaded{k}{q}") for q in range(NQB)] for k in range(2)]
        block = ctx.enter_context(nc.Block())
        S = SLOT_TILES

        @block.gpsimd
        def _(pool):
            def gather(t):
                b = t % X_BUFS
                pool.tensor_copy(si[:, b:b + 1], src_idx[:, t:t + 1]).then_inc(si_ready, 1)
                pool.wait_ge(si_ready, t + 1)
                pool.indirect_dma_start(xg[:, b], None, xn_dram, bass.IndirectOffsetOnAxis(si[:, b:b + 1], 0)).then_inc(gathered[b], 16)

            def scatter(t):
                b = t % 2
                if t >= 2:
                    pool.wait_ge(scattered[b], t // 2 * 16)
                pool.tensor_copy(di[:, b:b + 1], dst_idx[:, t:t + 1]).then_inc(di_ready, 1)
                pool.wait_ge(di_ready, t + 1)
                pool.wait_ge(y_copied, t + 1)
                pool.indirect_dma_start(y_dram, bass.IndirectOffsetOnAxis(di[:, b:b + 1], 0), yo[:, b], None).then_inc(scattered[b], 16)

            for t in range(AHEAD):
                gather(t)
            for t in range(S + 1):
                if t + AHEAD < S:
                    if t:
                        pool.wait_ge(x_turned, t)
                    gather(t + AHEAD)
                if t >= 1:
                    scatter(t - 1)

        def load_y(eng, k):
            for b in range(2):
                eng.wait_ge(scattered[b], 8 * S)
            for q in range(NQB):
                rows = y_dram[k * T + q * QB:k * T + (q + 1) * QB, :]
                eng.dma_start(yb[:, k, q * TPB:(q + 1) * TPB], rows.rearrange("(t p) d -> p t d", p=P)).then_inc(y_loaded[k][q], 16)

        @block.sync
        def _(sp):
            load_y(sp, 0)

        @block.tensor
        def _(pe):
            def turn_x(t):
                pe.wait_ge(gathered[t % X_BUFS], 16 * (t // X_BUFS + 1))
                if t >= 1:
                    pe.wait_ge(x_copied, t)
                pe.transpose(x_ps[:], xg[:, t % X_BUFS], ident).then_inc(x_turned, 1)

            def turn_h(t):
                pe.wait_ge(h_done, t + 1)
                for c in range(HC):
                    last = pe.transpose(h_ps[:, t % 2, c * P:(c + 1) * P], h[:, t % 2, c * P:(c + 1) * P], ident)
                last.then_inc(h_turned, 1)

            def down(t, col):
                if t >= 1:
                    pe.wait_ge(y_copied, t)
                pe.wait_ge(h_copied, t + 1)
                for c in range(HC):
                    last = pe.matmul(y_ps[:], ht[:, t % 2, c * P:(c + 1) * P], w_down[:, DS(col + c * P, P)],
                                     start=(c == 0), stop=(c == HC - 1))
                last.then_inc(down_done, 1)

            def column(t):
                return pe.value_load(expert_of[0:1, t:t + 1], min_val=0, max_val=(NE - 1) * DH)

            turn_x(0)
            before, col = None, column(0)
            for t in range(S):
                if t + 1 < S:
                    turn_x(t + 1)
                if t >= 1:
                    turn_h(t - 1)
                pe.wait_ge(x_copied, t + 1)
                if t >= 2:
                    pe.wait_ge(h_done, t - 1)
                pe.matmul(g_ps[:, t % 2], xt[:, t % 2], w_gate[:, DS(col, DH)], start=True, stop=True).then_inc(gate_done, 1)
                after = column(t + 1) if t + 1 < S else None
                pe.matmul(u_ps[:, t % 2], xt[:, t % 2], w_up[:, DS(col, DH)], start=True, stop=True).then_inc(up_done, 1)
                if t >= 1:
                    down(t - 1, before)
                before, col = col, after
            turn_h(S - 1)
            down(S - 1, before)

        @block.scalar
        def _(act):
            for t in range(S):
                act.wait_ge(gate_done, t + 1)
                if t >= 2:
                    act.wait_ge(h_done, t - 1)
                act.activation(sg[:, t % 2], g_ps[:, t % 2], ACT.Silu).then_inc(silu_done, 1)
            load_y(act, 1)

        @block.vector
        def _(dve):
            def copy_x(t):
                dve.wait_ge(x_turned, t + 1)
                if t >= 2:
                    dve.wait_ge(up_done, t - 1)
                dve.tensor_copy(xt[:, t % 2], x_ps[:]).then_inc(x_copied, 1)

            copy_x(0)
            for t in range(S + 1):
                n = t - 1
                if t + 1 < S:
                    copy_x(t + 1)
                if t >= 1:
                    dve.wait_ge(h_turned, n + 1)
                    if n >= 2:
                        dve.wait_ge(down_done, n - 1)
                    dve.tensor_copy(ht[:, n % 2], h_ps[:, n % 2]).then_inc(h_copied, 1)
                if t < S:
                    dve.wait_ge(up_done, t + 1)
                    dve.wait_ge(silu_done, t + 1)
                    if t >= 2:
                        dve.wait_ge(h_turned, t - 1)
                    dve.tensor_tensor(h[:, t % 2], sg[:, t % 2], u_ps[:, t % 2], ALU.mult).then_inc(h_done, 1)
                if t >= 1:
                    dve.wait_ge(down_done, n + 1)
                    if n >= 2:
                        dve.wait_ge(scattered[n % 2], n // 2 * 16)
                    dve.tensor_copy(yo[:, n % 2], y_ps[:]).then_inc(y_copied, 1)
            for q in range(NQB):
                for k in range(2):
                    dve.wait_ge(y_loaded[k][q], 16)
                    for i in range(TPB):
                        t = q * TPB + i
                        if k:
                            dve.wait_ge(added, q * 2 * TPB + i + 1)
                        dve.scalar_tensor_tensor(x[:, t], yb[:, k, t], weights[:, k, t:t + 1], x[:, t], ALU.mult, ALU.add).then_inc(added, 1)


DI, DST, HD = 256, 64, 64
MH = DI // HD
DCONV = 4
CCH = (DI + 2 * DST) // P
FC = 512 // P
PAD = DCONV - 1
SERIES = 9


def mamba_in_block(nc, xnt, w_conv_in, w_z, w_dt, small, conv, sz, dt_raw):
    cw, cb = small["conv_w"], small["conv_b"]
    ctx, sb, ps, sem = stage(nc)
    with ctx:
        raw = sb("raw", [P, CCH, PAD + T])
        acc = sb("acc", [P, 2, QB])
        c_ps = ps("c_ps", [P, CCH, QB])
        z_ps = ps("z_ps", [P, 2, 2, DI])
        d_ps = ps("d_ps", [P, NT, MH])
        padded, projected, raw_ready = sem("padded"), sem("mi_projected"), sem("raw_ready")
        z_done, z_read, d_done, d_read = sem("z_done"), sem("z_read"), sem("d_done"), sem("d_read")
        tap, conv_done, silu_done = sem("tap"), sem("conv_done"), sem("mi_silu")
        block = ctx.enter_context(nc.Block())

        @block.tensor
        def _(pe):
            for t in range(NT):
                last = pe.matmul(d_ps[:, t], xnt[:, t * P:(t + 1) * P], w_dt, start=True, stop=True)
            last.then_inc(d_done, 1)
            for b in range(NQB):
                for c in range(CCH):
                    if b:
                        pe.wait_ge(raw_ready, (b - 1) * CCH + c + 1)
                    pe.matmul(c_ps[:, c], w_conv_in[:, c * P:(c + 1) * P], xnt[:, b * QB:(b + 1) * QB],
                              start=True, stop=True).then_inc(projected, 1)
                for half in range(2):
                    n = 2 * b + half
                    if n >= 2:
                        pe.wait_ge(z_read, n - 1)
                    for i in range(2):
                        t = 2 * n + i
                        last = pe.matmul(z_ps[:, n % 2, i], xnt[:, t * P:(t + 1) * P], w_z, start=True, stop=True)
                    last.then_inc(z_done, 1)

        @block.scalar
        def _(act):
            for b in range(NQB):
                for c in range(CCH):
                    n = b * CCH + c
                    act.wait_ge(projected, n + 1)
                    act.copy(raw[:, c, PAD + b * QB:PAD + (b + 1) * QB], c_ps[:, c]).then_inc(raw_ready, 1)
                for half in range(2):
                    n = 2 * b + half
                    act.wait_ge(z_done, n + 1)
                    act.activation(sz[:, 2 * n:2 * n + 2], z_ps[:, n % 2], ACT.Silu).then_inc(z_read, 1)
                for c in range(CCH):
                    n = b * CCH + c
                    act.wait_ge(conv_done, n + 1)
                    blk = conv[:, c, b * QB:(b + 1) * QB]
                    act.activation(blk, acc[:, n % 2], ACT.Silu).then_inc(silu_done, 1)

        @block.vector
        def _(dve):
            dve.memset(raw[:, :, 0:PAD], 0.0).then_inc(padded, 1)
            dve.wait_ge(padded, 1)
            dve.wait_ge(d_done, 1)
            dve.tensor_copy(dt_raw[:], d_ps[:]).then_inc(d_read, 1)
            for b in range(NQB):
                for c in range(CCH):
                    n = b * CCH + c
                    dve.wait_ge(raw_ready, n + 1)
                    if n >= 2:
                        dve.wait_ge(silu_done, n - 1)
                    at = lambda k: raw[:, c, b * QB + k:b * QB + k + QB]
                    dve.tensor_scalar(acc[:, n % 2], at(0), cw[:, c, 0:1], cb[:, c:c + 1], ALU.mult, ALU.add).then_inc(tap, 1)
                    for k in range(1, DCONV):
                        dve.wait_ge(tap, n * (DCONV - 1) + k)
                        dve.scalar_tensor_tensor(acc[:, n % 2], at(k), cw[:, c, k:k + 1], acc[:, n % 2], ALU.mult, ALU.add).then_inc(
                            tap if k < DCONV - 1 else conv_done, 1)


def mamba_rates_block(nc, dt_raw, small, dt, a, ecum, dec, etot, w_out, norm_w, u_incl, below, ones):
    ctx, sb, ps, sem = stage(nc)
    with ctx:
        v = sb("sp_v", [P, 6, NT, MH])
        ea = sb("ea", [P, MH])
        sums = ps("sums", [P, 3, QB])
        step, asked, given, a_ready, summed, exped = (sem(f"mr_{n}") for n in ("step", "asked", "given", "a_ready", "summed", "exped"))
        block = ctx.enter_context(nc.Block())
        bias = small["dt_bias"].rearrange("p (o h) -> p o h", o=1).broadcast_to([P, NT, MH])

        @block.vector
        def _(dve):
            link = Chain(dve, step)
            for c in range(2):
                link(dve.tensor_scalar(w_out[:, c], w_out[:, c], norm_w[:, c:c + 1], None, ALU.mult))
            link(dve.tensor_tensor(v[:, 0], dt_raw[:], bias, ALU.add))
            link(dve.tensor_scalar(v[:, 1], v[:, 0], -1.0, None, ALU.mult))
            link(dve.tensor_tensor(v[:, 2], v[:, 0], v[:, 1], ALU.min))
            dve.sem_inc(asked, 1)
            dve.wait_ge(given, 2)
            link(dve.tensor_scalar(v[:, 4], v[:, 3], 2.0, None, ALU.add))
            link(dve.reciprocal(v[:, 4], v[:, 4]))
            link(dve.tensor_tensor(v[:, 3], v[:, 3], v[:, 4], ALU.mult))
            link(dve.tensor_tensor(v[:, 4], v[:, 3], v[:, 3], ALU.mult))
            link(dve.tensor_scalar(v[:, 5], v[:, 4], 1.0 / (2 * SERIES - 1), 1.0 / (2 * SERIES - 3), ALU.mult, ALU.add))
            for k in range(SERIES - 2, 0, -1):
                link(dve.tensor_tensor(v[:, 5], v[:, 5], v[:, 4], ALU.mult))
                link(dve.tensor_scalar(v[:, 5], v[:, 5], 1.0 / (2 * k - 1), None, ALU.add))
            link(dve.tensor_tensor(v[:, 5], v[:, 5], v[:, 3], ALU.mult))
            link(dve.tensor_scalar(v[:, 0], v[:, 0], 0.0, None, ALU.max))
            link(dve.scalar_tensor_tensor(dt[:], v[:, 5], 2.0, v[:, 0], ALU.mult, ALU.add))
            dve.scalar_tensor_tensor(a[:], dt[:], -1.0, ea[:].rearrange("p (o h) -> p o h", o=1).broadcast_to([P, NT, MH]),
                                     ALU.mult, ALU.mult).then_inc(a_ready, 1)

        @block.scalar
        def _(act):
            act.activation(ea[:], small["A_log"], ACT.Exp).then_inc(given, 1)
            act.wait_ge(asked, 1)
            act.activation(v[:, 3], v[:, 2], ACT.Exp).then_inc(given, 1)
            act.wait_ge(summed, 1)
            for i, out in enumerate((ecum, dec, etot)):
                act.activation(out[:].rearrange("p t h -> p (t h)"), sums[:, i, 0:NT * MH], ACT.Exp).then_inc(exped, 1)

        @block.tensor
        def _(pe):
            pe.wait_ge(a_ready, 1)
            for i, lhs in enumerate((u_incl, below, ones)):
                last = pe.matmul(sums[:, i, 0:NT * MH], lhs, a[:].rearrange("p t h -> p (t h)"), start=True, stop=True)
            last.then_inc(summed, 1)


def ssd_block(nc, conv, sz, dt, a, ecum, dec, etot, d_param, y, ssq, ident, u_incl, below):
    ctx, sb, ps, sem = stage(nc)
    with ctx:
        cin = sb("cin", [P, 2, CCH, P])
        tok = sb("tok", [P, 2, CCH, P])
        ct = sb("ct", [DST, 2, P])
        r = sb("seg_in", [P, 2, MH, P])
        e = sb("seg_exp", [P, 2, MH, P])
        gm = sb("gm", [P, 2, P])
        mt = sb("mt", [P, 2, MH, P])
        dtx, dtxd, dx = sb("dtx", [P, 2, MH, HD]), sb("dtxd", [P, 2, MH, HD]), sb("dx", [P, 2, MH, HD])
        state = sb("state", [DST, 2, MH, HD])
        yt = sb("yt", [P, 2, MH, HD])
        sq = sb("sq", [P, 2, DI])
        bank = lambda name: ps(name, [P, QB])
        t_ps, c_ps, g_ps, s_ps, i_ps, y_ps, u_ps = (bank(f"ssd_{n}") for n in "tcgsiyu")
        names = ("staged r_ready dtx_ready dtxd_ready dx_ready t_done t_copied c_done c_copied g_done s_done e_done "
                 "pe_passed gm_done mt_done i_done y_done u_done sdec_done state_ready yt1 yt2 yt3 y_ready sq_done")
        s = {n: sem("ssd_" + n) for n in names.split()}
        block = ctx.enter_context(nc.Block())
        N = NT

        def turns(eng, step):
            for t in range(2):
                step(t, t % 2, t)
            with eng.Fori(0, (N - 4) // 2) as turn:
                for k in range(2):
                    step(turn * 2 + (2 + k), k, None)
            for t in range(N - 2, N):
                step(t, t % 2, t)

        some = lambda at, n: at is None or at >= n
        head = lambda v, t: v[:, DS(t, 1), :].rearrange("p o h -> p (o h)").rearrange("p (h o) -> p h o", o=1)

        @block.gpsimd
        def _(pool):
            def step(t, b, at):
                if some(at, 2):
                    pool.wait_ge(s["g_done"], t - 1)
                    pool.wait_ge(s["s_done"], t - 1)
                pool.tensor_copy(cin[:, b], conv[:, :, DS(t * P, P)]).then_inc(s["staged"], 1)
                pool.wait_ge(s["staged"], t + 1)
                pool.tensor_tensor(r[:, b], u_incl.rearrange("p (o i) -> p o i", o=1).broadcast_to([P, MH, P]),
                                   head(a, t).broadcast_to([P, MH, P]), ALU.mult).then_inc(s["r_ready"], 1)
                pool.wait_ge(s["r_ready"], t + 1)
                pool.wait_ge(s["t_copied"], t + 1)
                if some(at, 2):
                    pool.wait_ge(s["y_done"], t - 1)
                    pool.wait_ge(s["u_done"], t - 1)
                    pool.wait_ge(s["yt2"], t - 1)
                xs = tok[:, b, 0:2].rearrange("p c (h d) -> p (c h) d", d=HD)
                pool.tensor_tensor(dtx[:, b], xs, head(dt, t).broadcast_to([P, MH, HD]), ALU.mult).then_inc(s["dtx_ready"], 1)
                pool.wait_ge(s["dtx_ready"], t + 1)
                pool.tensor_tensor(dtxd[:, b], dtx[:, b], head(dec, t).broadcast_to([P, MH, HD]), ALU.mult).then_inc(s["dtxd_ready"], 1)
                pool.wait_ge(s["dtxd_ready"], t + 1)
                pool.tensor_tensor(dx[:, b], xs, d_param.rearrange("p (h o) -> p h o", o=1).broadcast_to([P, MH, HD]),
                                   ALU.mult).then_inc(s["dx_ready"], 1)
                pool.wait_ge(s["dx_ready"], t + 1)

            turns(pool, step)

        @block.tensor
        def _(pe):
            def front(t, b, at):
                pe.wait_ge(s["staged"], t + 1)
                if some(at, 1):
                    pe.wait_ge(s["t_copied"], t)
                for c in range(CCH):
                    last = pe.transpose(t_ps[:, c * P:(c + 1) * P], cin[:, b, c], ident)
                last.then_inc(s["t_done"], 1)
                pe.wait_ge(s["r_ready"], t + 1)
                if some(at, 1):
                    pe.wait_ge(s["e_done"], t)
                pe.matmul(s_ps[:], below, r[:, b].rearrange("p h i -> p (h i)"), start=True, stop=True).then_inc(s["s_done"], 1)
                wait_apart(pe, s["t_copied"], t + 1, s["pe_passed"])
                pe.transpose(c_ps[0:DST, 0:P], tok[:, b, 2, DST:P], ident).then_inc(s["c_done"], 1)
                pe.wait_ge(s["c_copied"], t + 1)
                if some(at, 1):
                    pe.wait_ge(s["gm_done"], t)
                pe.matmul(g_ps[:, 0:P], cin[0:DST, b, 2], ct[:, b], start=True, stop=True).then_inc(s["g_done"], 1)

            def step(t, b, at):
                if at is None or at < N - 1:
                    front(t + 1, 1 - b, None if at is None else at + 1)
                pe.wait_ge(s["dtxd_ready"], t + 1)
                if some(at, 1):
                    pe.wait_ge(s["state_ready"], t + 1)
                pe.matmul(u_ps[0:DST, 0:DI], tok[:, b, 2, 0:DST], dtxd[:, b].rearrange("p h d -> p (h d)"),
                          start=True, stop=True).then_inc(s["u_done"], 1)
                pe.wait_ge(s["state_ready"], t + 1)
                if some(at, 1):
                    pe.wait_ge(s["yt1"], t)
                pe.matmul(i_ps[:, 0:DI], ct[:, b], state[:, b].rearrange("p h d -> p (h d)"), start=True, stop=True).then_inc(s["i_done"], 1)
                pe.wait_ge(s["mt_done"], t + 1)
                if some(at, 1):
                    pe.wait_ge(s["yt2"], t)
                for h in range(MH):
                    last = pe.matmul(y_ps[:, h * HD:(h + 1) * HD], mt[:, b, h], dtx[:, b, h], start=True, stop=True)
                last.then_inc(s["y_done"], 1)

            front(0, 0, 0)
            turns(pe, step)

        @block.scalar
        def _(act):
            def front(t, b, at):
                act.wait_ge(s["t_done"], t + 1)
                if some(at, 2):
                    act.wait_ge(s["u_done"], t - 1)
                    act.wait_ge(s["dx_ready"], t - 1)
                act.copy(tok[:, b].rearrange("p c i -> p (c i)"), t_ps[:, 0:CCH * P]).then_inc(s["t_copied"], 1)
                act.wait_ge(s["s_done"], t + 1)
                if some(at, 2):
                    act.wait_ge(s["mt_done"], t - 1)
                act.activation(e[:, b].rearrange("p h i -> p (h i)"), s_ps[:], ACT.Exp).then_inc(s["e_done"], 1)
                act.wait_ge(s["c_done"], t + 1)
                if some(at, 2):
                    act.wait_ge(s["i_done"], t - 1)
                act.copy(ct[:, b], c_ps[0:DST, 0:P]).then_inc(s["c_copied"], 1)

            def step(t, b, at):
                if at is None or at < N - 1:
                    front(t + 1, 1 - b, None if at is None else at + 1)
                act.wait_ge(s["y_ready"], t + 1)
                if some(at, 2):
                    act.wait_ge(s["sq_done"], t - 1)
                act.activation(sq[:, b], y[:, DS(t, 1), :].rearrange("p o d -> p (o d)"), ACT.Square,
                               accum_out=ssq[:, DS(t, 1)]).then_inc(s["sq_done"], 1)

            front(0, 0, 0)
            turns(act, step)

        @block.vector
        def _(dve):
            dve.memset(state[:, 0], 0.0).then_inc(s["state_ready"], 1)

            def step(t, b, at):
                dve.wait_ge(s["g_done"], t + 1)
                if some(at, 2):
                    dve.wait_ge(s["mt_done"], t - 1)
                dve.tensor_tensor(gm[:, b], g_ps[:, 0:P], u_incl, ALU.mult).then_inc(s["gm_done"], 1)
                dve.wait_ge(s["gm_done"], t + 1)
                dve.wait_ge(s["e_done"], t + 1)
                if some(at, 2):
                    dve.wait_ge(s["y_done"], t - 1)
                dve.tensor_tensor(mt[:, b], e[:, b], gm[:, b].rearrange("p (o i) -> p o i", o=1).broadcast_to([P, MH, P]),
                                  ALU.mult).then_inc(s["mt_done"], 1)
                dve.wait_ge(s["state_ready"], t + 1)
                if some(at, 1):
                    dve.wait_ge(s["i_done"], t)
                dve.tensor_tensor(state[:, 1 - b], state[:, b], head(etot, t)[0:DST].broadcast_to([DST, MH, HD]), ALU.mult).then_inc(s["sdec_done"], 1)
                dve.wait_ge(s["sdec_done"], t + 1)
                dve.wait_ge(s["u_done"], t + 1)
                dve.tensor_tensor(state[:, 1 - b], state[:, 1 - b], u_ps[0:DST, 0:DI].rearrange("p (h d) -> p h d", d=HD), ALU.add).then_inc(s["state_ready"], 1)
                dve.wait_ge(s["i_done"], t + 1)
                if some(at, 2):
                    dve.wait_ge(s["y_ready"], t - 1)
                dve.tensor_tensor(yt[:, b], i_ps[:, 0:DI].rearrange("p (h d) -> p h d", d=HD), head(ecum, t).broadcast_to([P, MH, HD]), ALU.mult).then_inc(s["yt1"], 1)
                dve.wait_ge(s["yt1"], t + 1)
                dve.wait_ge(s["dx_ready"], t + 1)
                dve.tensor_tensor(yt[:, b], yt[:, b], dx[:, b], ALU.add).then_inc(s["yt3"], 1)
                dve.wait_ge(s["yt3"], t + 1)
                dve.wait_ge(s["y_done"], t + 1)
                dve.tensor_tensor(yt[:, b], yt[:, b], y_ps[:, 0:DI].rearrange("p (h d) -> p h d", d=HD), ALU.add).then_inc(s["yt2"], 1)
                dve.wait_ge(s["yt2"], t + 1)
                dve.tensor_tensor(y[:, DS(t, 1), :].rearrange("p o d -> p (o d)"), yt[:, b].rearrange("p h d -> p (h d)"),
                                  sz[:, DS(t, 1), :].rearrange("p o d -> p (o d)"), ALU.mult).then_inc(s["y_ready"], 1)

            turns(dve, step)


def mamba_out_block(nc, y, ssq, w_out, x0, ident):
    ctx, sb, ps, sem = stage(nc)
    with ctx:
        std, rstd = sb("mo_std", [P, NT]), sb("mo_rstd", [P, NT])
        yt = sb("mo_t", [P, 2, 2, 2, P])
        tr, out = ps("mo_tr", [P, 2, QB]), ps("mo_out", [P, 2, QB])
        std_ready, rstd_ready, turned, copied, projected, added = (
            sem(f"mo_{n}") for n in ("std", "rstd", "turned", "copied", "projected", "added"))
        block = ctx.enter_context(nc.Block())
        NPAIR = NT // 2

        @block.tensor
        def _(pe):
            for n in range(NPAIR + 1):
                if n < NPAIR:
                    if n >= 2:
                        pe.wait_ge(copied, n - 1)
                    for i in range(2):
                        for c in range(2):
                            last = pe.transpose(tr[:, n % 2, (2 * i + c) * P:(2 * i + c + 1) * P], y[:, 2 * n + i, c * P:(c + 1) * P], ident)
                    last.then_inc(turned, 1)
                if n >= 1:
                    m = n - 1
                    pe.wait_ge(copied, m + 1)
                    if m >= 2:
                        pe.wait_ge(added, 2 * (m - 1))
                    for i in range(2):
                        for c in range(2):
                            last = pe.matmul(out[:, m % 2, i * P:(i + 1) * P], yt[:, m % 2, i, c], w_out[:, c], start=(c == 0), stop=(c == 1))
                    last.then_inc(projected, 1)

        @block.scalar
        def _(act):
            act.activation(std[:], ssq[:], ACT.Sqrt, bias=EPS, scale=1.0 / DI).then_inc(std_ready, 1)
            for n in range(NPAIR):
                act.wait_ge(turned, n + 1)
                if n >= 2:
                    act.wait_ge(projected, n - 1)
                act.copy(yt[:, n % 2].rearrange("p i c t -> p (i c t)"), tr[:, n % 2]).then_inc(copied, 1)

        @block.vector
        def _(dve):
            dve.wait_ge(std_ready, 1)
            dve.reciprocal(rstd[:], std[:]).then_inc(rstd_ready, 1)
            dve.wait_ge(rstd_ready, 1)
            for n in range(NPAIR):
                dve.wait_ge(projected, n + 1)
                for i in range(2):
                    t = 2 * n + i
                    dve.scalar_tensor_tensor(x0[:, t], out[:, n % 2, i * P:(i + 1) * P], rstd[:, t:t + 1], x0[:, t], ALU.mult, ALU.add).then_inc(added, 1)


def mlp_block(nc, vt, w_fc, fc_b, w_proj, proj_b, x0, x):
    ctx, sb, ps, sem = stage(nc)
    with ctx:
        h = sb("mlp_h", [P, 2, FC, QB])
        h_ps, o_ps = ps("mlp_hps", [P, FC, QB]), ps("mlp_ops", [P, 2, QB])
        h_done, gelu_done, o_done, x_step, sum_done = (sem(f"mlp_{n}") for n in ("h_done", "gelu", "o_done", "x_step", "sum_done"))
        block = ctx.enter_context(nc.Block())

        @block.tensor
        def _(pe):
            for b in range(NQB + 1):
                if b < NQB:
                    for c in range(FC):
                        if b:
                            pe.wait_ge(gelu_done, (b - 1) * FC + c + 1)
                        pe.matmul(h_ps[:, c], w_fc[:, c * P:(c + 1) * P], vt[:, b * QB:(b + 1) * QB], start=True, stop=True).then_inc(h_done, 1)
                if b:
                    n = b - 1
                    pe.wait_ge(gelu_done, (n + 1) * FC)
                    if n >= 2:
                        pe.wait_ge(sum_done, n - 1)
                    for i in range(TPB):
                        for c in range(FC):
                            last = pe.matmul(o_ps[:, n % 2, i * P:(i + 1) * P], h[:, n % 2, c, i * P:(i + 1) * P], w_proj[:, c],
                                             start=(c == 0), stop=(c == FC - 1))
                    last.then_inc(o_done, 1)

        @block.scalar
        def _(act):
            for n in range(NQB * FC):
                b, c = n // FC, n % FC
                act.wait_ge(h_done, n + 1)
                if b >= 2:
                    act.wait_ge(o_done, b - 1)
                act.activation(h[:, b % 2, c], h_ps[:, c], ACT.Gelu, bias=fc_b[:, c:c + 1]).then_inc(gelu_done, 1)

        @block.vector
        def _(dve):
            flat = lambda v, b: v[:, b * TPB:(b + 1) * TPB, :]
            for b in range(NQB):
                dve.tensor_tensor(flat(x, b), flat(x, b), flat(x0, b), ALU.add).then_inc(x_step, 1)
            dve.wait_ge(x_step, NQB)
            for b in range(NQB):
                dve.tensor_tensor(flat(x, b), flat(x, b), proj_b.rearrange("p (o d) -> p o d", o=1).broadcast_to([P, TPB, P]), ALU.add).then_inc(x_step, 1)
            for b in range(NQB):
                dve.wait_ge(x_step, NQB + b + 1)
                dve.wait_ge(o_done, b + 1)
                dve.tensor_tensor(flat(x, b), flat(x, b), o_ps[:, b % 2].rearrange("p (t d) -> p t d", d=P), ALU.add).then_inc(sum_done, 1)


def store_block(nc, x, out):
    ctx, sb, ps, sem = stage(nc)
    with ctx:
        stored = sem("stored")
        block = ctx.enter_context(nc.Block())

        @block.sync
        def _(sp):
            sp.dma_start(out.rearrange("(t p) d -> p t d", p=P), x[:]).then_inc(stored, 16)
            sp.wait_ge(stored, 16)


def vectors_layout():
    at, cols = 0, {}
    for name, width in (("ln1_w", 1), ("ln1_b", 1), ("ln2_w", 1), ("ln2_b", 1), ("conv_w", CCH * DCONV), ("conv_b", CCH),
                        ("dt_bias", MH), ("A_log", MH), ("D", MH), ("norm_w", 2), ("fc_b", FC), ("proj_b", P)):
        cols[name] = (at, width)
        at += width
    return cols, at


def rope_tables():
    inv = (np.float32(10000.0) ** (-np.arange(0, DK // 2, dtype=np.float32) * np.float32(2.0) / np.float32(DK))).astype(np.float32)
    ang = (np.arange(T, dtype=np.float32)[:, None] * inv[None, :]).astype(np.float32)
    cos, sin = np.cos(ang).astype(np.float32), np.sin(ang).astype(np.float32)
    c = np.repeat(cos, 2, axis=1).T
    s = np.stack([-sin, sin], axis=-1).reshape(T, DK).T
    return np.ascontiguousarray(np.stack([np.tile(c, (NH, 1)), np.tile(s, (NH, 1))], axis=1))


def mask_tables():
    row, col = np.arange(P)[:, None], np.arange(P)[None, :]
    f = lambda c, v: np.where(c, np.float32(v), np.float32(0))
    zero = np.zeros((P, P), np.float32)
    return np.ascontiguousarray(np.stack([f(row == col, 1), zero, zero, zero, f(col > row, NEG), f(row <= col, 1), f(row > col, 1)], axis=1))


def setup_block(nc, loads, masks, small):
    ctx, sb, ps, sem = stage(nc)
    with ctx:
        loaded, cast = sem("loaded"), sem("cast")
        block = ctx.enter_context(nc.Block())

        @block.sync
        def _(sp):
            for dst, src in loads:
                sp.dma_start(dst, src).then_inc(loaded, 16)
            sp.wait_ge(loaded, 16 * len(loads))

        @block.vector
        def _(dve):
            dve.wait_ge(loaded, 16 * len(loads))
            for i, m in enumerate(small):
                dve.tensor_copy(m, masks[:, i]).then_inc(cast, 1)
            dve.wait_ge(cast, len(small))


def program(nc, a, out, only=("att", "moe1", "mamba", "moe2")):
    ctx, sb, ps, sem = stage(nc)
    with ctx:
        before = nc.snapshot_sems()
        x = sb("x", [P, NT, P])
        masks = sb("masks", [P, 7, P])
        ident = masks[:, 0]
        identb = sb("identb", [P, P], BF16)
        maskq = masks[:, 1:5].rearrange("p a b -> p (a b)")
        watt = sb("watt", [P, 6, P])
        by_token = lambda t: t.rearrange("(t p) d -> p t d", p=P)
        watt_in = (watt[:], a["w_att"])
        w_gate, w_up, w_down = (sb(n, [P, NE * DH]) for n in ("w_gate", "w_up", "w_down"))
        wg, bg = sb("wg", [P, NE]), sb("bg", [P, NE])
        mt = sb("moe_tables", [P, a["moe_tables"].shape[1]])
        weights = sb("weights", [P, 2, NT])
        src_idx, dst_idx = sb("src_idx", [P, SLOT_TILES], U32), sb("dst_idx", [P, SLOT_TILES], U32)
        expert_of = sb("expert_of", [P, SLOT_TILES], I32)
        route = weights, src_idx, dst_idx, expert_of
        xn_dram = nc.dram_tensor("xn_rows", [T, P], F32).ap()
        y_dram = nc.dram_tensor("expert_rows", [DUMP + SLOT_TILES * P, P], F32).ap()
        w_mamba = sb("w_mamba", [P, CCH * P + DI + MH])
        w_out, w_fc, w_proj = sb("w_out", [P, 2, P]), sb("w_fc", [P, FC * P]), sb("w_proj", [P, FC, P])
        cols, width = vectors_layout()
        vectors = sb("vectors", [P, width])
        vec = {n: vectors[:, at:at + w] for n, (at, w) in cols.items()}
        small = dict(vec, conv_w=vec["conv_w"].rearrange("p (c k) -> p c k", k=DCONV))
        setup_block(nc, [(w_mamba[:], a["w_mamba"]), (w_out[:], a["w_out"]), (w_fc[:], a["w_fc"]), (w_proj[:], a["w_proj"]),
                         (vectors[:], a["vectors"]), (x[:], by_token(a["x"])), (masks[:], a["masks"]), watt_in, (mt[:], a["moe_tables"]),
                         (wg[:], a["wg"]), (bg[:], a["bg"]), (w_gate[:], a["w_gate"]), (w_up[:], a["w_up"]), (w_down[:], a["w_down"])],
                    masks, (identb[:],))

        def mixture(tag):
            with ExitStack() as m:
                xn = m.enter_context(nc.sbuf_tensor(f"{tag}_xn", [P, NT, P], F32))
                xnt = m.enter_context(nc.sbuf_tensor(f"{tag}_xnt", [P, T], F32))
                norm_block(nc, tag, x, xn, xnt, ident)
                route_block(nc, tag + "_", xn, xnt, wg[:], bg[:], mt[:], route, xn_dram)
            experts_block(nc, tag + "_", w_gate, w_up, w_down, route, x, ident, xn_dram, y_dram)

        if "att" in only:
            with ExitStack() as att:
                sba = lambda name, shape, dt=F32: att.enter_context(nc.sbuf_tensor(name, shape, dt))
                ao = sba("ao", [P, NT, P])
                vaug = sba("vaug", [P, NT, NH, DK + 1])
                qk = nc.dram_tensor("qk_parts", [2, 3, P, T], BF16).ap()
                stacks = [[sba(f"{n}{i}", [P, HG, T], BF16) for i in range(2)] for n in ("qst", "kst")]
                with ExitStack() as pre:
                    xnt = pre.enter_context(nc.sbuf_tensor("xnt", [P, T], F32))
                    norm_block(nc, "ln0", x, ao, xnt, ident)
                    qkv_block(nc, xnt, [watt[:, i] for i in range(5)], a["rope"], vaug, qk, stacks)
                attention_block(nc, stacks, qk, vaug, ao, ident, identb, maskq)
                project_add_block(nc, ao, watt[:, 5], x, ident)
        if "moe1" in only:
            mixture("moe1")
        nc.clear_and_free_semaphores(nc.allocated_since(before))
        nc.all_engine_barrier()
        if "mamba" in only:
            with ExitStack() as mam:
                sbm = lambda name, shape, dt=F32: mam.enter_context(nc.sbuf_tensor(name, shape, dt))
                x0 = sbm("x0", [P, NT, P])
                y, sz = sbm("y", [P, NT, DI]), sbm("sz", [P, NT, DI])
                conv = sbm("conv", [P, CCH, T])
                dt_raw, dt, rate, ecum, dec, etot = (sbm(n, [P, NT, MH]) for n in ("dt_raw", "dt", "rate", "ecum", "dec", "etot"))
                ssq = sbm("ssq", [P, NT])
                u_incl, below = masks[:, 5], masks[:, 6]
                norm_block(nc, "ln2", x, x0, None, ident)
                with ExitStack() as pre:
                    x0n = pre.enter_context(nc.sbuf_tensor("x0n", [P, NT, P], F32))
                    xnt = pre.enter_context(nc.sbuf_tensor("mxnt", [P, T], F32))
                    norm_block(nc, "ln3", x0, x0n, xnt, ident, vec["ln1_w"], vec["ln1_b"])
                    mamba_in_block(nc, xnt, w_mamba[:, 0:CCH * P], w_mamba[:, CCH * P:CCH * P + DI], w_mamba[:, CCH * P + DI:],
                                   small, conv, sz, dt_raw)
                mamba_rates_block(nc, dt_raw, small, dt, rate, ecum, dec, etot, w_out, vec["norm_w"], u_incl, below, mt[:, -P:])
                ssd_block(nc, conv, sz, dt, rate, ecum, dec, etot, vec["D"], y, ssq, ident, u_incl, below)
                mamba_out_block(nc, y, ssq, w_out, x0, ident)
                with ExitStack() as post:
                    x1n = post.enter_context(nc.sbuf_tensor("x1n", [P, NT, P], F32))
                    vt = post.enter_context(nc.sbuf_tensor("vt", [P, T], F32))
                    norm_block(nc, "ln4", x0, x1n, vt, ident, vec["ln2_w"], vec["ln2_b"])
                    mlp_block(nc, vt, w_fc, vec["fc_b"], w_proj, vec["proj_b"], x0, x)
        if "moe2" in only:
            mixture("moe2")
        store_block(nc, x, out)


def layouts(i):
    c = np.ascontiguousarray
    swap = np.arange(P) ^ 1
    att = [i["L0_attn_a_Wq"], i["L0_attn_a_Wq"][swap], i["L0_attn_a_Wk"], i["L0_attn_a_Wk"][swap],
           i["L0_attn_a_Wv"], i["L0_attn_a_Wo"]]
    rows = lambda v: np.broadcast_to(v, (P,) + v.shape)
    b = lambda name: i["L0_attn_b_" + name]
    w_in = b("in_proj_w")
    by_chunk = lambda v: v.reshape(-1, P).T
    vectors = {
        "ln1_w": b("ln1_w")[:, None], "ln1_b": b("ln1_b")[:, None], "ln2_w": b("ln2_w")[:, None], "ln2_b": b("ln2_b")[:, None],
        "conv_w": b("conv_w").reshape(CCH, P, DCONV).transpose(1, 0, 2).reshape(P, -1), "conv_b": by_chunk(b("conv_b")),
        "dt_bias": rows(b("dt_bias")), "A_log": rows(b("A_log")), "D": rows(b("D_param")), "norm_w": by_chunk(b("norm_w")),
        "fc_b": by_chunk(b("fc_b")), "proj_b": rows(b("proj_b")),
    }
    return {
        "x": c(i["L0_attn_a_x"].reshape(T, P)),
        "masks": mask_tables(), "rope": rope_tables(), "moe_tables": moe_tables(),
        "w_mamba": c(np.concatenate([w_in[DI:2 * DI + 2 * DST], w_in[:DI], w_in[2 * DI + 2 * DST:]]).T),
        "w_out": c(b("out_proj_w").reshape(P, 2, P).transpose(2, 1, 0)),
        "w_fc": c(b("fc_w").T), "w_proj": c(b("proj_w").reshape(P, FC, P).transpose(2, 1, 0)),
        "vectors": c(np.concatenate([vectors[n] for n in vectors_layout()[0]], axis=1)),
        "w_att": c(np.stack([w.T for w in att], axis=1)),
        "wg": c(i["L0_ffn_wg"].T), "bg": c(rows(i["L0_ffn_bg"])),
        "w_gate": c(i["L0_ffn_Wgate"].transpose(2, 0, 1).reshape(P, NE * DH)),
        "w_up": c(i["L0_ffn_Wup"].transpose(2, 0, 1).reshape(P, NE * DH)),
        "w_down": c(i["L0_ffn_Wdown"].reshape(NE, P, HC, P).transpose(3, 0, 2, 1).reshape(P, NE * DH)),
    }


def kernel(**inputs):
    import concourse.bacc as bacc
    from concourse.bass_utils import run_bass_kernel_spmd

    nc = bacc.Bacc("TRN2", target_bir_lowering=False, num_devices=1)
    arrays = {f"in_{k}": v for k, v in layouts({k: np.asarray(v) for k, v in inputs.items()}).items()}
    a = {k[3:]: nc.dram_tensor(k, v.shape, F32, kind="ExternalInput").ap() for k, v in arrays.items()}
    out = nc.dram_tensor("out_0", (T, P), F32, kind="ExternalOutput").ap()
    program(nc, a, out)
    r = run_bass_kernel_spmd(nc, [arrays], core_ids=[0])
    return r.results[0]["out_0"].reshape(1, T, P)
```

```python
from contextlib import ExitStack

import numpy as np

import concourse.bass as bass
from concourse import mybir

F32 = mybir.dt.float32
BF16 = mybir.dt.bfloat16
U32 = mybir.dt.uint32
I32 = mybir.dt.int32
ALU = mybir.AluOpType
ACT = mybir.ActivationFunctionType
AX_X = mybir.AxisListType.X
DS = bass.DynSlice

P = 128
T = 2048
NT = T // P
QB = 512
NQB = T // QB
TPB = QB // P
EPS = 1e-5
ROPE_BUFS = 3
ONES_BF16 = 0x3F803F80

NH, DK = 16, 8
HG = 4
NG = NH // HG
SCALE = float(1.0 / np.sqrt(np.float32(DK)))
NEG = -1e30
Q_PARTS = (0, 0, 1, 1, 0, 2, 1, 2)
K_PARTS = (0, 1, 0, 1, 2, 0, 2, 1)
MROW = 64
M_BANKS, S_BANKS = 3, 3
P_BUFS = 4
KROWS = 96


class Chain:

    def __init__(self, eng, sem):
        self.eng, self.sem, self.n = eng, sem, 0

    def __call__(self, ins):
        self.n += 1
        ins.then_inc(self.sem, 1)
        self.eng.wait_ge(self.sem, self.n)


def stage(nc, tag=""):
    ctx = ExitStack()
    sb = lambda name, shape, dt=F32: ctx.enter_context(nc.sbuf_tensor(tag + name, shape, dt))
    ps = lambda name, shape, dt=F32: ctx.enter_context(nc.psum_tensor(tag + name, shape, dt))
    sem = lambda name: nc.alloc_semaphore(tag + name)
    return ctx, sb, ps, sem


def norm_block(nc, tag, src, xn, xnt, ident, w=None, b=None, logits=None, xn_dram=None, measured=None, beside=None):
    ctx, sb, ps, sem = stage(nc)
    with ctx:
        st = measured if measured is not None else sb(f"{tag}_st", [P, NT, 6])
        half = sb(f"{tag}_half", [P, 4, NT])
        mean, var = half[:, 0], half[:, 1]
        rstd, shift = sb(f"{tag}_rstd", [P, NT]), sb(f"{tag}_shift", [P, NT])
        std = sb(f"{tag}_std", [P, NT])
        tr = ps(f"{tag}_tr", [P, 2, QB])
        stats, step, var_ready = sem(f"{tag}_stats"), sem(f"{tag}_step"), sem(f"{tag}_var_ready")
        std_ready, rstd_ready = sem(f"{tag}_std_ready"), sem(f"{tag}_rstd_ready")
        dve_ready, act_ready = sem(f"{tag}_dve_ready"), sem(f"{tag}_act_ready")
        dve_tiles = [t for t in range(NT) if t % TPB != TPB - 1]
        turned, evacuated = sem(f"{tag}_turned"), sem(f"{tag}_evacuated")
        multiplied, rows_out, beside_step = sem(f"{tag}_multiplied"), sem(f"{tag}_rows_out"), sem(f"{tag}_beside")
        block = ctx.enter_context(nc.Block())

        @block.vector
        def _(dve):
            link = Chain(dve, step)
            if measured is None:
                for t in range(NT):
                    dve.bn_stats(st[:, t, :], src[:, t, :]).then_inc(stats, 1)
                dve.wait_ge(stats, NT)
            link(dve.tensor_tensor(half[:, 2], st[:, :, 1], st[:, :, 4], ALU.subtract))
            link(dve.scalar_tensor_tensor(half[:, 2], half[:, 2], 0.25, half[:, 2], ALU.mult, ALU.mult))
            link(dve.tensor_tensor(half[:, 3], st[:, :, 2], st[:, :, 5], ALU.add))
            dve.scalar_tensor_tensor(var, half[:, 3], 1.0 / P, half[:, 2], ALU.mult, ALU.add).then_inc(var_ready, 1)
            link(dve.tensor_tensor(mean, st[:, :, 1], st[:, :, 4], ALU.add))
            link(dve.tensor_scalar(mean, mean, 0.5, None, ALU.mult))
            dve.wait_ge(std_ready, 1)
            link(dve.reciprocal(rstd[:], std[:]))
            dve.scalar_tensor_tensor(shift[:], mean, -1.0, rstd[:], ALU.mult, ALU.mult).then_inc(rstd_ready, 1)
            for t in dve_tiles:
                dve.tensor_scalar(xn[:, t, :], src[:, t, :], half[:, 0, t:t + 1], rstd[:, t:t + 1],
                                  ALU.subtract, ALU.mult).then_inc(dve_ready, 1)

        @block.gpsimd
        def _(pool):
            if beside is not None:
                beside(pool, Chain(pool, beside_step))

        @block.sync
        def _(sp):
            if xn_dram is not None:
                sp.wait_ge(dve_ready, len(dve_tiles))
                sp.wait_ge(act_ready, NT - len(dve_tiles))
                sp.dma_start(xn_dram.rearrange("(t p) d -> p t d", p=P), xn[:]).then_inc(rows_out, 16)
                sp.wait_ge(rows_out, 16)

        @block.scalar
        def _(act):
            act.wait_ge(var_ready, 1)
            act.activation(std[:], var, ACT.Sqrt, bias=EPS).then_inc(std_ready, 1)
            act.wait_ge(rstd_ready, 1)
            for q in range(NQB + 1):
                if q < NQB:
                    t = q * TPB + TPB - 1
                    act.activation(xn[:, t, :], src[:, t, :], ACT.Identity, bias=shift[:, t:t + 1], scale=rstd[:, t:t + 1]).then_inc(act_ready, 1)
                if xnt is None or not q:
                    continue
                q -= 1
                act.wait_ge(turned, q + 1)
                if w is None:
                    act.copy(xnt[:, q * QB:(q + 1) * QB], tr[:, q % 2, :]).then_inc(evacuated, 1)
                else:
                    act.activation(xnt[:, q * QB:(q + 1) * QB], tr[:, q % 2, :], ACT.Identity,
                                   bias=b, scale=w).then_inc(evacuated, 1)

        @block.tensor
        def _(pe):
            for q in range(NQB + 1 if xnt is not None else 0):
                if q < NQB:
                    if q >= 2:
                        pe.wait_ge(evacuated, q - 1)
                    for i in range(TPB):
                        t = q * TPB + i
                        if t in dve_tiles:
                            pe.wait_ge(dve_ready, dve_tiles.index(t) + 1)
                        else:
                            pe.wait_ge(act_ready, q + 1)
                        last = pe.transpose(tr[:, q % 2, i * P:(i + 1) * P], xn[:, t, :], ident[:])
                    last.then_inc(turned, 1)
                if q and logits is not None:
                    pe.wait_ge(evacuated, q)
                    for t in range((q - 1) * TPB, q * TPB):
                        last = pe.matmul(logits[0][:, t], xnt[:, t * P:(t + 1) * P], logits[1], start=True, stop=True)
                    last.then_inc(multiplied, 1)
            if logits is not None:
                pe.wait_ge(multiplied, NQB)


def qkv_block(nc, xnt, weights, cs, rope, rope_in, vaug, qk_dram, stacks):
    PARTS = 4
    wq, wqs, wk, wks, wv = weights
    ctx, sb, ps, sem = stage(nc)
    with ctx:
        t1, t2 = sb("rope_a", [P, 2, QB]), sb("rope_b", [P, 2, QB])
        rot, rest = sb("rot", [P, 3, QB]), sb("rest", [P, 3, QB])
        parts = sb("parts", [P, PARTS, 3, QB], BF16)
        proj = ps("proj", [P, 2, 2, QB])
        vps = ps("vps", [P, 2, QB])
        prepared = sem("prepared")
        projected, rope_read, rope_sum = sem("projected"), sem("rope_read"), sem("rope_sum")
        hi_done, rest_done, mid_done, lo_done = sem("hi_done"), sem("rest_done"), sem("mid_done"), sem("lo_done")
        parts_sent = [sem(f"parts_sent{i}") for i in range(PARTS)]
        v_done, v_copied = sem("v_done"), sem("v_copied")
        block = ctx.enter_context(nc.Block())
        NU = 2 * NQB

        @block.sync
        def _(sp):
            for n in range(NU):
                if n % 2 and n // 2 + ROPE_BUFS < NQB:
                    b = n // 2 + ROPE_BUFS
                    sp.wait_ge(rope_read, 2 * (n + 1))
                    sp.dma_start(cs[:, b % ROPE_BUFS], rope[:, :, b * QB:(b + 1) * QB]).then_inc(rope_in[b], 16)
                sp.wait_ge(lo_done, n + 1)
                blk = slice(n // 2 * QB, (n // 2 + 1) * QB)
                sp.dma_start(qk_dram[n % 2, :, :, blk].rearrange("c p n -> p c n"), parts[:, n % PARTS]).then_inc(parts_sent[n % PARTS], 16)
            for i in range(PARTS):
                sp.wait_ge(parts_sent[i], 16 * len(range(i, NU, PARTS)))

        @block.gpsimd
        def _(pool):
            link = Chain(pool, prepared)
            link(pool.memset(stacks[1][0][MROW:MROW + 3].bitcast(U32), ONES_BF16))
            for s in range(NU + 1):
                if s < NU:
                    pool.wait_ge(hi_done, s + 1)
                    pool.tensor_tensor(rest[:, s % 3], rot[:, s % 3], parts[:, s % PARTS, 0], ALU.subtract).then_inc(rest_done, 1)
                    pool.wait_ge(rest_done, s + 1)
                if s >= 1:
                    n = s - 1
                    pool.wait_ge(mid_done, n + 1)
                    pool.tensor_tensor(parts[:, n % PARTS, 2], rest[:, n % 3], parts[:, n % PARTS, 1], ALU.subtract).then_inc(lo_done, 1)
                    pool.wait_ge(lo_done, n + 1)

        @block.tensor
        def _(pe):
            for n in range(NU):
                if n >= 2:
                    pe.wait_ge(rope_read, 2 * (n - 1))
                blk = slice(n // 2 * QB, (n // 2 + 1) * QB)
                for s, wt in enumerate(((wq, wqs), (wk, wks))[n % 2]):
                    last = pe.matmul(proj[:, n % 2, s, :], wt, xnt[:, blk], start=True, stop=True)
                last.then_inc(projected, 1)
                if n % 2:
                    b = n // 2
                    if b >= 2:
                        pe.wait_ge(v_copied, b - 1)
                    for i in range(TPB):
                        t = b * TPB + i
                        last = pe.matmul(vps[:, b % 2, i * P:(i + 1) * P], xnt[:, t * P:(t + 1) * P], wv,
                                         start=True, stop=True)
                    last.then_inc(v_done, 1)

        @block.vector
        def _(dve):
            for s in range(NU):
                tab = cs[:, s // 2 % ROPE_BUFS]
                dve.wait_ge(rope_in[s // 2], 16)
                dve.wait_ge(projected, s + 1)
                dve.tensor_tensor(t1[:, s % 2], proj[:, s % 2, 0], tab[:, 0], ALU.mult).then_inc(rope_read, 1)
                dve.tensor_tensor(t2[:, s % 2], proj[:, s % 2, 1], tab[:, 1], ALU.mult).then_inc(rope_read, 1)
                dve.wait_ge(rope_read, 2 * s + 2)
                if s >= 3:
                    dve.wait_ge(rest_done, s - 2)
                dve.tensor_tensor(rot[:, s % 3], t1[:, s % 2], t2[:, s % 2], ALU.add).then_inc(rope_sum, 1)

        @block.scalar
        def _(act):
            for s in range(NU + 1):
                if s < NU:
                    act.wait_ge(rope_sum, s + 1)
                    if s >= PARTS:
                        act.wait_ge(parts_sent[s % PARTS], 16 * (s // PARTS))
                    act.copy(parts[:, s % PARTS, 0], rot[:, s % 3]).then_inc(hi_done, 1)
                if s >= 1:
                    n = s - 1
                    act.wait_ge(rest_done, n + 1)
                    act.copy(parts[:, n % PARTS, 1], rest[:, n % 3]).then_inc(mid_done, 1)
                if s % 2 and s < NU:
                    b = s // 2
                    act.wait_ge(v_done, b + 1)
                    act.copy(vaug[:, b * TPB:(b + 1) * TPB, :, 0:DK],
                             vps[:, b % 2].rearrange("p (i h d) -> p i h d", i=TPB, d=DK)).then_inc(v_copied, 1)


def attention_plan():
    blocks = [(g, j) for g in range(NG) for j in (range(NQB) if g < NG - 1 else reversed(range(NQB)))]
    steps = []
    for c, (g, j) in enumerate(blocks):
        d = TPB * j
        steps += [(c, [(kt, 0, 0)], HG) for kt in range(d)]
        steps += [(c, [(d, 0, 0)], HG), (c, [(d + 1, 0, P), (d + 3, 3 * P, 3 * P)], HG), (c, [(d + 2, 0, 2 * P)], HG // 2)]
    slots = [(s, k) for s, st in enumerate(steps) for k in range(st[2])]
    units = [(c, i, h, b) for c, (g, j) in enumerate(blocks) for i in range(TPB) for h in range(HG) for b in range(j + 1)]
    last_step = {st[0]: s for s, st in enumerate(steps)}
    SEM, NEVER = 0.1, 1e9
    now = dve = act = pool = 0.0
    reduced, exped, cut, valued = [], [], {}, []
    nt_at, rows_at, gathered, o_free = {}, {}, {}, 0.0
    stack_at = {0: 0.0, 1: 1.0}
    events = []
    m = s = v = rows = turned = 0
    slot_end = []
    for st in steps:
        slot_end.append((slot_end[-1] if slot_end else 0) + st[2])
    while turned < len(blocks):
        cand = []
        if rows in nt_at:
            cand.append((nt_at[rows], 0, "rows"))
        if turned in gathered:
            cand.append((gathered[turned], 1, "turn"))
        if m < len(units):
            g = blocks[units[m][0]][0]
            if g in stack_at:
                cand.append((max(stack_at[g], reduced[m - M_BANKS] + SEM if m >= M_BANKS else 0.0), 2, "max"))
        if s < len(slots):
            step = slots[s][0]
            if steps[step][0] in rows_at and (step < P_BUFS or v > step - P_BUFS):
                t = rows_at[steps[step][0]]
                if s >= S_BANKS:
                    t = max(t, exped[s - S_BANKS] + SEM)
                cand.append((t, 3, "scores"))
        if v < len(steps) and slot_end[v] <= len(exped):
            t = max(exped[slot_end[v] - 1] + SEM, cut.get(v, 0.0) + SEM)
            if v == 0 or steps[v - 1][0] != steps[v][0]:
                t = max(t, o_free + SEM)
            cand.append((t, 4, "values"))
        t, _, what = min((max(t, now), rank, what) for t, rank, what in cand)
        now = t
        if what == "max":
            c, i, h, b = units[m]
            w = QB if b < blocks[c][1] else (i + 1) * P
            now += 0.216 * w / QB
            dve = max(dve, now + SEM) + 0.065 + 0.535 * w / QB
            reduced.append(dve)
            events.append(("max", units[m], m))
            m += 1
            if m == len(units) or units[m][0] != c:
                events.append(("chain", c, m))
                dve += 0.15
                pool = max(pool, dve + SEM) + 1.8
                nt_at[c] = pool + SEM
        elif what == "rows":
            now += 0.22
            act = max(act, now + SEM) + 0.48
            rows_at[rows] = act + 3.0
            events.append(("rows", rows))
            rows += 1
        elif what == "scores":
            step, k = slots[s]
            now += 0.216
            act = max(act, now + SEM, valued[step - P_BUFS] + SEM if step >= P_BUFS else 0.0) + 0.48
            exped.append(act)
            events.append(("scores", step, k, s))
            s += 1
            if k == steps[step][2] - 1:
                if steps[step][1][0][0] >= TPB * blocks[steps[step][0]][1]:
                    pool = max(pool, act + SEM) + 0.65 * len(steps[step][1])
                    cut[step] = pool
                c = steps[step][0]
                if s == len(slots) or steps[slots[s][0]][0] != c:
                    g = blocks[c][0]
                    if all(blocks[x][0] != g for x in range(c + 1, len(blocks))):
                        stack_at[g + 2] = now + 12.0
        elif what == "values":
            now += 0.86
            valued.append(now)
            events.append(("values", v))
            c = steps[v][0]
            v += 1
            if last_step[c] == v - 1:
                act = max(act, now + SEM) + 0.48
                gathered[c] = act + SEM
                o_free = act
                events.append(("gather", c, v))
        else:
            now += 0.45
            dve = max(dve, now + SEM) + 0.4
            events.append(("turn", turned))
            turned += 1
    return blocks, steps, slot_end, events


def attention_block(nc, stacks, qk_dram, vaug, ao, ident, identb, maskq, late):
    blocks, steps, slot_end, events = attention_plan()
    qst, kst = stacks
    ctx, sb, ps, sem = stage(nc)
    with ctx:
        prob = sb("prob", [P, P_BUFS, HG, QB])
        pmax = sb("pmax", [P, 2, TPB * HG, NQB])
        small = sb("small", [P, 3, TPB * HG])
        nt = sb("nt", [P, TPB, 3, HG], BF16)
        ntt = sb("ntt", [3 * HG, QB], BF16)
        osb = sb("osb", [P, QB])
        rec = sb("rec", [P, TPB, HG])
        s_ps = ps("s_ps", [P, S_BANKS, QB])
        m_ps = ps("m_ps", [P, M_BANKS, QB])
        o_ps = ps("o_ps", [P, QB])
        t_ps = ps("t_ps", [P, QB])
        stack_in, cleared = [sem(f"stack_in{i}") for i in range(2)], sem("cleared")
        late_in, first_in, ones_there = sem("late_in"), sem("first_in"), sem("ones_there")
        DIRECT = 6
        scores_ready, exp_done, cut_done, pv_done = sem("scores_ready"), sem("exp_done"), sem("cut_done"), sem("pv_done")
        max_ready, reduced, max_found = sem("max_ready"), sem("reduced"), sem("max_found")
        pool_step, nt_ready, nt_turned = sem("pool_step"), sem("nt_ready"), sem("nt_turned")
        ntt_ready, mrow_in, turn_free = sem("ntt_ready"), sem("mrow_in"), sem("turn_free")
        o_copied, o_turned, rec_done = sem("o_copied"), sem("o_turned"), sem("rec_done")
        block = ctx.enter_context(nc.Block())
        cuts = {}
        for s, (c, tiles, _) in enumerate(steps):
            if tiles[0][0] >= TPB * blocks[c][1]:
                cuts[s] = len(cuts)
        uses = [e for e in events if e[0] in ("rows", "turn")]
        first_step = lambda s: s == 0 or steps[s - 1][0] != steps[s][0]

        def head_at(step, slot, h):
            return (h, 0) if steps[step][2] == HG else (h // 2, h % 2 * 2 * P)

        def load_stack(eng, g, which, rows=range(len(Q_PARTS)), done=None):
            stack, order = (qst, kst)[which][g % 2], (Q_PARTS, K_PARTS)[which]
            for r in rows:
                part = qk_dram[which, order[r], g * HG * DK:(g + 1) * HG * DK, :]
                eng.dma_start(stack[r * DK:(r + 1) * DK], part.rearrange("(h d) n -> d h n", d=DK)).then_inc(
                    done or stack_in[g % 2], 16)

        def clear_maxima(eng, g):
            eng.dma_start(qst[g % 2][MROW:MROW + 3], qst[g % 2][MROW + 3:MROW + 6]).then_inc(stack_in[g % 2], 16)

        def stacks_in(g):
            direct = (2 * DIRECT, 2 * len(Q_PARTS))[g % 2]
            return 16 * (direct + (g // 2) * (2 * len(Q_PARTS) + 1))

        @block.tensor
        def _(pe):
            pe.wait_ge(cleared, 1)
            for e in events:
                if e[0] == "max":
                    _, (c, i, h, b), n = e
                    g, j = blocks[c]
                    if i == h == b == 0:
                        pe.wait_ge(stack_in[g % 2], stacks_in(g))
                        if g == 1:
                            pe.wait_ge(ones_there, 1)
                        if c == 0:
                            pe.wait_ge(first_in, 16 * 2 * (len(Q_PARTS) - DIRECT))
                    if n >= M_BANKS:
                        pe.wait_ge(reduced, n - M_BANKS + 1)
                    w = QB if b < j else (i + 1) * P
                    tile = TPB * j + i
                    pe.matmul(m_ps[:, n % M_BANKS, 0:w], qst[g % 2][0:KROWS, h, tile * P:(tile + 1) * P],
                              kst[g % 2][0:KROWS, h, b * QB:b * QB + w], start=True, stop=True).then_inc(max_ready, 1)
                elif e[0] == "rows":
                    pe.wait_ge(nt_ready, e[1] + 1)
                    if uses.index(e):
                        pe.wait_ge(turn_free, uses.index(e))
                    for i in range(TPB):
                        last = pe.transpose(t_ps[:].bitcast(BF16)[0:3 * HG, i * P:(i + 1) * P],
                                            nt[:, i].rearrange("p c h -> p (c h)"), identb[:])
                    last.then_inc(nt_turned, 1)
                elif e[0] == "scores":
                    _, s, k, slot = e
                    c, tiles, n_slots = steps[s]
                    g, j = blocks[c]
                    if slot >= S_BANKS:
                        pe.wait_ge(exp_done, slot - S_BANKS + 1)
                    if k == 0 and first_step(s):
                        pe.wait_ge(mrow_in, 48 * (c + 1))
                    for h in range(HG):
                        if head_at(s, k, h)[0] != k:
                            continue
                        for kt, col, q0 in tiles:
                            at = head_at(s, k, h)[1] + col
                            last = pe.matmul(s_ps[:, slot % S_BANKS, at:at + QB - q0], kst[g % 2][0:KROWS, h, kt * P:(kt + 1) * P],
                                             qst[g % 2][0:KROWS, h, j * QB + q0:(j + 1) * QB], start=True, stop=True)
                    last.then_inc(scores_ready, 1)
                elif e[0] == "values":
                    s = e[1]
                    c, tiles, _ = steps[s]
                    g, j = blocks[c]
                    pe.wait_ge(exp_done, slot_end[s])
                    if s in cuts:
                        pe.wait_ge(cut_done, cuts[s] + 1)
                    if first_step(s) and c:
                        pe.wait_ge(o_copied, c)
                    for kt, col, q0 in tiles:
                        for h in range(HG):
                            k, at = head_at(s, None, h)
                            last = pe.matmul(o_ps[32 * h:32 * h + DK + 1, q0:QB], vaug[:, kt, g * HG + h, :],
                                             prob[:, s % P_BUFS, k, at + col:at + col + QB - q0],
                                             start=(kt == 0), stop=(kt == TPB * j + 2), skip_group_check=True, tile_position=(0, 32 * h))
                    last.then_inc(pv_done, 1)
                elif e[0] == "turn":
                    pe.wait_ge(o_copied, e[1] + 1)
                    pe.wait_ge(turn_free, uses.index(e))
                    for i in range(TPB):
                        last = pe.transpose(t_ps[:, i * P:(i + 1) * P], osb[:, i * P:(i + 1) * P], ident[:])
                    last.then_inc(o_turned, 1)

        @block.vector
        def _(dve):
            dve.memset(o_ps[:], 0.0).then_inc(cleared, 1)
            for e in events:
                if e[0] == "max":
                    _, (c, i, h, b), n = e
                    dve.wait_ge(max_ready, n + 1)
                    found = pmax[:, c % 2, i * HG + h, b:b + 1]
                    if b < blocks[c][1]:
                        dve.reduce_max(found, m_ps[:, n % M_BANKS], AX_X).then_inc(reduced, 1)
                    else:
                        w = (i + 1) * P
                        dve.tensor_tensor_reduce(m_ps[:, n % M_BANKS, 0:w], m_ps[:, n % M_BANKS, 0:w], maskq[:, QB - w:QB], 1.0, NEG,
                                                 ALU.add, ALU.max, found).then_inc(reduced, 1)
                elif e[0] == "chain":
                    _, c, n = e
                    dve.wait_ge(reduced, n)
                    if c:
                        dve.wait_ge(nt_ready, c)
                    dve.reduce_max(small[:, 0].rearrange("p (a o) -> p a o", o=1), pmax[:, c % 2, :, 0:blocks[c][1] + 1],
                                   AX_X).then_inc(max_found, 1)
                elif e[0] == "turn":
                    c = e[1]
                    g, j = blocks[c]
                    dve.wait_ge(o_turned, c + 1)
                    v = t_ps[:].rearrange("p (i h d) -> p i h d", i=TPB, h=HG)
                    dve.reciprocal(rec[:], v[:, :, :, DK]).then_inc(rec_done, 1)
                    dve.wait_ge(rec_done, c + 1)
                    dve.tensor_tensor(ao[:, j * TPB:(j + 1) * TPB, g * HG * DK:(g + 1) * HG * DK].rearrange("p i (h d) -> p i h d", h=HG),
                                      v[:, :, :, 0:DK], rec[:].rearrange("p i (h o) -> p i h o", o=1).broadcast_to([P, TPB, HG, DK]),
                                      ALU.mult).then_inc(turn_free, 1)

        @block.scalar
        def _(act):
            load_stack(act, 0, 1, range(DIRECT))
            load_stack(act, 1, 1)
            for e in events:
                if e[0] == "rows":
                    c = e[1]
                    act.wait_ge(nt_turned, c + 1)
                    if c:
                        act.wait_ge(mrow_in, 48 * c)
                    act.copy(ntt[:], t_ps[:].bitcast(BF16)[0:3 * HG, 0:QB]).then_inc(ntt_ready, 1)
                    act.wait_ge(ntt_ready, c + 1)
                    act.sem_inc(turn_free, 1)
                elif e[0] == "scores":
                    _, s, k, slot = e
                    act.wait_ge(scores_ready, slot + 1)
                    if k == 0 and s >= P_BUFS:
                        act.wait_ge(pv_done, s - P_BUFS + 1)
                    act.activation(prob[:, s % P_BUFS, k, :], s_ps[:, slot % S_BANKS], ACT.Exp, scale=SCALE).then_inc(exp_done, 1)
                elif e[0] == "gather":
                    _, c, done = e
                    act.wait_ge(pv_done, done)
                    if c:
                        act.wait_ge(o_turned, c)
                    act.copy(osb[:], o_ps[:]).then_inc(o_copied, 1)

        @block.gpsimd
        def _(pool):
            for which in range(2):
                load_stack(pool, 0, which, range(DIRECT, len(Q_PARTS)), first_in)
            pool.memset(kst[1][MROW:MROW + 3].bitcast(U32), ONES_BF16).then_inc(ones_there, 1)
            pool.wait_ge(ones_there, 1)
            link = Chain(pool, pool_step)
            for e in events:
                if e[0] == "chain":
                    c = e[1]
                    pool.wait_ge(max_found, c + 1)
                    hi, mid, lo = (nt[:, :, k, :] for k in range(3))
                    neg = small[:, 1].rearrange("p (i h) -> p i h", h=HG)
                    rst = small[:, 2].rearrange("p (i h) -> p i h", h=HG)
                    if c:
                        pool.wait_ge(nt_turned, c)
                    link(pool.tensor_scalar(small[:, 1], small[:, 0], -1.0, None, ALU.mult))
                    link(pool.tensor_copy(hi, neg))
                    link(pool.tensor_tensor(rst, neg, hi, ALU.subtract))
                    link(pool.tensor_copy(mid, rst))
                    pool.tensor_tensor(lo, rst, mid, ALU.subtract).then_inc(nt_ready, 1)
                    pool.wait_ge(nt_ready, c + 1)
                elif e[0] == "scores":
                    _, s, k, slot = e
                    c, tiles, n_slots = steps[s]
                    if s not in cuts or k < n_slots - 1:
                        continue
                    pool.wait_ge(exp_done, slot + 1)
                    src = prob[:, s % P_BUFS]
                    if n_slots == HG:
                        where = [src[:, :, col:col + P] for _, col, _ in tiles]
                    else:
                        where = [src[:, 0:n_slots].rearrange("p s (k q) -> p (s k) q", k=2)[:, :, 0:P]]
                    for cut in where:
                        last = pool.affine_select(out=cut, in_=cut, compare_op=ALU.is_ge, fill=0.0, base=0,
                                                  pattern=[[0, HG], [1, P]], channel_multiplier=-1)
                    last.then_inc(cut_done, 1)

        @block.sync
        def _(sp):
            load_stack(sp, 0, 0, range(DIRECT))
            load_stack(sp, 1, 0)
            for e in events:
                if e[0] == "rows":
                    c = e[1]
                    g, j = blocks[c]
                    sp.wait_ge(ntt_ready, c + 1)
                    for k in range(3):
                        sp.dma_start(qst[g % 2][MROW + k:MROW + k + 1, :, j * QB:(j + 1) * QB],
                                     ntt[HG * k:HG * (k + 1), :]).then_inc(mrow_in, 16)
                    for dst, src in late[2 * c:2 * c + 2]:
                        sp.dma_start(dst, src).then_inc(late_in, 16)
                elif e[0] == "scores" and e[3] + 1 == slot_end[e[1]]:
                    g = blocks[steps[e[1]][0]][0]
                    ends = e[1] + 1 == len(steps) or blocks[steps[e[1] + 1][0]][0] != g
                    if ends and g + 2 < NG:
                        sp.wait_ge(scores_ready, e[3] + 1)
                        clear_maxima(sp, g + 2)
                        load_stack(sp, g + 2, 0)
                        load_stack(sp, g + 2, 1)
            assert len(late) <= 2 * len(blocks)
            sp.wait_ge(late_in, 16 * len(late))
            sp.wait_ge(mrow_in, 48 * len(blocks))
            for i in range(2):
                sp.wait_ge(stack_in[i], stacks_in(NG - 2 + i))


def project_add_block(nc, src, w, x, ident, st):
    ctx, sb, ps, sem = stage(nc)
    with ctx:
        turned_sb = sb("pa_t", [P, 2, QB])
        tr, out = ps("pa_tr", [P, 2, QB]), ps("pa_out", [P, 2, QB])
        turned, copied, projected, added = sem("pa_turned"), sem("pa_copied"), sem("pa_projected"), sem("pa_added")
        measured = sem("pa_measured")
        block = ctx.enter_context(nc.Block())

        @block.tensor
        def _(pe):
            for q in range(NQB + 1):
                if q < NQB:
                    if q >= 2:
                        pe.wait_ge(copied, q - 1)
                    for i in range(TPB):
                        last = pe.transpose(tr[:, q % 2, i * P:(i + 1) * P], src[:, q * TPB + i, :], ident[:])
                    last.then_inc(turned, 1)
                if q >= 1:
                    n = q - 1
                    pe.wait_ge(copied, n + 1)
                    if n >= 2:
                        pe.wait_ge(added, n - 1)
                    for i in range(TPB):
                        last = pe.matmul(out[:, n % 2, i * P:(i + 1) * P], turned_sb[:, n % 2, i * P:(i + 1) * P], w,
                                         start=True, stop=True)
                    last.then_inc(projected, 1)

        @block.scalar
        def _(act):
            for q in range(NQB):
                act.wait_ge(turned, q + 1)
                if q >= 2:
                    act.wait_ge(projected, q - 1)
                act.copy(turned_sb[:, q % 2], tr[:, q % 2]).then_inc(copied, 1)

        @block.vector
        def _(dve):
            for q in range(NQB):
                dve.wait_ge(projected, q + 1)
                xs = x[:, q * TPB:(q + 1) * TPB, :].rearrange("p t d -> p (t d)")
                dve.tensor_tensor(xs, xs, out[:, q % 2], ALU.add).then_inc(added, 1)
                dve.wait_ge(added, q + 1)
                for t in range(q * TPB, (q + 1) * TPB):
                    dve.bn_stats(st[:, t, :], x[:, t, :]).then_inc(measured, 1)
            dve.wait_ge(measured, NT)


NE, DH = 8, 512
HC = DH // P
SLOT_TILES = (2 * T + NE * (P - 1)) // P
X_BUFS, AHEAD = 4, 3
DUMP = 2 * T


def moe_tables():
    row = lambda v: np.broadcast_to(np.asarray(v, np.float32), (P, len(v)))
    return np.ascontiguousarray(np.concatenate([
        row(NE - np.arange(NE)), row(np.arange(P)), row(np.arange(SLOT_TILES)), row(np.arange(2 * NT)), np.arange(1, P + 1, dtype=np.float32)[:, None],
        (DUMP + 1 + np.arange(SLOT_TILES)[None, :] * P + np.arange(P)[:, None]).astype(np.float32), row(np.arange(NE * NT) % NT != 0),
        -(np.arange(P)[None, :] <= np.arange(P)[:, None]).astype(np.float32),
        np.ones((P, P), np.float32)], axis=1).astype(np.float32))


def moe_table_slices(t):
    out, at = [], 0
    for n in (NE, P, SLOT_TILES, 2 * NT, 1, SLOT_TILES, NE * NT, P, P):
        out.append(t[:, at:at + n])
        at += n
    return out


def route_block(nc, tag, lg_ps, bg, tables, route):
    weights, src_idx, dst_idx, expert_of = route
    desc, iota_lo, iota_hi, row_tile, row_in_tile, dump, not_first, not_before, ones = moe_table_slices(tables)
    NHOT, HOTS = 2 * NT, 8
    NG_HOT = NHOT // HOTS
    ctx, sb, ps, sem = stage(nc, tag)
    with ctx:
        lg = sb("lg", [P, NT, NE])
        one = sb("one", [P, 2, NT, NE])
        tmp, key = sb("rt_tmp", [P, NT, NE]), sb("rt_key", [P, NT, NE])
        both = sb("both", [P, NT, NE])
        top, kmax = sb("top", [P, 2, NT]), sb("kmax", [P, 2, NT])
        ex, den = sb("rt_ex", [P, 2, NT]), sb("rt_den", [P, NT])
        cum = sb("cum", [P, NE, NT])
        cnt = sb("cnt", [P, NE], I32)
        tiles_e, tcum, base = sb("tiles_e", [P, NE]), sb("tcum", [P, NE]), sb("base", [P, NE])
        mine = sb("mine", [P, 2, NT, NE])
        slot = sb("slot", [P, 2 * NT])
        sloti, part = sb("sloti", [P, 2 * NT], I32), sb("part", [P, 2, 2 * NT], I32)
        hilo = sb("hilo", [P, 2, 2 * NT])
        onelo, onehi = sb("onelo", [P, 2, HOTS, P], BF16), sb("onehi", [P, NHOT, SLOT_TILES])
        hot = sb("hot", [P, NHOT, 2, SLOT_TILES], BF16)
        inv, t2 = sb("inv", [P, SLOT_TILES]), sb("inv2", [P, 3, SLOT_TILES])
        ge = sb("ge", [P, SLOT_TILES, NE])
        eo = sb("eo", [P, SLOT_TILES])
        rank_ps, tot_ps = ps("rank_ps", [P, NT, NE]), ps("tot_ps", [P, NE, NT])
        inv_ps = ps("inv_ps", [P, 2, SLOT_TILES])
        step, gap_ready, exp_ready, mask_ready, ranked = (sem(n) for n in ("rt_step", "gap_ready", "exp_ready", "mask_ready", "ranked"))
        parts_ready, hi_found, tile_ready, row_ready, lo_ready, hot_used = (sem(n) for n in ("parts_ready", "hi_found", "tile_ready", "row_ready", "lo_ready", "hot_used"))
        block = ctx.enter_context(nc.Block())
        bc = lambda v: v.rearrange("p (t o) -> p t o", o=1).broadcast_to([P, NT, NE])
        row = lambda v, n: v.rearrange("p (o e) -> p o e", o=1).broadcast_to([P, n, v.shape[-1]])
        col = lambda v, n: v.rearrange("p (t o) -> p t o", o=1).broadcast_to([P, v.shape[-1], n])

        @block.tensor
        def _(pe):
            pe.wait_ge(mask_ready, 1)
            pe.matmul(rank_ps[:].rearrange("p t e -> p (t e)"), not_before, both[:].rearrange("p t e -> p (t e)"), start=True, stop=True)
            pe.matmul(tot_ps[:], ones, both[:].rearrange("p t e -> p e t"), start=True, stop=True).then_inc(ranked, 1)
            for g in range(NG_HOT):
                pe.wait_ge(tile_ready, g + 1)
                pe.wait_ge(row_ready, g + 1)
                pe.wait_ge(lo_ready, g + 1)
                for k in range(HOTS):
                    n = g * HOTS + k
                    last = pe.matmul(inv_ps[:], onelo[:, g % 2, k], hot[:, n], start=(n == 0), stop=(n == NHOT - 1))
                last.then_inc(hot_used, 1)

        @block.scalar
        def _(act):
            act.wait_ge(gap_ready, 1)
            act.activation(ex[:, 1], ex[:, 0], ACT.Exp).then_inc(exp_ready, 1)
            for g in range(NG_HOT):
                hots = slice(g * HOTS, (g + 1) * HOTS)
                act.wait_ge(hi_found, g + 1)
                act.activation(hot[:, hots, 1], onehi[:, hots], ACT.Copy, scale=row_in_tile).then_inc(row_ready, 1)

        @block.gpsimd
        def _(pool):
            for g in range(NG_HOT):
                hots = slice(g * HOTS, (g + 1) * HOTS)
                pool.wait_ge(hi_found, g + 1)
                pool.tensor_tensor(hot[:, hots, 0], onehi[:, hots], col(row_tile[:, hots], SLOT_TILES), ALU.mult).then_inc(tile_ready, 1)
                pool.wait_ge(tile_ready, g + 1)

        @block.vector
        def _(dve):
            link = Chain(dve, step)
            link(dve.tensor_tensor(lg[:], lg_ps[:], row(bg, NT), ALU.add))
            for k in range(2):
                link(dve.reduce_max(top[:, k].rearrange("p (t o) -> p t o", o=1), lg[:], AX_X))
                link(dve.tensor_tensor(tmp[:], lg[:], bc(top[:, k]), ALU.is_equal))
                link(dve.tensor_tensor(key[:], tmp[:], row(desc, NT), ALU.mult))
                link(dve.reduce_max(kmax[:, k].rearrange("p (t o) -> p t o", o=1), key[:], AX_X))
                link(dve.tensor_tensor(one[:, k], key[:], bc(kmax[:, k]), ALU.is_equal))
                if k == 0:
                    link(dve.tensor_scalar(tmp[:], one[:, 0], 0.0, None, ALU.is_equal))
                    link(dve.tensor_tensor(lg[:], lg[:], tmp[:], ALU.mult))
                    link(dve.scalar_tensor_tensor(lg[:], one[:, 0], -3e38, lg[:], ALU.mult, ALU.add))
            dve.tensor_tensor(both[:], one[:, 0], one[:, 1], ALU.add).then_inc(mask_ready, 1)
            dve.tensor_tensor(ex[:, 0], top[:, 1], top[:, 0], ALU.subtract).then_inc(gap_ready, 1)
            dve.wait_ge(exp_ready, 1)
            link(dve.tensor_scalar(den[:], ex[:, 1], 1.0, None, ALU.add))
            link(dve.reciprocal(weights[:, 0], den[:]))
            link(dve.tensor_tensor(weights[:, 1], weights[:, 0], ex[:, 1], ALU.mult))
            dve.wait_ge(ranked, 1)
            link(dve.tensor_tensor_scan(cum[:].rearrange("p e t -> p (e t)"), not_first, tot_ps[:].rearrange("p e t -> p (e t)"),
                                        0.0, ALU.mult, ALU.add))
            link(dve.tensor_scalar(cnt[:], cum[:, :, NT - 1], float(P - 1), None, ALU.add))
            link(dve.tensor_scalar(cnt[:], cnt[:], 7, None, ALU.arith_shift_right))
            link(dve.tensor_copy(tiles_e[:], cnt[:]))
            link(dve.tensor_tensor_scan(tcum[:], ones[:, 0:NE], tiles_e[:], 0.0, ALU.mult, ALU.add))
            link(dve.tensor_tensor(base[:], tcum[:], tiles_e[:], ALU.subtract))
            link(dve.tensor_tensor(tmp[:], cum[:].rearrange("p e t -> p t e"), rank_ps[:], ALU.add))
            link(dve.scalar_tensor_tensor(tmp[:], row(base[:], NT), float(P), tmp[:], ALU.mult, ALU.add))
            for k in range(2):
                link(dve.tensor_tensor(mine[:, k], one[:, k], tmp[:], ALU.mult))
            link(dve.reduce_sum(slot[:].rearrange("p (t o) -> p t o", o=1), mine[:].rearrange("p k t e -> p (k t) e"), AX_X))
            link(dve.tensor_copy(sloti[:], slot[:]))
            link(dve.tensor_scalar(part[:, 0], sloti[:], 7, None, ALU.arith_shift_right))
            link(dve.tensor_scalar(part[:, 1], sloti[:], P - 1, None, ALU.bitwise_and))
            dve.tensor_copy(hilo[:], part[:]).then_inc(parts_ready, 1)
            dve.wait_ge(parts_ready, 1)
            for g in range(NG_HOT):
                hots = slice(g * HOTS, (g + 1) * HOTS)
                dve.tensor_tensor(onehi[:, hots], row(iota_hi, HOTS), col(hilo[:, 0, hots], SLOT_TILES), ALU.is_equal).then_inc(hi_found, 1)
                if g >= 2:
                    dve.wait_ge(hot_used, g - 1)
                dve.tensor_tensor(onelo[:, g % 2], row(iota_lo, HOTS), col(hilo[:, 1, hots], P),
                                  ALU.is_equal).then_inc(lo_ready, 1)
                if g == NG_HOT - 1:
                    link(dve.tensor_tensor(ge[:], col(iota_hi, NE), row(tcum[:], SLOT_TILES), ALU.is_ge))
                    link(dve.reduce_sum(eo[:].rearrange("p (s o) -> p s o", o=1), ge[:], AX_X))
                    link(dve.tensor_scalar(expert_of[:], eo[:], float(NE - 1), float(DH), ALU.min, ALU.mult))
            dve.wait_ge(hot_used, NG_HOT)
            link(dve.tensor_copy(inv[:], inv_ps[:, 1]))
            link(dve.scalar_tensor_tensor(inv[:], inv_ps[:, 0], float(P), inv[:], ALU.mult, ALU.add))
            link(dve.tensor_scalar(t2[:, 0], inv[:], 0.0, None, ALU.is_equal))
            link(dve.tensor_scalar(t2[:, 1], inv[:], float(T), float(-T), ALU.is_gt, ALU.mult))
            link(dve.tensor_tensor(t2[:, 1], t2[:, 1], t2[:, 0], ALU.add))
            link(dve.tensor_tensor(t2[:, 1], t2[:, 1], inv[:], ALU.add))
            link(dve.tensor_scalar(src_idx[:], t2[:, 1], -1.0, None, ALU.add))
            link(dve.tensor_tensor(t2[:, 2], t2[:, 0], dump, ALU.mult))
            link(dve.tensor_tensor(t2[:, 2], t2[:, 2], inv[:], ALU.add))
            link(dve.tensor_scalar(dst_idx[:], t2[:, 2], -1.0, None, ALU.add))


def experts_block(nc, tag, w_gate, w_up, w_down, route, x, ident, xn_dram, y_dram, out):
    weights, src_idx, dst_idx, expert_of = route
    ctx, sb, ps, sem = stage(nc, tag)
    with ctx:
        xg, xt = sb("xg", [P, X_BUFS, P]), sb("xt", [P, 2, P])
        wg_now, wu_now = sb("wg_now", [P, 2, DH]), sb("wu_now", [P, 2, DH])
        sg, h = sb("sg", [P, 2, DH]), sb("h", [P, 2, DH])
        yo = sb("yo", [P, 2, P])
        yb = sb("yb", [P, 2, NT, P])
        g_ps, u_ps = ps("g_ps", [P, 2, DH]), ps("u_ps", [P, 2, DH])
        x_ps, y_ps = ps("x_ps", [P, 2, QB]), ps("y_ps", [P, 2, QB])
        gathered, scattered = [sem(f"gathered{i}") for i in range(X_BUFS)], [sem(f"scattered{i}") for i in range(2)]
        gate_here, up_here = sem("gate_here"), sem("up_here")
        x_turned, x_copied, gate_done, up_done = sem("x_turned"), sem("x_copied"), sem("gate_done"), sem("up_done")
        silu_done, h_done = sem("silu_done"), sem("h_done")
        first_added, y_scaled = sem("first_added"), sem("y_scaled")
        down_done, y_copied, added, stored = sem("down_done"), sem("y_copied"), sem("added"), sem("stored")
        y_loaded = [[sem(f"y_loaded{k}{q}") for q in range(NQB)] for k in range(2)]
        block = ctx.enter_context(nc.Block())
        S = SLOT_TILES

        def column(eng, t):
            return eng.value_load(expert_of[0:1, t:t + 1], min_val=0, max_val=(NE - 1) * DH)

        @block.gpsimd
        def _(pool):
            def gather(t):
                pool.indirect_dma_start(xg[:, t % X_BUFS], None, xn_dram,
                                        bass.IndirectOffsetOnAxis(src_idx[:, t:t + 1], 0)).then_inc(gathered[t % X_BUFS], 16)

            for t in range(AHEAD):
                gather(t)
            for t in range(S + 1):
                if t + AHEAD < S:
                    if t:
                        pool.wait_ge(x_turned, t)
                    gather(t + AHEAD)
                if t >= 1:
                    n = t - 1
                    pool.wait_ge(y_copied, n + 1)
                    pool.indirect_dma_start(y_dram, bass.IndirectOffsetOnAxis(dst_idx[:, n:n + 1], 0),
                                            yo[:, n % 2], None).then_inc(scattered[n % 2], 16)
            for q in range(NQB):
                pool.wait_ge(y_loaded[1][q], 16)
                rows = yb[:, 1, q * TPB:(q + 1) * TPB]
                w = weights[:, 1, q * TPB:(q + 1) * TPB].rearrange("p (t o) -> p t o", o=1).broadcast_to([P, TPB, P])
                pool.tensor_tensor(rows, rows, w, ALU.mult).then_inc(y_scaled, 1)
                pool.wait_ge(y_scaled, q + 1)

        def load_y(eng, k):
            for b in range(2):
                eng.wait_ge(scattered[b], 16 * ((S + 1 - b) // 2))
            for q in range(NQB):
                rows = y_dram[k * T + q * QB:k * T + (q + 1) * QB, :]
                eng.dma_start(yb[:, k, q * TPB:(q + 1) * TPB], rows.rearrange("(t p) d -> p t d", p=P)).then_inc(y_loaded[k][q], 16)

        @block.sync
        def _(sp):
            load_y(sp, 1)
            if out is not None:
                for q in range(NQB):
                    sp.wait_ge(added, q + 1)
                    sp.dma_start(out[:, q * TPB:(q + 1) * TPB], x[:, q * TPB:(q + 1) * TPB]).then_inc(stored, 16)
                sp.wait_ge(stored, 16 * NQB)

        @block.tensor
        def _(pe):
            def turn_x(t):
                pe.wait_ge(gathered[t % X_BUFS], 16 * (t // X_BUFS + 1))
                if t >= 2:
                    pe.wait_ge(x_copied, t - 1)
                pe.transpose(x_ps[:, t % 2, 0:P], xg[:, t % X_BUFS], ident).then_inc(x_turned, 1)

            def hidden(t, out, w, done):
                for c in range(HC):
                    last = pe.matmul(out[:, t % 2, c * P:(c + 1) * P], w[:, t % 2, c * P:(c + 1) * P], xt[:, t % 2], start=True, stop=True)
                last.then_inc(done, 1)

            def down(t):
                col = column(pe, t)
                pe.wait_ge(h_done, t + 1)
                if t >= 2:
                    pe.wait_ge(y_copied, t - 1)
                for c in range(HC):
                    last = pe.matmul(y_ps[:, t % 2, 0:P], h[:, t % 2, c * P:(c + 1) * P], w_down[:, DS(col + c * P, P)],
                                     start=(c == 0), stop=(c == HC - 1))
                last.then_inc(down_done, 1)

            turn_x(0)
            for t in range(S):
                if t + 1 < S:
                    turn_x(t + 1)
                pe.wait_ge(x_copied, t + 1)
                pe.wait_ge(gate_here, t + 1)
                if t >= 2:
                    pe.wait_ge(h_done, t - 1)
                hidden(t, g_ps, wg_now, gate_done)
                pe.wait_ge(up_here, t + 1)
                hidden(t, u_ps, wu_now, up_done)
                if t >= 1:
                    down(t - 1)
            down(S - 1)

        @block.scalar
        def _(act):
            def copy_gate(t):
                col = column(act, t)
                if t >= 2:
                    act.wait_ge(gate_done, t - 1)
                act.copy(wg_now[:, t % 2], w_gate[:, DS(col, DH)]).then_inc(gate_here, 1)

            copy_gate(0)
            for t in range(S):
                if t + 1 < S:
                    copy_gate(t + 1)
                act.wait_ge(gate_done, t + 1)
                if t >= 2:
                    act.wait_ge(h_done, t - 1)
                act.activation(sg[:, t % 2], g_ps[:, t % 2], ACT.Silu).then_inc(silu_done, 1)
            load_y(act, 0)

        @block.vector
        def _(dve):
            def copy_x(t):
                dve.wait_ge(x_turned, t + 1)
                if t >= 2:
                    dve.wait_ge(up_done, t - 1)
                dve.tensor_copy(xt[:, t % 2], x_ps[:, t % 2, 0:P]).then_inc(x_copied, 1)

            def copy_up(t):
                col = column(dve, t)
                if t >= 2:
                    dve.wait_ge(up_done, t - 1)
                dve.tensor_copy(wu_now[:, t % 2], w_up[:, DS(col, DH)]).then_inc(up_here, 1)

            copy_up(0)
            copy_x(0)
            for t in range(S + 1):
                n = t - 1
                if t + 1 < S:
                    copy_x(t + 1)
                    copy_up(t + 1)
                if t < S:
                    dve.wait_ge(up_done, t + 1)
                    dve.wait_ge(silu_done, t + 1)
                    if t >= 2:
                        dve.wait_ge(down_done, t - 1)
                    dve.tensor_tensor(h[:, t % 2], sg[:, t % 2], u_ps[:, t % 2], ALU.mult).then_inc(h_done, 1)
                if t >= 1:
                    dve.wait_ge(down_done, n + 1)
                    if n >= 2:
                        dve.wait_ge(scattered[n % 2], n // 2 * 16)
                    dve.tensor_copy(yo[:, n % 2], y_ps[:, n % 2, 0:P]).then_inc(y_copied, 1)
            for q in range(NQB):
                dve.wait_ge(y_loaded[0][q], 16)
                for t in range(q * TPB, (q + 1) * TPB):
                    dve.scalar_tensor_tensor(x[:, t], yb[:, 0, t], weights[:, 0, t:t + 1], x[:, t], ALU.mult, ALU.add).then_inc(first_added, 1)
                dve.wait_ge(first_added, (q + 1) * TPB)
                dve.wait_ge(y_scaled, q + 1)
                tiles = slice(q * TPB, (q + 1) * TPB)
                dve.tensor_tensor(x[:, tiles], x[:, tiles], yb[:, 1, tiles], ALU.add).then_inc(added, 1)


DI, DST, HD = 256, 64, 64
MH = DI // HD
DCONV = 4
CCH = (DI + 2 * DST) // P
FC = 512 // P
PAD = DCONV - 1
SERIES = 9


def mamba_in_block(nc, xnt, w_conv_in, w_z, d_ps, small, conv, sz, dt, a, ecum, dec, etot, w_out, u_incl, below, ones):
    cw, cb = small["conv_w"], small["conv_b"]
    ACCS = 4
    NU = NQB * CCH
    ctx, sb, ps, sem = stage(nc)
    with ctx:
        raw = sb("raw", [P, CCH, PAD + T])
        acc = sb("acc", [P, ACCS, QB])
        v = sb("sp_v", [P, 7, NT, MH])
        d_in, pos, neg_abs, ex, rcp, ratio, square = (v[:, i] for i in range(7))
        series = sb("series", [P, NT, MH])
        ea, nea = sb("ea", [P, MH]), sb("nea", [P, MH])
        c_ps = ps("c_ps", [P, CCH, QB])
        z_ps = ps("z_ps", [P, 2, 2, DI])
        sums = ps("sums", [P, 3, NT * MH])
        padded, projected, raw_ready = sem("padded"), sem("mi_projected"), sem("raw_ready")
        z_done, z_read, d_read = sem("z_done"), sem("z_read"), sem("d_read")
        last_tap, tap, conv_done, silu_done = sem("last_tap"), sem("tap"), sem("conv_done"), sem("mi_silu")
        rate_step, ea_ready, asked, given, rcp_asked, rcp_given, a_ready, summed, exped, scaled = (
            sem(f"mr_{n}") for n in ("step", "ea_ready", "asked", "given", "rcp_asked", "rcp_given", "a_ready", "summed", "exped", "scaled"))
        block = ctx.enter_context(nc.Block())

        @block.tensor
        def _(pe):
            for n in range(NU):
                b, c = n // CCH, n % CCH
                if b:
                    pe.wait_ge(last_tap, n - CCH + 1)
                pe.matmul(c_ps[:, c], w_conv_in[:, c * P:(c + 1) * P], xnt[:, b * QB:(b + 1) * QB],
                          start=True, stop=True).then_inc(projected, 1)
                if c:
                    m = 2 * b + c - 1
                    if m >= 2:
                        pe.wait_ge(z_read, m - 1)
                    for i in range(2):
                        t = 2 * m + i
                        last = pe.matmul(z_ps[:, m % 2, i], xnt[:, t * P:(t + 1) * P], w_z, start=True, stop=True)
                    last.then_inc(z_done, 1)
            pe.wait_ge(a_ready, 1)
            for i, lhs in enumerate((u_incl, below, ones)):
                last = pe.matmul(sums[:, i], lhs, a[:].rearrange("p t h -> p (t h)"), start=True, stop=True)
            last.then_inc(summed, 1)

        @block.scalar
        def _(act):
            act.copy(d_in, d_ps[:]).then_inc(d_read, 1)
            act.activation(ea[:], small["A_log"], ACT.Exp).then_inc(ea_ready, 1)
            act.wait_ge(asked, 1)
            act.activation(ex, neg_abs, ACT.Exp).then_inc(given, 1)
            for n in range(NU + CCH):
                b, c = n // CCH, n % CCH
                if n < NU:
                    act.wait_ge(projected, n + 1)
                    act.copy(raw[:, c, PAD + b * QB:PAD + (b + 1) * QB], c_ps[:, c]).then_inc(raw_ready, 1)
                    if n >= ACCS:
                        act.wait_ge(silu_done, n - ACCS + 1)
                    act.activation(acc[:, n % ACCS], c_ps[:, c], ACT.Identity, bias=cb[:, c:c + 1], scale=cw[:, c, PAD:PAD + 1]).then_inc(last_tap, 1)
                    if c:
                        m = 2 * b + c - 1
                        act.wait_ge(z_done, m + 1)
                        act.activation(sz[:, 2 * m:2 * m + 2], z_ps[:, m % 2], ACT.Silu).then_inc(z_read, 1)
                if n >= CCH:
                    m = n - CCH
                    act.wait_ge(conv_done, m + 1)
                    act.activation(conv[:, m % CCH, m // CCH * QB:(m // CCH + 1) * QB], acc[:, m % ACCS], ACT.Silu).then_inc(silu_done, 1)
            act.wait_ge(summed, 1)
            for i, out in enumerate((ecum, dec, etot)):
                act.activation(out[:].rearrange("p t h -> p (t h)"), sums[:, i], ACT.Exp).then_inc(exped, 1)

        @block.vector
        def _(dve):
            dve.memset(raw[:, :, 0:PAD], 0.0).then_inc(padded, 1)
            dve.wait_ge(padded, 1)
            for c in range(2):
                dve.tensor_scalar(w_out[:, c], w_out[:, c], small["norm_w"][:, c:c + 1], None, ALU.mult).then_inc(scaled, 1)
            dve.wait_ge(rcp_asked, 1)
            dve.reciprocal(rcp, rcp).then_inc(rcp_given, 1)
            for first in range(0, NU, 2):
                for k in range(PAD):
                    for n in range(first, first + 2):
                        b, c = n // CCH, n % CCH
                        if k == 0:
                            dve.wait_ge(raw_ready, n + 1)
                            dve.wait_ge(last_tap, n + 1)
                        else:
                            dve.wait_ge(tap, first * (PAD - 1) + 2 * (k - 1) + n - first + 1)
                        dve.scalar_tensor_tensor(acc[:, n % ACCS], raw[:, c, b * QB + k:b * QB + k + QB], cw[:, c, k:k + 1], acc[:, n % ACCS],
                                                 ALU.mult, ALU.add).then_inc(tap if k < PAD - 1 else conv_done, 1)

        @block.gpsimd
        def _(pool):
            link = Chain(pool, rate_step)
            all_heads = lambda w: w.rearrange("p (o h) -> p o h", o=1).broadcast_to([P, NT, MH])
            pool.wait_ge(d_read, 1)
            link(pool.tensor_tensor(d_in, d_in, all_heads(small["dt_bias"]), ALU.add))
            link(pool.tensor_scalar(pos, d_in, 0.0, None, ALU.max))
            link(pool.tensor_scalar(neg_abs, pos, -2.0, None, ALU.mult))
            pool.tensor_tensor(neg_abs, neg_abs, d_in, ALU.add).then_inc(asked, 1)
            pool.wait_ge(given, 1)
            pool.tensor_scalar(rcp, ex, 2.0, None, ALU.add).then_inc(rcp_asked, 1)
            pool.wait_ge(rcp_given, 1)
            link(pool.tensor_tensor(ratio, ex, rcp, ALU.mult))
            link(pool.tensor_tensor(square, ratio, ratio, ALU.mult))
            link(pool.tensor_scalar(series[:], square, 1.0 / (2 * SERIES - 1), 1.0 / (2 * SERIES - 3), ALU.mult, ALU.add))
            for k in range(SERIES - 2, 0, -1):
                link(pool.tensor_tensor(series[:], series[:], square, ALU.mult))
                link(pool.tensor_scalar(series[:], series[:], 1.0 / (2 * k - 1), None, ALU.add))
            link(pool.tensor_tensor(series[:], series[:], ratio, ALU.mult))
            link(pool.tensor_scalar(series[:], series[:], 2.0, None, ALU.mult))
            link(pool.tensor_tensor(dt[:], series[:], pos, ALU.add))
            pool.wait_ge(ea_ready, 1)
            link(pool.tensor_scalar(nea[:], ea[:], -1.0, None, ALU.mult))
            pool.tensor_tensor(a[:], dt[:], all_heads(nea[:]), ALU.mult).then_inc(a_ready, 1)


def ssd_block(nc, conv, sz, dt, a, ecum, dec, etot, d_param, y, ssq, ident, u_incl, below):
    ctx, sb, ps, sem = stage(nc)
    with ctx:
        tok = sb("tok", [P, 2, CCH, P])
        ct = sb("ct", [DST, 2, P])
        r = sb("seg_in", [P, 2, MH, P])
        e = sb("seg_exp", [P, 2, MH, P])
        gm = sb("gm", [P, 2, P])
        mt = sb("mt", [P, 2, MH, P])
        dtx, dtxd, dx = sb("dtx", [P, 2, MH, HD]), sb("dtxd", [P, 2, MH, HD]), sb("dx", [P, 2, MH, HD])
        state = sb("state", [DST, 2, MH, HD])
        yt = sb("yt", [P, 2, MH, HD])
        sq = sb("sq", [P, 2, DI])
        bank = lambda name: ps(name, [P, QB])
        t_ps, c_ps, g_ps, s_ps, i_ps, y_ps, u_ps = (bank(f"ssd_{n}") for n in "tcgsiyu")
        names = ("r_ready dtx_ready dtxd_ready dx_ready t_done t_copied c_done c_copied g_done s_done e_done "
                 "gm_done mt_done i_done y_done u_done sdec_done state_ready from_state with_dx y_summed y_ready sq_done")
        s = {n: sem("ssd_" + n) for n in names.split()}
        block = ctx.enter_context(nc.Block())

        def after(eng, name, count):
            if count > 0:
                eng.wait_ge(s[name], count)

        flat = lambda v: v.rearrange("p h d -> p (h d)")
        head = lambda v, t: v[:, t].rearrange("p (h o) -> p h o", o=1)
        chunk = lambda c, t: conv[:, c, t * P:(t + 1) * P]

        @block.gpsimd
        def _(pool):
            def rates(t):
                after(pool, "s_done", t - 1)
                pool.tensor_tensor(r[:, t % 2], u_incl.rearrange("p (o i) -> p o i", o=1).broadcast_to([P, MH, P]),
                                   head(a, t).broadcast_to([P, MH, P]), ALU.mult).then_inc(s["r_ready"], 1)
                pool.wait_ge(s["r_ready"], t + 1)

            rates(0)
            rates(1)
            for t in range(NT):
                b = t % 2
                pool.wait_ge(s["t_copied"], t + 1)
                after(pool, "y_done", t - 1)
                xs = tok[:, b, 0:2].rearrange("p c (h d) -> p (c h) d", d=HD)
                pool.tensor_tensor(dtx[:, b], xs, head(dt, t).broadcast_to([P, MH, HD]), ALU.mult).then_inc(s["dtx_ready"], 1)
                pool.wait_ge(s["dtx_ready"], t + 1)
                after(pool, "u_done", t - 1)
                pool.tensor_tensor(dtxd[:, b], dtx[:, b], head(dec, t).broadcast_to([P, MH, HD]), ALU.mult).then_inc(s["dtxd_ready"], 1)
                pool.wait_ge(s["dtxd_ready"], t + 1)
                after(pool, "with_dx", t - 1)
                pool.tensor_tensor(dx[:, b], xs, d_param.rearrange("p (h o) -> p h o", o=1).broadcast_to([P, MH, HD]),
                                   ALU.mult).then_inc(s["dx_ready"], 1)
                pool.wait_ge(s["dx_ready"], t + 1)
                if t + 2 < NT:
                    rates(t + 2)

        @block.tensor
        def _(pe):
            def turn(t):
                after(pe, "t_copied", t)
                for c in range(CCH):
                    last = pe.transpose(t_ps[:, c * P:(c + 1) * P], chunk(c, t), ident)
                last.then_inc(s["t_done"], 1)
                pe.wait_ge(s["r_ready"], t + 1)
                after(pe, "e_done", t)
                pe.matmul(s_ps[:], below, flat(r[:, t % 2]), start=True, stop=True).then_inc(s["s_done"], 1)
                pe.wait_ge(s["t_copied"], t + 1)
                after(pe, "c_copied", t)
                pe.transpose(c_ps[0:DST, 0:P], tok[:, t % 2, 2, DST:P], ident).then_inc(s["c_done"], 1)

            def products(t):
                pe.wait_ge(s["c_copied"], t + 1)
                after(pe, "gm_done", t)
                pe.matmul(g_ps[:, 0:P], chunk(2, t)[0:DST], ct[:, t % 2], start=True, stop=True).then_inc(s["g_done"], 1)

            turn(0)
            products(0)
            for t in range(NT):
                b = t % 2
                if t + 1 < NT:
                    turn(t + 1)
                pe.wait_ge(s["dtxd_ready"], t + 1)
                pe.wait_ge(s["state_ready"], t + 1)
                pe.matmul(u_ps[0:DST, 0:DI], tok[:, b, 2, 0:DST], flat(dtxd[:, b]), start=True, stop=True).then_inc(s["u_done"], 1)
                if t + 1 < NT:
                    products(t + 1)
                after(pe, "from_state", t)
                pe.matmul(i_ps[:, 0:DI], ct[:, b], flat(state[:, b]), start=True, stop=True).then_inc(s["i_done"], 1)
                pe.wait_ge(s["mt_done"], t + 1)
                after(pe, "y_summed", t)
                for h in range(MH):
                    last = pe.matmul(y_ps[:, h * HD:(h + 1) * HD], mt[:, b, h], dtx[:, b, h], start=True, stop=True)
                last.then_inc(s["y_done"], 1)

        @block.scalar
        def _(act):
            def square(t):
                act.wait_ge(s["y_ready"], t + 1)
                act.activation(sq[:, t % 2], y[:, t], ACT.Square, accum_out=ssq[:, t:t + 1]).then_inc(s["sq_done"], 1)

            for t in range(NT):
                b = t % 2
                act.wait_ge(s["t_done"], t + 1)
                after(act, "u_done", t - 1)
                after(act, "dx_ready", t - 1)
                act.copy(tok[:, b].rearrange("p c i -> p (c i)"), t_ps[:, 0:CCH * P]).then_inc(s["t_copied"], 1)
                act.wait_ge(s["c_done"], t + 1)
                after(act, "i_done", t - 1)
                act.copy(ct[:, b], c_ps[0:DST, 0:P]).then_inc(s["c_copied"], 1)
                act.wait_ge(s["s_done"], t + 1)
                after(act, "mt_done", t - 1)
                act.activation(flat(e[:, b]), s_ps[:], ACT.Exp).then_inc(s["e_done"], 1)
                if t >= 2:
                    after(act, "sq_done", t - 3)
                    square(t - 2)
            for t in range(NT - 2, NT):
                act.wait_ge(s["sq_done"], t - 1)
                square(t)

        @block.vector
        def _(dve):
            dve.memset(state[:, 0], 0.0).then_inc(s["state_ready"], 1)
            for t in range(NT):
                b = t % 2
                dve.wait_ge(s["g_done"], t + 1)
                dve.tensor_tensor(gm[:, b], g_ps[:, 0:P], u_incl, ALU.mult).then_inc(s["gm_done"], 1)
                dve.wait_ge(s["gm_done"], t + 1)
                dve.wait_ge(s["e_done"], t + 1)
                after(dve, "y_done", t - 1)
                dve.tensor_tensor(mt[:, b], e[:, b], gm[:, b].rearrange("p (o i) -> p o i", o=1).broadcast_to([P, MH, P]),
                                  ALU.mult).then_inc(s["mt_done"], 1)
                dve.wait_ge(s["state_ready"], t + 1)
                after(dve, "i_done", t)
                dve.tensor_tensor(state[:, 1 - b], state[:, b], head(etot, t)[0:DST].broadcast_to([DST, MH, HD]), ALU.mult).then_inc(s["sdec_done"], 1)
                dve.wait_ge(s["sdec_done"], t + 1)
                dve.wait_ge(s["u_done"], t + 1)
                dve.tensor_tensor(flat(state[:, 1 - b]), flat(state[:, 1 - b]), u_ps[0:DST, 0:DI], ALU.add).then_inc(s["state_ready"], 1)
                dve.wait_ge(s["i_done"], t + 1)
                dve.tensor_tensor(yt[:, b], i_ps[:, 0:DI].rearrange("p (h d) -> p h d", d=HD), head(ecum, t).broadcast_to([P, MH, HD]),
                                  ALU.mult).then_inc(s["from_state"], 1)
                dve.wait_ge(s["from_state"], t + 1)
                dve.wait_ge(s["dx_ready"], t + 1)
                dve.tensor_tensor(yt[:, b], yt[:, b], dx[:, b], ALU.add).then_inc(s["with_dx"], 1)
                dve.wait_ge(s["with_dx"], t + 1)
                dve.wait_ge(s["y_done"], t + 1)
                dve.tensor_tensor(flat(yt[:, b]), flat(yt[:, b]), y_ps[:, 0:DI], ALU.add).then_inc(s["y_summed"], 1)
                dve.wait_ge(s["y_summed"], t + 1)
                dve.tensor_tensor(y[:, t], flat(yt[:, b]), sz[:, t], ALU.mult).then_inc(s["y_ready"], 1)


def mamba_out_block(nc, y, ssq, w_out, x0, ident, st):
    ctx, sb, ps, sem = stage(nc)
    with ctx:
        std, rstd = sb("mo_std", [P, NT]), sb("mo_rstd", [P, NT])
        yt = sb("mo_t", [P, 2, 2, 2, P])
        tr, out = ps("mo_tr", [P, 2, QB]), ps("mo_out", [P, 2, QB])
        std_ready, rstd_ready, turned, copied, projected, added, measured = (
            sem(f"mo_{n}") for n in ("std", "rstd", "turned", "copied", "projected", "added", "measured"))
        block = ctx.enter_context(nc.Block())
        NPAIR = NT // 2

        @block.tensor
        def _(pe):
            for n in range(NPAIR + 1):
                if n < NPAIR:
                    if n >= 2:
                        pe.wait_ge(copied, n - 1)
                    for i in range(2):
                        for c in range(2):
                            last = pe.transpose(tr[:, n % 2, (2 * i + c) * P:(2 * i + c + 1) * P], y[:, 2 * n + i, c * P:(c + 1) * P], ident)
                    last.then_inc(turned, 1)
                if n >= 1:
                    m = n - 1
                    pe.wait_ge(copied, m + 1)
                    if m >= 2:
                        pe.wait_ge(added, 2 * (m - 1))
                    for i in range(2):
                        for c in range(2):
                            last = pe.matmul(out[:, m % 2, i * P:(i + 1) * P], yt[:, m % 2, i, c], w_out[:, c], start=(c == 0), stop=(c == 1))
                    last.then_inc(projected, 1)

        @block.scalar
        def _(act):
            act.activation(std[:], ssq[:], ACT.Sqrt, bias=EPS, scale=1.0 / DI).then_inc(std_ready, 1)
            for n in range(NPAIR):
                act.wait_ge(turned, n + 1)
                if n >= 2:
                    act.wait_ge(projected, n - 1)
                act.copy(yt[:, n % 2].rearrange("p i c t -> p (i c t)"), tr[:, n % 2]).then_inc(copied, 1)

        @block.vector
        def _(dve):
            dve.wait_ge(std_ready, 1)
            dve.reciprocal(rstd[:], std[:]).then_inc(rstd_ready, 1)
            dve.wait_ge(rstd_ready, 1)
            for n in range(NPAIR):
                dve.wait_ge(projected, n + 1)
                for i in range(2):
                    t = 2 * n + i
                    dve.scalar_tensor_tensor(x0[:, t], out[:, n % 2, i * P:(i + 1) * P], rstd[:, t:t + 1], x0[:, t], ALU.mult, ALU.add).then_inc(added, 1)
                for t in range(2 * n, 2 * n + 2):
                    dve.wait_ge(added, t + 1)
                    dve.bn_stats(st[:, t, :], x0[:, t, :]).then_inc(measured, 1)
            dve.wait_ge(measured, NT)


def mlp_block(nc, vt, w_fc, fc_b, w_proj, proj_b, x0, x, st):
    ctx, sb, ps, sem = stage(nc)
    with ctx:
        h = sb("mlp_h", [P, 2, FC, QB])
        h_ps, o_ps = ps("mlp_hps", [P, FC, QB]), ps("mlp_ops", [P, 2, QB])
        h_done, gelu_done, o_done, x_step, sum_done, measured = (
            sem(f"mlp_{n}") for n in ("h_done", "gelu", "o_done", "x_step", "sum_done", "measured"))
        block = ctx.enter_context(nc.Block())

        @block.tensor
        def _(pe):
            for b in range(NQB + 1):
                if b < NQB:
                    for c in range(FC):
                        if b:
                            pe.wait_ge(gelu_done, (b - 1) * FC + c + 1)
                        pe.matmul(h_ps[:, c], w_fc[:, c * P:(c + 1) * P], vt[:, b * QB:(b + 1) * QB], start=True, stop=True).then_inc(h_done, 1)
                if b:
                    n = b - 1
                    pe.wait_ge(gelu_done, (n + 1) * FC)
                    if n >= 2:
                        pe.wait_ge(sum_done, n - 1)
                    for i in range(TPB):
                        for c in range(FC):
                            last = pe.matmul(o_ps[:, n % 2, i * P:(i + 1) * P], h[:, n % 2, c, i * P:(i + 1) * P], w_proj[:, c],
                                             start=(c == 0), stop=(c == FC - 1))
                    last.then_inc(o_done, 1)

        @block.scalar
        def _(act):
            for n in range(NQB * FC):
                b, c = n // FC, n % FC
                act.wait_ge(h_done, n + 1)
                if b >= 2:
                    act.wait_ge(o_done, b - 1)
                act.activation(h[:, b % 2, c], h_ps[:, c], ACT.Gelu, bias=fc_b[:, c:c + 1]).then_inc(gelu_done, 1)

        @block.vector
        def _(dve):
            flat = lambda v, b: v[:, b * TPB:(b + 1) * TPB, :]
            for b in range(NQB):
                dve.tensor_tensor(flat(x, b), flat(x, b), flat(x0, b), ALU.add).then_inc(x_step, 1)
            dve.wait_ge(x_step, NQB)
            for b in range(NQB):
                dve.tensor_tensor(flat(x, b), flat(x, b), proj_b.rearrange("p (o d) -> p o d", o=1).broadcast_to([P, TPB, P]), ALU.add).then_inc(x_step, 1)
            for b in range(NQB):
                dve.wait_ge(x_step, NQB + b + 1)
                dve.wait_ge(o_done, b + 1)
                dve.tensor_tensor(flat(x, b), flat(x, b), o_ps[:, b % 2].rearrange("p (t d) -> p t d", d=P), ALU.add).then_inc(sum_done, 1)
                dve.wait_ge(sum_done, b + 1)
                for t in range(b * TPB, (b + 1) * TPB):
                    dve.bn_stats(st[:, t, :], x[:, t, :]).then_inc(measured, 1)
            dve.wait_ge(measured, NT)


def vectors_layout():
    at, cols = 0, {}
    for name, width in (("ln1_w", 1), ("ln1_b", 1), ("ln2_w", 1), ("ln2_b", 1), ("conv_w", CCH * DCONV), ("conv_b", CCH),
                        ("dt_bias", MH), ("A_log", MH), ("D", MH), ("norm_w", 2), ("fc_b", FC), ("proj_b", P)):
        cols[name] = (at, width)
        at += width
    return cols, at


def rope_tables():
    inv = (np.float32(10000.0) ** (-np.arange(0, DK // 2, dtype=np.float32) * np.float32(2.0) / np.float32(DK))).astype(np.float32)
    ang = (np.arange(T, dtype=np.float32)[:, None] * inv[None, :]).astype(np.float32)
    cos, sin = np.cos(ang).astype(np.float32), np.sin(ang).astype(np.float32)
    c = np.repeat(cos, 2, axis=1).T
    s = np.stack([-sin, sin], axis=-1).reshape(T, DK).T
    return np.ascontiguousarray(np.stack([np.tile(c, (NH, 1)), np.tile(s, (NH, 1))], axis=1))


def mask_tables():
    row, col = np.arange(P)[:, None], np.arange(P)[None, :]
    f = lambda c, v: np.where(c, np.float32(v), np.float32(0))
    zero = np.zeros((P, P), np.float32)
    return np.ascontiguousarray(np.stack([f(row == col, 1), zero, zero, zero, f(col > row, NEG), f(row <= col, 1), f(row > col, 1)], axis=1))


def setup_block(nc, x, x_in, loads, masks, identb, st, vaug, stacks, cs, rope, rope_in):
    ctx, sb, ps, sem = stage(nc)
    with ctx:
        loaded, cast, measured, prepared = sem("loaded"), sem("cast"), sem("setup_measured"), sem("setup_prepared")
        x_loaded = [sem(f"x_loaded{q}") for q in range(NQB)]
        block = ctx.enter_context(nc.Block())

        @block.sync
        def _(sp):
            for q in range(NQB):
                tiles = slice(q * TPB, (q + 1) * TPB)
                sp.dma_start(x[:, tiles], x_in[:, tiles]).then_inc(x_loaded[q], 16)

        @block.scalar
        def _(act):
            for dst, src in loads:
                act.dma_start(dst, src).then_inc(loaded, 16)
            act.wait_ge(loaded, 16 * len(loads))
            for q in range(NQB):
                act.wait_ge(x_loaded[q], 16)
            for b in range(ROPE_BUFS):
                act.dma_start(cs[:, b], rope[:, :, b * QB:(b + 1) * QB]).then_inc(rope_in[b], 16)

        @block.vector
        def _(dve):
            for q in range(NQB):
                dve.wait_ge(x_loaded[q], 16)
                for t in range(q * TPB, (q + 1) * TPB):
                    dve.bn_stats(st[:, t, :], x[:, t, :]).then_inc(measured, 1)
            dve.wait_ge(measured, NT)
            dve.wait_ge(loaded, 16 * len(loads))
            dve.tensor_copy(identb[:], masks[:, 0]).then_inc(cast, 1)
            dve.wait_ge(cast, 1)

        @block.gpsimd
        def _(pool):
            link = Chain(pool, prepared)
            link(pool.memset(vaug[:, :, :, DK:DK + 1], 1.0))
            link(pool.memset(stacks[0][0][MROW:KROWS].bitcast(U32), 0))
            link(pool.memset(stacks[1][0][MROW:KROWS].bitcast(U32), 0))


def program(nc, a, out):
    ctx, sb, ps, sem = stage(nc)
    with ctx:
        before = nc.snapshot_sems()
        x = sb("x", [P, NT, P])
        masks = sb("masks", [P, 7, P])
        ident = masks[:, 0]
        identb = sb("identb", [P, P], BF16)
        maskq = masks[:, 1:5].rearrange("p a b -> p (a b)")
        watt = sb("watt", [P, 6, P])
        by_token = lambda t: t.rearrange("(t p) d -> p t d", p=P)
        w_gate, w_up, w_down = (sb(n, [P, NE * DH]) for n in ("w_gate", "w_up", "w_down"))
        wg, bg = sb("wg", [P, NE]), sb("bg", [P, NE])
        st = sb("statistics", [P, NT, 6])
        mt = sb("moe_tables", [P, a["moe_tables"].shape[1]])
        weights = sb("weights", [P, 2, NT])
        src_idx, dst_idx = sb("src_idx", [P, SLOT_TILES], U32), sb("dst_idx", [P, SLOT_TILES], U32)
        expert_of = sb("expert_of", [P, SLOT_TILES], I32)
        route = weights, src_idx, dst_idx, expert_of
        xn_dram = nc.dram_tensor("xn_rows", [T, P], F32).ap()
        y_dram = nc.dram_tensor("expert_rows", [DUMP + SLOT_TILES * P, P], F32).ap()
        w_mamba = sb("w_mamba", [P, CCH * P + DI + MH])
        w_out, w_fc, w_proj = sb("w_out", [P, 2, P]), sb("w_fc", [P, FC * P]), sb("w_proj", [P, FC, P])
        cols, width = vectors_layout()
        vectors = sb("vectors", [P, width])
        vec = {n: vectors[:, at:at + w] for n, (at, w) in cols.items()}
        small = dict(vec, conv_w=vec["conv_w"].rearrange("p (c k) -> p c k", k=DCONV))
        late = [(vectors[:], a["vectors"]), (mt[:], a["moe_tables"]), (wg[:], a["wg"]), (bg[:], a["bg"])]
        for q in range(4):
            cols_q = slice(q * NE * DH // 4, (q + 1) * NE * DH // 4)
            late += [(w[:, cols_q], a[n][:, cols_q]) for w, n in ((w_gate, "w_gate"), (w_up, "w_up"), (w_down, "w_down"))]
        late += [(w_mamba[:], a["w_mamba"]), (w_out[:], a["w_out"]), (w_fc[:], a["w_fc"]), (w_proj[:], a["w_proj"])]
        def mixture(tag, out=None):
            with ExitStack() as m:
                xn = m.enter_context(nc.sbuf_tensor(f"{tag}_xn", [P, NT, P], F32))
                xnt = m.enter_context(nc.sbuf_tensor(f"{tag}_xnt", [P, T], F32))
                lg_ps = m.enter_context(nc.psum_tensor(f"{tag}_lg_ps", [P, NT, NE], F32))
                norm_block(nc, tag, x, xn, xnt, ident, logits=(lg_ps, wg[:]), xn_dram=xn_dram, measured=st)
                route_block(nc, tag + "_", lg_ps, bg[:], mt[:], route)
            experts_block(nc, tag + "_", w_gate, w_up, w_down, route, x, ident, xn_dram, y_dram, out)

        with ExitStack() as att:
            sba = lambda name, shape, dt=F32: att.enter_context(nc.sbuf_tensor(name, shape, dt))
            ao = sba("ao", [P, NT, P])
            vaug = sba("vaug", [P, NT, NH, DK + 1])
            qk = nc.dram_tensor("qk_parts", [2, 3, P, T], BF16).ap()
            stacks = [[sba(f"{n}{i}", [P, HG, T], BF16) for i in range(2)] for n in ("qst", "kst")]
            rope_in = [sem(f"rope_in{b}") for b in range(NQB)]
            with ExitStack() as pre:
                cs = pre.enter_context(nc.sbuf_tensor("rope_sb", [P, ROPE_BUFS, 2, QB], F32))
                setup_block(nc, x, by_token(a["x"]), [(masks[:], a["masks"]), (watt[:], a["w_att"])], masks, identb, st,
                            vaug, stacks, cs, a["rope"], rope_in)
                xnt = pre.enter_context(nc.sbuf_tensor("xnt", [P, T], F32))
                def clear_second(pool, link):
                    link(pool.memset(stacks[0][1][MROW:KROWS].bitcast(U32), 0))
                    link(pool.memset(stacks[1][1][MROW:KROWS].bitcast(U32), 0))

                norm_block(nc, "ln0", x, ao, xnt, ident, measured=st, beside=clear_second)
                qkv_block(nc, xnt, [watt[:, i] for i in range(5)], cs, a["rope"], rope_in, vaug, qk, stacks)
            attention_block(nc, stacks, qk, vaug, ao, ident, identb, maskq, late)
            project_add_block(nc, ao, watt[:, 5], x, ident, st)
        mixture("moe1")
        nc.clear_and_free_semaphores(nc.allocated_since(before))
        nc.all_engine_barrier()
        with ExitStack() as mam:
            sbm = lambda name, shape, dt=F32: mam.enter_context(nc.sbuf_tensor(name, shape, dt))
            x0 = sbm("x0", [P, NT, P])
            y, sz = sbm("y", [P, NT, DI]), sbm("sz", [P, NT, DI])
            conv = sbm("conv", [P, CCH, T])
            dt, rate, ecum, dec, etot = (sbm(n, [P, NT, MH]) for n in ("dt", "rate", "ecum", "dec", "etot"))
            ssq = sbm("ssq", [P, NT])
            u_incl, below = masks[:, 5], masks[:, 6]
            norm_block(nc, "ln2", x, x0, None, ident)
            with ExitStack() as pre:
                x0n = pre.enter_context(nc.sbuf_tensor("x0n", [P, NT, P], F32))
                xnt = pre.enter_context(nc.sbuf_tensor("mxnt", [P, T], F32))
                d_ps = pre.enter_context(nc.psum_tensor("d_ps", [P, NT, MH], F32))
                norm_block(nc, "ln3", x0, x0n, xnt, ident, vec["ln1_w"], vec["ln1_b"], logits=(d_ps, w_mamba[:, CCH * P + DI:]))
                mamba_in_block(nc, xnt, w_mamba[:, 0:CCH * P], w_mamba[:, CCH * P:CCH * P + DI], d_ps, small, conv, sz,
                               dt, rate, ecum, dec, etot, w_out, u_incl, below, mt[:, -P:])
            ssd_block(nc, conv, sz, dt, rate, ecum, dec, etot, vec["D"], y, ssq, ident, u_incl, below)
            mamba_out_block(nc, y, ssq, w_out, x0, ident, st)
            with ExitStack() as post:
                x1n = post.enter_context(nc.sbuf_tensor("x1n", [P, NT, P], F32))
                vt = post.enter_context(nc.sbuf_tensor("vt", [P, T], F32))
                norm_block(nc, "ln4", x0, x1n, vt, ident, vec["ln2_w"], vec["ln2_b"], measured=st)
                mlp_block(nc, vt, w_fc, vec["fc_b"], w_proj, vec["proj_b"], x0, x, st)
        mixture("moe2", by_token(out))


def layouts(i):
    c = np.ascontiguousarray
    swap = np.arange(P) ^ 1
    att = [i["L0_attn_a_Wq"], i["L0_attn_a_Wq"][swap], i["L0_attn_a_Wk"], i["L0_attn_a_Wk"][swap],
           i["L0_attn_a_Wv"], i["L0_attn_a_Wo"]]
    rows = lambda v: np.broadcast_to(v, (P,) + v.shape)
    b = lambda name: i["L0_attn_b_" + name]
    w_in = b("in_proj_w")
    by_chunk = lambda v: v.reshape(-1, P).T
    vectors = {
        "ln1_w": b("ln1_w")[:, None], "ln1_b": b("ln1_b")[:, None], "ln2_w": b("ln2_w")[:, None], "ln2_b": b("ln2_b")[:, None],
        "conv_w": b("conv_w").reshape(CCH, P, DCONV).transpose(1, 0, 2).reshape(P, -1), "conv_b": by_chunk(b("conv_b")),
        "dt_bias": rows(b("dt_bias")), "A_log": rows(b("A_log")), "D": rows(b("D_param")), "norm_w": by_chunk(b("norm_w")),
        "fc_b": by_chunk(b("fc_b")), "proj_b": rows(b("proj_b")),
    }
    return {
        "x": c(i["L0_attn_a_x"].reshape(T, P)),
        "masks": mask_tables(), "rope": rope_tables(), "moe_tables": moe_tables(),
        "w_mamba": c(np.concatenate([w_in[DI:2 * DI + 2 * DST], w_in[:DI], w_in[2 * DI + 2 * DST:]]).T),
        "w_out": c(b("out_proj_w").reshape(P, 2, P).transpose(2, 1, 0)),
        "w_fc": c(b("fc_w").T), "w_proj": c(b("proj_w").reshape(P, FC, P).transpose(2, 1, 0)),
        "vectors": c(np.concatenate([vectors[n] for n in vectors_layout()[0]], axis=1)),
        "w_att": c(np.stack([w.T for w in att], axis=1)),
        "wg": c(i["L0_ffn_wg"].T), "bg": c(rows(i["L0_ffn_bg"])),
        "w_gate": c(i["L0_ffn_Wgate"].transpose(2, 0, 1).reshape(P, NE * DH)),
        "w_up": c(i["L0_ffn_Wup"].transpose(2, 0, 1).reshape(P, NE * DH)),
        "w_down": c(i["L0_ffn_Wdown"].reshape(NE, P, HC, P).transpose(3, 0, 2, 1).reshape(P, NE * DH)),
    }


def kernel(**inputs):
    import concourse.bacc as bacc
    from concourse.bass_utils import run_bass_kernel_spmd

    nc = bacc.Bacc("TRN2", target_bir_lowering=False, num_devices=1)
    arrays = {f"in_{k}": v for k, v in layouts({k: np.asarray(v) for k, v in inputs.items()}).items()}
    a = {k[3:]: nc.dram_tensor(k, v.shape, F32, kind="ExternalInput").ap() for k, v in arrays.items()}
    out = nc.dram_tensor("out_0", (T, P), F32, kind="ExternalOutput").ap()
    program(nc, a, out)
    r = run_bass_kernel_spmd(nc, [arrays], core_ids=[0])
    return r.results[0]["out_0"].reshape(1, T, P)
```
